# Optimizing a Trainium2 kernel written in Bass

```python
import numpy as np
import jax
import jax.numpy as jnp

def _softmax(x, axis=-1):
    return jax.nn.softmax(x, axis=axis)

def _gelu(x):
    return jax.nn.gelu(x, approximate=True)

def _silu(x):
    return jax.nn.silu(x)

def _sigmoid(x):
    return jax.nn.sigmoid(x)

def _layernorm(x, axis=-1, eps=1e-05):
    m = jnp.mean(x, axis=axis, keepdims=True)
    v = jnp.var(x, axis=axis, keepdims=True)
    return (x - m) / jnp.sqrt(v + eps)

def _scatter_add(tgt, idx, src, axis=0):
    return tgt.at[idx].add(src)

def _segment_sum(src, seg, n):
    return jax.ops.segment_sum(src, seg, n)
kernel_name = 'mk_decoder_preln_d2_seqx_r4_8dfe55'

def setup_inputs(seed: int=0):
    np.random.seed(seed)
    _w = jnp.asarray

    def _rec_inputs():
        import jax
        import jax.numpy as jnp
        _rk = jax.random.key(seed)
        x = 0.0003765 + 1 * jax.random.normal(jax.random.fold_in(_rk, 1), (8, 256, 512), jnp.float32)
        _lenS = 256 - jax.random.randint(jax.random.fold_in(_rk, 7), (8,), 0, max(1, 256 // 4) + 1, jnp.int32)
        _lenS2 = 256 - jax.random.randint(jax.random.fold_in(_rk, 8), (8,), 0, max(1, 256 // 4) + 1, jnp.int32)
        _ctx_2048P = jax.random.normal(jax.random.fold_in(_rk, 11), (8, 16, 512), jnp.float32)
        _ctx_2048c = jax.random.dirichlet(jax.random.fold_in(_rk, 511), 0.3 * jnp.ones((16,), jnp.float32), (8, 256))
        _ctx_2048t = jnp.einsum('bsk,bkd->bsd', _ctx_2048c, _ctx_2048P)
        _ctx_2048t = _ctx_2048t * jax.lax.rsqrt(jnp.mean(jnp.square(_ctx_2048t)) + 1e-12) * 0.953939
        ctx_2048 = -0.000292821 + 1.00034 * (_ctx_2048t + 0.3 * jax.random.normal(jax.random.fold_in(_rk, 611), (8, 256, 512), jnp.float32))
        return (x, ctx_2048)
    x, ctx_2048 = _rec_inputs()

    def _L0_attn_setup():
        import math
        import jax, jax.numpy as jnp
        import numpy as np
        EMBED_DIM = 512
        NUM_HEADS = 16
        HEAD_DIM = EMBED_DIM // NUM_HEADS
        CHUNK = 128
        RMS_EPS = 1e-05

        def _build_slopes(n):

            def pow2(n):
                start = 2.0 ** (-2.0 ** (-(math.log2(n) - 3)))
                return [start * start ** i for i in range(n)]
            if math.log2(n).is_integer():
                s = pow2(n)
            else:
                closest = 2 ** math.floor(math.log2(n))
                s = pow2(closest) + pow2(2 * closest)[0::2][:n - closest]
            return jnp.asarray(s, dtype=jnp.float32)

        def _rotary(x_BTHD, offset=0):
            T, D = (x_BTHD.shape[1], x_BTHD.shape[-1])
            freq = (1.0 / 1024.0) ** jnp.linspace(0.0, 1.0, D // 4, dtype=jnp.float32)
            freq = jnp.concatenate([freq, jnp.zeros(D // 4, dtype=jnp.float32)])
            t = jnp.arange(offset, offset + T, dtype=jnp.float32)
            theta = t[:, None] * freq[None, :]
            cos = jnp.cos(theta)[None, :, None, :]
            sin = jnp.sin(theta)[None, :, None, :]
            x1, x2 = jnp.split(x_BTHD.astype(jnp.float32), 2, axis=-1)
            y1 = x1 * cos + x2 * sin
            y2 = -x1 * sin + x2 * cos
            return jnp.concatenate([y1, y2], axis=-1).astype(x_BTHD.dtype)

        def _lightning_attn(q, k, v, slopes):
            B, H, T, D = q.shape
            C = CHUNK
            NC = T // C
            r = jnp.exp(-slopes)
            i = jnp.arange(C, dtype=jnp.float32)
            q_decay = r[:, None] ** (i[None, :] + 1.0)
            k_decay = r[:, None] ** (C - 1.0 - i[None, :])
            diff = i[:, None] - i[None, :]
            mask = diff >= 0
            dmask = jnp.where(mask[None], r[:, None, None] ** jnp.where(mask, diff, 0.0)[None], 0.0)
            r_C = r ** float(C)

            def reshape_chunks(x):
                return x.reshape(B, H, NC, C, D).transpose(2, 0, 1, 3, 4)
            qc, kc, vc = (reshape_chunks(q), reshape_chunks(k), reshape_chunks(v))

            def step(kv, qkv):
                qi, ki, vi = qkv
                inter = jnp.einsum('bhcd,bhde->bhce', qi * q_decay[None, :, :, None], kv)
                scores = jnp.einsum('bhcd,bhsd->bhcs', qi, ki) * dmask[None]
                intra = jnp.einsum('bhcs,bhse->bhce', scores, vi)
                kv_new = r_C[None, :, None, None] * kv + jnp.einsum('bhcd,bhce->bhde', ki * k_decay[None, :, :, None], vi)
                return (kv_new, inter + intra)
            kv0 = jnp.zeros((B, H, D, D), dtype=q.dtype)
            _, out = jax.lax.scan(step, kv0, (qc, kc, vc))
            return out.transpose(1, 2, 0, 3, 4).reshape(B, H, T, D)

        def _rms_norm(x, w):
            var = jnp.mean(jnp.square(x), axis=-1, keepdims=True)
            return x * jax.lax.rsqrt(var + RMS_EPS) * w
        key = jax.random.key(seed)
        ks = jax.random.split(key, 6)
        sc = 1.0 / math.sqrt(EMBED_DIM)
        return {'x': jax.random.normal(ks[0], (4, 1024, EMBED_DIM), dtype=jnp.float32), 'Wq': jax.random.normal(ks[1], (EMBED_DIM, EMBED_DIM), dtype=jnp.float32) * sc, 'Wk': jax.random.normal(ks[2], (EMBED_DIM, EMBED_DIM), dtype=jnp.float32) * sc, 'Wv': jax.random.normal(ks[3], (EMBED_DIM, EMBED_DIM), dtype=jnp.float32) * sc, 'Wo': jax.random.normal(ks[4], (EMBED_DIM, EMBED_DIM), dtype=jnp.float32) * sc, 'rms_w': jnp.ones((EMBED_DIM,), dtype=jnp.float32)}
    _L0_attn_all = _L0_attn_setup()
    _L0_attn_in = {k: v for k, v in _L0_attn_all.items() if k in ('Wq', 'Wk', 'Wv', 'Wo', 'rms_w')}
    del _L0_attn_all

    def _L0_xattn_setup():
        import jax, jax.numpy as jnp
        import numpy as np
        key = jax.random.key(seed)
        k1, k2, k3, k4, k5 = jax.random.split(key, 5)
        B, D_MODEL, L = (2, 256, 512)
        HEAD_DIM = 8
        H = D_MODEL // HEAD_DIM
        return {'k': jax.random.normal(k1, (B, D_MODEL, L), dtype=jnp.float32), 'v': jax.random.normal(k2, (B, D_MODEL, L), dtype=jnp.float32), 'q': jax.random.normal(k3, (B, D_MODEL, L), dtype=jnp.float32), 'ssm_kernel': jax.random.normal(k4, (H, L), dtype=jnp.float32), 'D': jax.random.normal(k5, (H,), dtype=jnp.float32), 'head_dim': HEAD_DIM}
    _L0_xattn_all = _L0_xattn_setup()
    _L0_xattn_in = {k: v for k, v in _L0_xattn_all.items() if k in ('ssm_kernel', 'D')}
    del _L0_xattn_all

    def _L0_ffn_setup():
        import jax, jax.numpy as jnp
        import numpy as np
        HIDDEN = 512
        N_EXPERTS = 8
        N_SHARED = 2
        TOP_K = 2
        MOE_FF = 352
        SHARED_FF = N_SHARED * MOE_FF
        SCALE = 2.5
        BATCH, SEQ = (2, 256)
        key = jax.random.key(seed)
        ks = jax.random.split(key, 8)
        s = 0.02
        return {'hidden_states': jax.random.normal(ks[0], (BATCH, SEQ, HIDDEN), jnp.float32), 'gate_w': jax.random.normal(ks[1], (N_EXPERTS, HIDDEN), jnp.float32) * s, 'shared_wg': jax.random.normal(ks[2], (SHARED_FF, HIDDEN), jnp.float32) * s, 'shared_wu': jax.random.normal(ks[3], (SHARED_FF, HIDDEN), jnp.float32) * s, 'shared_wd': jax.random.normal(ks[4], (HIDDEN, SHARED_FF), jnp.float32) * s, 'exp_wg': jax.random.normal(ks[5], (N_EXPERTS, MOE_FF, HIDDEN), jnp.float32) * s, 'exp_wu': jax.random.normal(ks[6], (N_EXPERTS, MOE_FF, HIDDEN), jnp.float32) * s, 'exp_wd': jax.random.normal(ks[7], (N_EXPERTS, HIDDEN, MOE_FF), jnp.float32) * s}
    _L0_ffn_all = _L0_ffn_setup()
    _L0_ffn_in = {k: v for k, v in _L0_ffn_all.items() if k in ('gate_w', 'shared_wg', 'shared_wu', 'shared_wd', 'exp_wg', 'exp_wu', 'exp_wd')}
    del _L0_ffn_all

    def _L1_attn_setup():
        import jax, jax.numpy as jnp
        import numpy as np
        EMBED_DIM = 512
        NUM_HEADS = 16
        BLOCK_SIZE = 128

        def _flash_attention_v2(q, k, v, block_size, scale):
            B, H, S, D = q.shape
            nb = S // block_size
            qb = q.reshape(B, H, nb, block_size, D)
            kb = k.reshape(B, H, nb, block_size, D).transpose(2, 0, 1, 3, 4)
            vb = v.reshape(B, H, nb, block_size, D).transpose(2, 0, 1, 3, 4)
            out0 = jnp.zeros_like(qb)
            l0 = jnp.zeros((B, H, nb, block_size, 1), dtype=q.dtype)
            m0 = jnp.full((B, H, nb, block_size, 1), -jnp.inf, dtype=q.dtype)

            def step(carry, kv):
                out, l, m = carry
                k_j, v_j = kv
                s = jnp.einsum('bhnqd,bhkd->bhnqk', qb, k_j) * scale
                m_ij = jnp.max(s, axis=-1, keepdims=True)
                p = jnp.exp(s - m_ij)
                l_ij = jnp.sum(p, axis=-1, keepdims=True)
                m_new = jnp.maximum(m, m_ij)
                alpha = jnp.exp(m - m_new)
                beta = jnp.exp(m_ij - m_new)
                l_new = alpha * l + beta * l_ij
                pv = jnp.einsum('bhnqk,bhkd->bhnqd', p, v_j)
                out_new = alpha * l / l_new * out + beta * l_ij / l_new * pv
                return ((out_new, l_new, m_new), None)
            (out, _, _), _ = jax.lax.scan(step, (out0, l0, m0), (kb, vb))
            return out.reshape(B, H, S, D)
        key = jax.random.key(seed)
        k1, k2, k3 = jax.random.split(key, 3)
        B, S, E = (2, 1024, EMBED_DIM)
        x = jax.random.normal(k1, (B, S, E), dtype=jnp.float32)
        w_qkv = jax.random.normal(k2, (3 * E, E), dtype=jnp.float32) * 0.02
        w_out = jax.random.normal(k3, (E, E), dtype=jnp.float32) * 0.02
        b_out = jnp.zeros((E,), dtype=jnp.float32)
        return {'x': x, 'w_qkv': w_qkv, 'w_out': w_out, 'b_out': b_out}
    _L1_attn_all = _L1_attn_setup()
    _L1_attn_in = {k: v for k, v in _L1_attn_all.items() if k in ('w_qkv', 'w_out', 'b_out')}
    del _L1_attn_all

    def _L1_xattn_setup():
        import jax, jax.numpy as jnp
        import numpy as np
        import math
        EMBED = 512
        HEADS = 32
        GROUPS = 8
        GROUP_HEADS = HEADS // GROUPS
        HEAD_DIM = EMBED // HEADS
        B, S = (4, 256)
        key = jax.random.key(seed)
        ks = jax.random.split(key, 8)
        sc = 0.02
        return {'q': jax.random.normal(ks[0], (B, S, EMBED), jnp.float32), 'k': jax.random.normal(ks[1], (B, S, EMBED), jnp.float32), 'v': jax.random.normal(ks[2], (B, S, EMBED), jnp.float32), 'Wq': jax.random.normal(ks[3], (EMBED, EMBED), jnp.float32) * sc, 'Wk': jax.random.normal(ks[4], (GROUPS * HEAD_DIM, EMBED), jnp.float32) * sc, 'Wv': jax.random.normal(ks[5], (GROUPS * HEAD_DIM, EMBED), jnp.float32) * sc, 'Wfc': jax.random.normal(ks[6], (EMBED, EMBED), jnp.float32) * sc, 'bfc': jnp.zeros((EMBED,), jnp.float32)}
    _L1_xattn_all = _L1_xattn_setup()
    _L1_xattn_in = {k: v for k, v in _L1_xattn_all.items() if k in ('Wq', 'Wk', 'Wv', 'Wfc', 'bfc')}
    del _L1_xattn_all

    def _L1_ffn_setup():
        import jax, jax.numpy as jnp
        import numpy as np
        B, S, D, E, R, TOP_K = (4, 1024, 512, 6, 16, 2)
        key = jax.random.key(seed)
        ks = jax.random.split(key, 9)
        scale = 0.02
        return {'x': jax.random.normal(ks[0], (B, S, D), dtype=jnp.float32), 'W_base': jax.random.normal(ks[1], (D, D), dtype=jnp.float32) * scale, 'b_base': jax.random.normal(ks[2], (D,), dtype=jnp.float32) * scale, 'A_s': jax.random.normal(ks[3], (D, R), dtype=jnp.float32) * scale, 'B_s': jax.random.normal(ks[4], (R, D), dtype=jnp.float32) * scale, 'A_r': jax.random.normal(ks[5], (E, D, R), dtype=jnp.float32) * scale, 'B_r': jax.random.normal(ks[6], (E, R, D), dtype=jnp.float32) * scale, 'W_router': jax.random.normal(ks[7], (D, E), dtype=jnp.float32) * scale, 'b_router': jax.random.normal(ks[8], (E,), dtype=jnp.float32) * scale}
    _L1_ffn_all = _L1_ffn_setup()
    _L1_ffn_in = {k: v for k, v in _L1_ffn_all.items() if k in ('W_base', 'b_base', 'A_s', 'B_s', 'A_r', 'B_r', 'W_router', 'b_router')}
    del _L1_ffn_all
    return {'x': x, 'ctx_2048': ctx_2048, 'L0_attn_Wq': _L0_attn_in['Wq'], 'L0_attn_Wk': _L0_attn_in['Wk'], 'L0_attn_Wv': _L0_attn_in['Wv'], 'L0_attn_Wo': _L0_attn_in['Wo'], 'L0_attn_rms_w': _L0_attn_in['rms_w'], 'L0_xattn_ssm_kernel': _L0_xattn_in['ssm_kernel'], 'L0_xattn_D': _L0_xattn_in['D'], 'L0_ffn_gate_w': _L0_ffn_in['gate_w'], 'L0_ffn_shared_wg': _L0_ffn_in['shared_wg'], 'L0_ffn_shared_wu': _L0_ffn_in['shared_wu'], 'L0_ffn_shared_wd': _L0_ffn_in['shared_wd'], 'L0_ffn_exp_wg': _L0_ffn_in['exp_wg'], 'L0_ffn_exp_wu': _L0_ffn_in['exp_wu'], 'L0_ffn_exp_wd': _L0_ffn_in['exp_wd'], 'L1_attn_w_qkv': _L1_attn_in['w_qkv'], 'L1_attn_w_out': _L1_attn_in['w_out'], 'L1_attn_b_out': _L1_attn_in['b_out'], 'L1_xattn_Wq': _L1_xattn_in['Wq'], 'L1_xattn_Wk': _L1_xattn_in['Wk'], 'L1_xattn_Wv': _L1_xattn_in['Wv'], 'L1_xattn_Wfc': _L1_xattn_in['Wfc'], 'L1_xattn_bfc': _L1_xattn_in['bfc'], 'L1_ffn_W_base': _L1_ffn_in['W_base'], 'L1_ffn_b_base': _L1_ffn_in['b_base'], 'L1_ffn_A_s': _L1_ffn_in['A_s'], 'L1_ffn_B_s': _L1_ffn_in['B_s'], 'L1_ffn_A_r': _L1_ffn_in['A_r'], 'L1_ffn_B_r': _L1_ffn_in['B_r'], 'L1_ffn_W_router': _L1_ffn_in['W_router'], 'L1_ffn_b_router': _L1_ffn_in['b_router']}

def reference(x, ctx_2048, L0_attn_Wq, L0_attn_Wk, L0_attn_Wv, L0_attn_Wo, L0_attn_rms_w, L0_xattn_ssm_kernel, L0_xattn_D, L0_ffn_gate_w, L0_ffn_shared_wg, L0_ffn_shared_wu, L0_ffn_shared_wd, L0_ffn_exp_wg, L0_ffn_exp_wu, L0_ffn_exp_wd, L1_attn_w_qkv, L1_attn_w_out, L1_attn_b_out, L1_xattn_Wq, L1_xattn_Wk, L1_xattn_Wv, L1_xattn_Wfc, L1_xattn_bfc, L1_ffn_W_base, L1_ffn_b_base, L1_ffn_A_s, L1_ffn_B_s, L1_ffn_A_r, L1_ffn_B_r, L1_ffn_W_router, L1_ffn_b_router):
    import jax
    import jax.numpy as jnp

    def _L0_attn_ref(x, Wq, Wk, Wv, Wo, rms_w):
        import math
        import jax, jax.numpy as jnp
        import numpy as np
        EMBED_DIM = 512
        NUM_HEADS = 16
        HEAD_DIM = EMBED_DIM // NUM_HEADS
        CHUNK = 128
        RMS_EPS = 1e-05

        def _build_slopes(n):

            def pow2(n):
                start = 2.0 ** (-2.0 ** (-(math.log2(n) - 3)))
                return [start * start ** i for i in range(n)]
            if math.log2(n).is_integer():
                s = pow2(n)
            else:
                closest = 2 ** math.floor(math.log2(n))
                s = pow2(closest) + pow2(2 * closest)[0::2][:n - closest]
            return jnp.asarray(s, dtype=jnp.float32)

        def _rotary(x_BTHD, offset=0):
            T, D = (x_BTHD.shape[1], x_BTHD.shape[-1])
            freq = (1.0 / 1024.0) ** jnp.linspace(0.0, 1.0, D // 4, dtype=jnp.float32)
            freq = jnp.concatenate([freq, jnp.zeros(D // 4, dtype=jnp.float32)])
            t = jnp.arange(offset, offset + T, dtype=jnp.float32)
            theta = t[:, None] * freq[None, :]
            cos = jnp.cos(theta)[None, :, None, :]
            sin = jnp.sin(theta)[None, :, None, :]
            x1, x2 = jnp.split(x_BTHD.astype(jnp.float32), 2, axis=-1)
            y1 = x1 * cos + x2 * sin
            y2 = -x1 * sin + x2 * cos
            return jnp.concatenate([y1, y2], axis=-1).astype(x_BTHD.dtype)

        def _lightning_attn(q, k, v, slopes):
            B, H, T, D = q.shape
            C = CHUNK
            NC = T // C
            r = jnp.exp(-slopes)
            i = jnp.arange(C, dtype=jnp.float32)
            q_decay = r[:, None] ** (i[None, :] + 1.0)
            k_decay = r[:, None] ** (C - 1.0 - i[None, :])
            diff = i[:, None] - i[None, :]
            mask = diff >= 0
            dmask = jnp.where(mask[None], r[:, None, None] ** jnp.where(mask, diff, 0.0)[None], 0.0)
            r_C = r ** float(C)

            def reshape_chunks(x):
                return x.reshape(B, H, NC, C, D).transpose(2, 0, 1, 3, 4)
            qc, kc, vc = (reshape_chunks(q), reshape_chunks(k), reshape_chunks(v))

            def step(kv, qkv):
                qi, ki, vi = qkv
                inter = jnp.einsum('bhcd,bhde->bhce', qi * q_decay[None, :, :, None], kv)
                scores = jnp.einsum('bhcd,bhsd->bhcs', qi, ki) * dmask[None]
                intra = jnp.einsum('bhcs,bhse->bhce', scores, vi)
                kv_new = r_C[None, :, None, None] * kv + jnp.einsum('bhcd,bhce->bhde', ki * k_decay[None, :, :, None], vi)
                return (kv_new, inter + intra)
            kv0 = jnp.zeros((B, H, D, D), dtype=q.dtype)
            _, out = jax.lax.scan(step, kv0, (qc, kc, vc))
            return out.transpose(1, 2, 0, 3, 4).reshape(B, H, T, D)

        def _rms_norm(x, w):
            var = jnp.mean(jnp.square(x), axis=-1, keepdims=True)
            return x * jax.lax.rsqrt(var + RMS_EPS) * w
        B, T, E = x.shape
        H, D = (NUM_HEADS, HEAD_DIM)
        q = (x @ Wq).reshape(B, T, H, D)
        k = (x @ Wk).reshape(B, T, H, D)
        v = (x @ Wv).reshape(B, T, H, D)
        q = _rotary(q)
        k = _rotary(k)
        q, k, v = (t.transpose(0, 2, 1, 3) for t in (q, k, v))
        slopes = _build_slopes(H)
        attn = _lightning_attn(q, k, v, slopes)
        attn = attn.transpose(0, 2, 1, 3).reshape(B, T, E)
        attn = _rms_norm(attn, rms_w)
        return attn @ Wo

    def _L0_xattn_ref(k, v, q, ssm_kernel, D, head_dim):
        import jax, jax.numpy as jnp
        import numpy as np
        B, HD, L = k.shape
        H = HD // head_dim
        fft_size = 2 * L
        k_ = k.reshape(B, H, head_dim, L)
        v_ = v.reshape(B, H, head_dim, L)
        q_ = q.reshape(B, H, head_dim, L)
        kv = jnp.einsum('bhil,bhjl->bijhl', k_, v_)
        kv_f = jnp.fft.rfft(kv, n=fft_size)
        kernel_f = jnp.fft.rfft(ssm_kernel, n=fft_size)
        y = jnp.fft.irfft(kv_f * kernel_f, n=fft_size)[..., :L]
        out = y + kv * D[None, None, None, :, None]
        out = jnp.einsum('bijhl,bhil->bjhl', out, q_)
        out = jnp.transpose(out, (0, 2, 1, 3)).reshape(B, H * head_dim, L)
        return out.astype(k.dtype)

    def _L0_ffn_ref(hidden_states, gate_w, shared_wg, shared_wu, shared_wd, exp_wg, exp_wu, exp_wd):
        import jax, jax.numpy as jnp
        import numpy as np
        HIDDEN = 512
        N_EXPERTS = 8
        N_SHARED = 2
        TOP_K = 2
        MOE_FF = 352
        SHARED_FF = N_SHARED * MOE_FF
        SCALE = 2.5
        BATCH, SEQ = (2, 256)
        B, S, D = hidden_states.shape
        T = B * S
        xf = hidden_states.reshape(T, D)
        scores = jax.nn.sigmoid(xf @ gate_w.T)
        topk_w, topk_idx = jax.lax.top_k(scores, TOP_K)
        topk_w = topk_w / (topk_w.sum(axis=-1, keepdims=True) + 1e-20)
        topk_w = topk_w * SCALE
        shared_out = jax.nn.silu(xf @ shared_wg.T) * (xf @ shared_wu.T) @ shared_wd.T
        h = jax.nn.silu(jnp.einsum('td,efd->etf', xf, exp_wg)) * jnp.einsum('td,efd->etf', xf, exp_wu)
        all_out = jnp.einsum('etf,edf->etd', h, exp_wd)
        picked = all_out[topk_idx, jnp.arange(T)[:, None]]
        routed_out = (topk_w[..., None] * picked).sum(axis=1)
        return (shared_out + routed_out).reshape(B, S, D)

    def _L1_attn_ref(x, w_qkv, w_out, b_out):
        import jax, jax.numpy as jnp
        import numpy as np
        EMBED_DIM = 512
        NUM_HEADS = 16
        BLOCK_SIZE = 128

        def _flash_attention_v2(q, k, v, block_size, scale):
            B, H, S, D = q.shape
            nb = S // block_size
            qb = q.reshape(B, H, nb, block_size, D)
            kb = k.reshape(B, H, nb, block_size, D).transpose(2, 0, 1, 3, 4)
            vb = v.reshape(B, H, nb, block_size, D).transpose(2, 0, 1, 3, 4)
            out0 = jnp.zeros_like(qb)
            l0 = jnp.zeros((B, H, nb, block_size, 1), dtype=q.dtype)
            m0 = jnp.full((B, H, nb, block_size, 1), -jnp.inf, dtype=q.dtype)

            def step(carry, kv):
                out, l, m = carry
                k_j, v_j = kv
                s = jnp.einsum('bhnqd,bhkd->bhnqk', qb, k_j) * scale
                m_ij = jnp.max(s, axis=-1, keepdims=True)
                p = jnp.exp(s - m_ij)
                l_ij = jnp.sum(p, axis=-1, keepdims=True)
                m_new = jnp.maximum(m, m_ij)
                alpha = jnp.exp(m - m_new)
                beta = jnp.exp(m_ij - m_new)
                l_new = alpha * l + beta * l_ij
                pv = jnp.einsum('bhnqk,bhkd->bhnqd', p, v_j)
                out_new = alpha * l / l_new * out + beta * l_ij / l_new * pv
                return ((out_new, l_new, m_new), None)
            (out, _, _), _ = jax.lax.scan(step, (out0, l0, m0), (kb, vb))
            return out.reshape(B, H, S, D)
        B, S, E = x.shape
        H = NUM_HEADS
        D = E // H
        scale = 1.0 / np.sqrt(D).astype(np.float32)
        qkv = (x @ w_qkv.T).reshape(B, S, 3, H, D)
        q, k, v = jnp.moveaxis(qkv, 2, 0)
        q = q.transpose(0, 2, 1, 3)
        k = k.transpose(0, 2, 1, 3)
        v = v.transpose(0, 2, 1, 3)
        out = _flash_attention_v2(q, k, v, BLOCK_SIZE, scale)
        out = out.transpose(0, 2, 1, 3).reshape(B, S, E)
        return out @ w_out.T + b_out

    def _L1_xattn_ref(q, k, v, Wq, Wk, Wv, Wfc, bfc):
        import jax, jax.numpy as jnp
        import numpy as np
        import math
        EMBED = 512
        HEADS = 32
        GROUPS = 8
        GROUP_HEADS = HEADS // GROUPS
        HEAD_DIM = EMBED // HEADS
        B, S = (4, 256)
        N, S_, _ = q.shape
        qh = (q @ Wq.T).reshape(N, S_, HEADS, HEAD_DIM).transpose(0, 2, 1, 3)
        kh = (k @ Wk.T).reshape(N, S_, GROUPS, HEAD_DIM).transpose(0, 2, 1, 3)
        vh = (v @ Wv.T).reshape(N, S_, GROUPS, HEAD_DIM).transpose(0, 2, 1, 3)
        kh = jnp.repeat(kh, GROUP_HEADS, axis=1)
        vh = jnp.repeat(vh, GROUP_HEADS, axis=1)
        score = jnp.einsum('bhqd,bhkd->bhqk', qh, kh) / math.sqrt(HEAD_DIM)
        attn = jax.nn.softmax(score, axis=-1)
        out = jnp.einsum('bhqk,bhkd->bhqd', attn, vh)
        out = out.transpose(0, 2, 1, 3).reshape(N, S_, EMBED)
        return out @ Wfc.T + bfc

    def _L1_ffn_ref(x, W_base, b_base, A_s, B_s, A_r, B_r, W_router, b_router):
        import jax, jax.numpy as jnp
        import numpy as np
        B, S, D, E, R, TOP_K = (4, 1024, 512, 6, 16, 2)
        base_out = jax.lax.stop_gradient(jnp.einsum('bsd,df->bsf', x, W_base) + b_base)
        shared_out = jnp.einsum('bsr,rf->bsf', jnp.einsum('bsd,dr->bsr', x, A_s), B_s)
        gates = jax.nn.softmax(jnp.einsum('bsd,de->bse', x, W_router) + b_router, axis=-1)
        topk_w, topk_i = jax.lax.top_k(gates, TOP_K)
        w_per_e = jnp.sum(topk_w[..., None] * jax.nn.one_hot(topk_i, E, dtype=x.dtype), axis=2)
        h = jnp.einsum('bsd,edr->bser', x, A_r)
        hw = h * w_per_e[..., None]
        routed_out = jnp.einsum('bser,erf->bsf', hw, B_r)
        return base_out + shared_out + routed_out
    x = x + _L0_attn_ref(_layernorm(x, axis=-1), L0_attn_Wq, L0_attn_Wk, L0_attn_Wv, L0_attn_Wo, L0_attn_rms_w)
    x = x + _L0_xattn_ref(ctx_2048, ctx_2048, _layernorm(x, axis=-1), L0_xattn_ssm_kernel, L0_xattn_D, 8)
    x = x + _L0_ffn_ref(_layernorm(x, axis=-1), L0_ffn_gate_w, L0_ffn_shared_wg, L0_ffn_shared_wu, L0_ffn_shared_wd, L0_ffn_exp_wg, L0_ffn_exp_wu, L0_ffn_exp_wd)
    x = x + _L1_attn_ref(_layernorm(x, axis=-1), L1_attn_w_qkv, L1_attn_w_out, L1_attn_b_out)
    x = x + _L1_xattn_ref(_layernorm(x, axis=-1), ctx_2048, ctx_2048, L1_xattn_Wq, L1_xattn_Wk, L1_xattn_Wv, L1_xattn_Wfc, L1_xattn_bfc)
    x = x + _L1_ffn_ref(_layernorm(x, axis=-1), L1_ffn_W_base, L1_ffn_b_base, L1_ffn_A_s, L1_ffn_B_s, L1_ffn_A_r, L1_ffn_B_r, L1_ffn_W_router, L1_ffn_b_router)
    return x

_drawn_inputs = setup_inputs


def setup_inputs(seed=0):
    import zlib

    import numpy as np

    out = dict(_drawn_inputs(seed))
    spreads = {'L0_attn_rms_w': (1.0, 0.2), 'L1_attn_b_out': (0.0, 2.0), 'L1_xattn_bfc': (0.0, 2.0)}
    factors = {'L0_ffn_gate_w': 8.0,
     'L0_ffn_shared_wg': 8.0,
     'L0_ffn_shared_wu': 8.0,
     'L0_ffn_shared_wd': 8.0,
     'L0_ffn_exp_wg': 8.0,
     'L0_ffn_exp_wu': 8.0,
     'L0_ffn_exp_wd': 8.0,
     'L1_xattn_Wq': 8.0,
     'L1_xattn_Wk': 8.0,
     'L1_xattn_Wv': 8.0,
     'L1_xattn_Wfc': 8.0,
     'L1_ffn_W_base': 6.89,
     'L1_ffn_b_base': 200.0,
     'L1_ffn_A_s': 8.0,
     'L1_ffn_B_s': 8.0,
     'L1_ffn_A_r': 8.0,
     'L1_ffn_B_r': 8.0,
     'L1_ffn_W_router': 22.705,
     'L1_ffn_b_router': 200.0}
    for name, (base, spread) in spreads.items():
        noise = np.random.default_rng([zlib.crc32(name.encode()), seed]).standard_normal(out[name].shape)
        drawn = base * np.exp(spread * noise) if base else spread * noise
        out[name] = jnp.asarray(drawn.astype(out[name].dtype))
    for name, factor in factors.items():
        out[name] = (out[name] * factor).astype(out[name].dtype)
    return out
```

```python
from contextlib import ExitStack, contextmanager

import numpy as np
import concourse.bass as bass
from concourse import mybir
from concourse.alu_op_type import AluOpType as ALU

F32 = mybir.dt.float32
U32 = mybir.dt.uint32
I32 = mybir.dt.int32
ACT = mybir.ActivationFunctionType
AX = mybir.AxisListType.X

P = 128
B, S, D = 8, 256, 512
TT = S // P
NT = B * TT
KD = D // P
HA = 16
DA = D // HA
HG = P // DA
HC, DC = 32, 8
NPAIR = DC * (DC + 1) // 2
NE, FE, FS = 8, 352, 704
FJ = [(0, 128), (128, 128), (256, 96)]
SJ = [(j * P, min(P, FS - j * P)) for j in range(-(-FS // P))]
SLOTS = 2 * B * S // P + NE - 1
ROUTE_SCALE = 2.5
HX, DX, GX = 32, 16, 8
NR, RR = 6, 16
RW = RR * (NR + 1)
LN_EPS = 1e-5
PAD = 4096


class Marks:

    def __init__(self, nc, stack, known):
        self.nc, self.stack, self.known = nc, stack, known
        self.sems, self.base, self.here, self.names, self.per = {}, {}, {}, {}, {}
        self.rings = {}
        self.scope, self.turn, self.turns, self.seen = 0, None, 1, {}

    def sem(self, key):
        if key not in self.sems:
            self.sems[key] = self.stack.enter_context(self.nc.semaphore(key))
        return self.sems[key]

    def start(self):
        for key in (self.known or self).base:
            if self.pad(key):
                self.nc.sync.sem_inc(self.sem(key), self.pad(key))

    @staticmethod
    def pad(key):
        return 0 if key.startswith("g_") else PAD

    def mark(self, key, name, instruction, by=1):
        instruction.then_inc(self.sem(key), by)
        self.here[key] = self.here.get(key, 0) + by
        assert name not in self.names, name
        self.names[name] = (key, self.scope, self.here[key])

    def wait(self, eng, *names, ago=0):
        if self.known is None:
            return
        for name in names:
            key, scope, k = self.known.names[name]
            base, per, turns = self.known.per[scope][key]
            who = (id(eng), key)
            if scope == self.scope and self.turn is not None:
                now = k - ago * per
                if self.seen.get((who, scope), -10**9) >= now:
                    continue
                self.seen[(who, scope)] = now
                eng.wait_ge(self.sem(key), self.turn * per + (self.pad(key) + base + now))
            else:
                now = base + (turns - 1) * per + k
                if self.seen.get(who, -1) >= now:
                    continue
                if self.turn is None:
                    self.seen[who] = now
                eng.wait_ge(self.sem(key), self.pad(key) + now)

    def close(self):
        self.per[self.scope] = {k: (self.base.get(k, 0), n, self.turns) for k, n in self.here.items()}
        for k, n in self.here.items():
            self.base[k] = self.base.get(k, 0) + n * self.turns
        self.scope, self.here, self.turn, self.turns = self.scope + 1, {}, None, 1

    @contextmanager
    def loop(self, turns):
        self.close()
        self.turns = turns
        with self.nc.Fori(0, turns) as i:
            self.turn = i
            yield i
        self.close()


class Ring:

    def __init__(self, marks, name, buffers):
        self.marks, self.name, self.buffers = marks, name, buffers
        self.scope, self.uses = None, []

    def take(self, eng, released):
        m = self.marks
        if self.scope != m.scope:
            self.scope, self.uses = m.scope, []
            m.rings[(self.name, self.scope)] = self.uses
        n, size = len(self.uses), len(self.buffers)
        self.uses.append(released)
        if n >= size:
            m.wait(eng, self.uses[n - size])
        elif m.turn is not None and m.known is not None:
            before = m.known.rings[(self.name, self.scope)]
            last = [r for k, r in enumerate(before) if k % size == n]
            m.wait(eng, last[-1], ago=1)
        return self.buffers[n % size]


def bc(ap, shape, at):
    return ap.unsqueeze(at).broadcast_to(shape)


def build(nc, io, known):
    pe, act, dve, pool, sp = nc.tensor, nc.scalar, nc.vector, nc.gpsimd, nc.sync
    with ExitStack() as whole:
        M = Marks(nc, whole, known)
        sb = lambda st, name, shape, dt=F32: st.enter_context(nc.sbuf_tensor(name, shape, dt))
        dram = lambda name, shape, dt=F32: nc.dram_tensor(name, shape, dt, kind="Internal").ap()
        psum = whole.enter_context(nc.psum_tensor("psum", [P, 8, 512], F32))
        banks = Ring(M, "bank", [psum[:, k, :] for k in range(8)])
        M.start()

        ident = sb(whole, "ident", [P, P])
        ones = sb(whole, "ones", [P, P])
        mhalf = sb(whole, "mhalf", [P, TT])
        ln_st = sb(whole, "ln_st", [P, TT, 6])
        ln_mv = sb(whole, "ln_mv", [P, TT, 2])
        ln_ve = sb(whole, "ln_ve", [P, TT])
        ln_rs = sb(whole, "ln_rs", [P, TT])
        slot_of = sb(whole, "slot_of", [P, 2, NT], U32)
        w_of = sb(whole, "w_of", [P, 2, NT])

        tile_expert = sb(whole, "tile_expert", [P, SLOTS], I32)

        x1_d = dram("x1_d", [B, S, D])
        x2s_d = dram("x2s_d", [B, S, D])
        xn3_d = dram("xn3_d", [B * S, D])
        ctxT_d = dram("ctxT_d", [B, P, KD, S])
        kpad_d = dram("kpad_d", [HC, P + D])
        slot_token_d = dram("slot_token_d", [SLOTS * P, 1], U32)
        ys_d = dram("ys_d", [SLOTS * P, D])

        tokens = lambda ap: ap.rearrange("b (t p) d -> b p t d", p=P)
        rows = lambda ap: ap.rearrange("(k p) n -> p k n", p=P)

        M.mark("d_const", "ident", sp.dma_start(ident[:, :], io["ident"]), 16)
        M.mark("dve", "ones", dve.memset(ones[:, :], 1.0))
        M.mark("dve", "mhalf", dve.memset(mhalf[:, :], -0.5))
        M.wait(pe, "ident", "ones")
        M.wait(pool, "mhalf")
        M.wait(dve, "ones")

        spare = {n: Ring(M, "spare_" + n, [sb(whole, f"spare_{n}{k}", [P, 1]) for k in range(2)]) for n in ("dve", "pool")}

        def wait_apart(eng, name):
            key = "dve" if eng is dve else "pool"
            column = spare[key].take(eng, "apart_" + name)
            M.wait(eng, name)
            M.mark(key, "apart_" + name, eng.tensor_tensor(column[:, :], ones[:, 0:1], ones[:, 0:1], ALU.mult))

        def layer_norm(tag, src, dst):
            for t in range(TT):
                i = dve.bn_stats(ln_st[:, t, :], src[:, t, :])
            M.mark("dve", tag + "_st", i)
            wait_apart(dve, tag + "_st")
            for t in range(TT):
                i = dve.bn_aggr(ln_mv[:, t, :], ln_st[:, t, :])
            M.mark("dve", tag + "_mv", i)
            M.wait(dve, tag + "_mv")
            M.mark("dve", tag + "_ve", dve.tensor_scalar(ln_ve[:, :], ln_mv[:, :, 1], LN_EPS, None, ALU.add))
            M.wait(pool, tag + "_ve")
            M.mark("pool", tag + "_rs", pool.tensor_tensor(ln_rs[:, :], ln_ve[:, :], mhalf[:, :], ALU.pow))
            M.wait(dve, tag + "_rs")
            for t in range(TT):
                M.mark("dve", f"{tag}_n{t}", dve.tensor_scalar(
                    dst[:, t, :], src[:, t, :], ln_mv[:, t, 0:1], ln_rs[:, t:t + 1], ALU.subtract, ALU.mult))

        def turn(tag, src, ready, write):
            for t in range(TT):
                M.wait(pe, ready(t))
                bank = banks.take(pe, f"{tag}_T{t}")
                for k in range(KD):
                    i = pe.transpose(bank[:, k * P:(k + 1) * P], src[:, t, k * P:(k + 1) * P], ident[:, :])
                M.mark("pe", f"{tag}_P{t}", i)
                write(t, bank.rearrange("p (k c) -> p k c", k=KD))

        def route(logits):
            with ExitStack() as st:
                step = [0]

                def done(key, eng, ins):
                    step[0] += 1
                    M.mark(key, f"route{step[0]}", ins)
                    M.wait(eng, f"route{step[0]}")
                    return f"route{step[0]}"

                def V(ins):
                    return done("dve", dve, ins)

                full = lambda name: sb(st, name, [P, NT, NE])
                few = lambda name: sb(st, name, [P, NT])
                score, eq, h1, h2, a2, pre, tot, run, run2 = (full("r_" + n) for n in (
                    "score", "eq", "h1", "h2", "a2", "pre", "tot", "run", "run2"))
                m1, m2, key, den = (few("r_" + n) for n in ("m1", "m2", "key", "den"))
                tri = sb(st, "tri", [P, P])
                rconst = sb(st, "rconst", [P, NE + NT + SLOTS])
                cnt = sb(st, "cnt", [P, NE, NT])
                tiles, first, first2 = (sb(st, "r_" + n, [P, NE]) for n in ("tiles", "first", "first2"))
                et = sb(st, "et", [P, SLOTS, NE])
                etf = sb(st, "etf", [P, SLOTS])
                ids = sb(st, "ids", [P, NT], U32)
                zero = sb(st, "zero", [P, SLOTS], U32)
                at = sb(st, "at", [P, 2 * NT, 1], U32)
                M.mark("d_tri", "tri", sp.dma_start(tri[:, :], io["tri"]), 16)
                M.mark("d_rconst", "rconst", sp.dma_start(rconst[:, :], io["rconst"]), 16)
                M.mark("d_ids", "ids", sp.dma_start(ids[:, :], io["token_ids"]), 16)
                M.mark("dve", "zero", dve.memset(zero[:, :], 0))
                M.wait(sp, "zero")
                M.mark("d_zero", "slots0", sp.dma_start(slot_token_d.rearrange("(p n) o -> p (n o)", p=P), zero[:, :]), 16)
                M.wait(act, "logits")
                M.mark("act", "score", act.activation(score[:, :, :], logits[:, :, :], ACT.Sigmoid))
                M.wait(dve, "score", "rconst")
                rank8 = bc(rconst[:, 0:NE], [P, NT, NE], 1)
                by_e = lambda t: bc(t[:, :], [P, NT, NE], 2)
                for m, hot in ((m1, h1), (m2, h2)):
                    V(dve.tensor_reduce(m[:, :], score[:, :, :], AX, ALU.max))
                    V(dve.tensor_tensor(eq[:, :, :], score[:, :, :], by_e(m), ALU.is_equal))
                    V(dve.tensor_tensor(eq[:, :, :], eq[:, :, :], rank8, ALU.mult))
                    V(dve.tensor_reduce(key[:, :], eq[:, :, :], AX, ALU.max))
                    V(dve.tensor_tensor(hot[:, :, :], eq[:, :, :], by_e(key), ALU.is_equal))
                    if m is m1:
                        V(dve.scalar_tensor_tensor(score[:, :, :], hot[:, :, :], -2.0, score[:, :, :], ALU.mult, ALU.add))
                V(dve.tensor_tensor(den[:, :], m1[:, :], m2[:, :], ALU.add))
                V(dve.tensor_scalar(den[:, :], den[:, :], 1e-20, None, ALU.add))
                V(dve.reciprocal(den[:, :], den[:, :]))
                for c, m in enumerate((m1, m2)):
                    V(dve.scalar_tensor_tensor(w_of[:, c, :], m[:, :], ROUTE_SCALE, den[:, :], ALU.mult, ALU.mult))
                at_a2 = V(dve.tensor_tensor(a2[:, :, :], h1[:, :, :], h2[:, :, :], ALU.add))
                M.wait(pe, at_a2, "tri")
                flat = a2[:, :, :].rearrange("p t e -> p (t e)")
                bank_p, bank_t = banks.take(pe, "r_tot"), banks.take(pe, "r_tot ")
                pe.matmul(bank_p[:, 0:NT * NE], tri[:, :], flat, start=True, stop=True)
                M.mark("pe", "r_counts", pe.matmul(bank_t[:, 0:NT * NE], ones[:, :], flat, start=True, stop=True))
                M.wait(dve, "r_counts")
                dve.tensor_copy(pre[:, :, :].rearrange("p t e -> p (t e)"), bank_p[:, 0:NT * NE])
                dve.tensor_copy(tot[:, :, :].rearrange("p t e -> p (t e)"), bank_t[:, 0:NT * NE])
                V(dve.tensor_copy(run[:, :, :].rearrange("p t e -> p (t e)"), bank_t[:, 0:NT * NE]))
                M.names["r_tot"] = M.names["r_tot "] = M.names[f"route{step[0]}"]
                src, dst, d = run, run2, 1
                while d < NT:
                    dve.tensor_copy(dst[:, 0:d, :], src[:, 0:d, :])
                    V(dve.tensor_tensor(dst[:, d:, :], src[:, d:, :], src[:, 0:NT - d, :], ALU.add))
                    src, dst, d = dst, src, 2 * d
                V(dve.tensor_tensor(cnt[:, :, :], bc(src[:, NT - 1, :], [P, NE, NT], 2),
                                    bc(rconst[:, NE:NE + NT], [P, NE, NT], 1), ALU.is_gt))
                V(dve.tensor_reduce(tiles[:, :], cnt[:, :, :], AX, ALU.add))
                V(dve.tensor_copy(first[:, :], tiles[:, :]))
                fs, fd, d = first, first2, 1
                while d < NE:
                    dve.tensor_copy(fd[:, 0:d], fs[:, 0:d])
                    V(dve.tensor_tensor(fd[:, d:], fs[:, d:], fs[:, 0:NE - d], ALU.add))
                    fs, fd, d = fd, fs, 2 * d
                V(dve.tensor_tensor(fs[:, :], fs[:, :], tiles[:, :], ALU.subtract))
                V(dve.tensor_tensor(et[:, :, :], bc(rconst[:, NE + NT:], [P, SLOTS, NE], 2),
                                    bc(fs[:, :], [P, SLOTS, NE], 1), ALU.is_ge))
                V(dve.tensor_reduce(etf[:, :], et[:, :, :], AX, ALU.add))
                V(dve.tensor_scalar(tile_expert[:, :], etf[:, :], -1.0, None, ALU.add))
                V(dve.tensor_tensor(pre[:, :, :], pre[:, :, :], src[:, :, :], ALU.add))
                V(dve.tensor_tensor(pre[:, :, :], pre[:, :, :], tot[:, :, :], ALU.subtract))
                V(dve.tensor_scalar(fd[:, :], fs[:, :], float(P), None, ALU.mult))
                V(dve.tensor_tensor(pre[:, :, :], pre[:, :, :], bc(fd[:, :], [P, NT, NE], 1), ALU.add))
                for c, hot in enumerate((h1, h2)):
                    V(dve.tensor_tensor(eq[:, :, :], pre[:, :, :], hot[:, :, :], ALU.mult))
                    V(dve.tensor_reduce(key[:, :], eq[:, :, :], AX, ALU.add))
                    V(dve.tensor_copy(slot_of[:, c, :], key[:, :]))
                    last = V(dve.tensor_copy(at[:, c * NT:(c + 1) * NT, 0], key[:, :]))
                M.wait(pool, last, "ids", "slots0")
                for c in range(2):
                    for t in range(NT):
                        i = pool.indirect_dma_start(
                            out=slot_token_d, out_offset=bass.IndirectOffsetOnAxis(ap=at[:, c * NT + t, :], axis=0),
                            in_=ids[:, t:t + 1], in_offset=None)
                        M.mark("g_scatter", f"scatter{c}_{t}", i, 16)
                M.wait(pool, f"scatter1_{NT - 1}")

        with ExitStack() as st12:
            ctxT = sb(st12, "ctxT", [P, KD, B, S])
            q2T = sb(st12, "q2T", [P, KD, B, S])
            with ExitStack() as st:
                w = sb(st, "w", [P, 4, KD, D])
                dmask = sb(st, "dmask", [P, HA, 3 * P])
                rot = sb(st, "rot", [P, 3, TT, DA // 2])
                rmsw = sb(st, "rmsw", [P, KD])
                kpad = sb(st, "kpad", [HC, P + D])
                skip = sb(st, "skip", [HC, 1])
                xin = sb(st, "xin", [P, TT, D])
                cin = sb(st, "cin", [P, TT, D])
                xn = sb(st, "xn", [P, TT, D])
                xnT = sb(st, "xnT", [P, KD, S])
                qk = [sb(st, f"qk{n}", [P, TT, D]) for n in range(2)]
                qkT = [sb(st, f"qkT{n}", [P, KD, S]) for n in range(2)]
                v = sb(st, "v", [P, TT, D])
                tmp = [Ring(M, f"rot{n}", [sb(st, f"rot{n}{k}", [P, D]) for k in range(2)]) for n in range(2)]
                dec = Ring(M, "dec", [sb(st, f"dec{k}", [P, 3 * P]) for k in range(4)])
                oT = sb(st, "oT", [P, KD, S])
                sq = sb(st, "sq", [P, KD, S])
                sq2 = sb(st, "sq2", [P, 2, S])
                ss = sb(st, "ss", [P, TT])
                rr = sb(st, "rr", [P, TT])
                x1 = sb(st, "x1", [P, TT, D])

                M.mark("dve", "kpad0", dve.memset(kpad[:, :], 0.0))
                M.wait(sp, "kpad0")
                M.mark("d_kpad", "kpad_in", sp.dma_start(kpad[:, P:P + D], io["ssm_kernel"]), 16)
                M.mark("d_skip", "skip_in", sp.dma_start(skip[:, :], io["skip"]), 16)
                M.wait(dve, "kpad_in", "skip_in")
                M.mark("dve", "kpad", dve.tensor_tensor(kpad[:, P:P + 1], kpad[:, P:P + 1], skip[:, :], ALU.add))
                M.wait(sp, "kpad")
                M.mark("d_kpadout", "kpad_d", sp.dma_start(kpad_d, kpad[:, :]), 16)

                for n, name in enumerate(("rot", "wq", "wk", "wv", "dmask", "rms_w", "wo")):
                    dst = {"rot": rot[:, :, :, :], "dmask": dmask[:, :, :], "rms_w": rmsw[:, :]}.get(name)
                    if dst is None:
                        j = ("wq", "wk", "wv", "wo").index(name)
                        M.mark("d_" + name, name, sp.dma_start(w[:, j, :, :], rows(io[name])), 16)
                    else:
                        M.mark("d_" + name, name, sp.dma_start(dst, io[name]), 16)
                M.wait(pe, "wq", "wk", "wv", "wo")
                M.wait(dve, "rot", "dmask")
                M.wait(act, "rms_w")

                with M.loop(B) as b:
                    M.wait(sp, "x1_1", ago=1)
                    M.mark("d_x", "x", sp.dma_start(xin[:, :, :], tokens(io["x"])[b]), 16)
                    M.wait(sp, "ctx_P1", ago=1)
                    M.mark("d_c", "ctx", sp.dma_start(cin[:, :, :], tokens(io["ctx"])[b]), 16)

                    def put_ctx(t, bank):
                        M.wait(act, f"ctx_P{t}")
                        M.mark("act", f"ctx_T{t}", act.copy(ctxT[:, :, b, t * P:(t + 1) * P], bank))
                    turn("ctx", cin, lambda t: "ctx", put_ctx)
                    M.wait(sp, "ctx_T1")
                    M.mark("d_ctxT", "ctxT_d", sp.dma_start(ctxT_d[b], ctxT[:, :, b, :]), 16)

                    M.wait(dve, "x")
                    M.wait(dve, "q2_P1", ago=1)
                    layer_norm("ln1", xin, xn)
                    M.wait(act, "v1_done", ago=1)

                    def put_xnT(t, bank):
                        M.wait(act, f"xn_P{t}")
                        M.mark("act", f"xn_T{t}", act.copy(xnT[:, :, t * P:(t + 1) * P], bank))
                    turn("xn", xn, lambda t: f"ln1_n{t}", put_xnT)

                    for t in range(TT):
                        M.wait(pe, f"xn_T{t}")
                        for n, name in enumerate("qkv"):
                            bank = banks.take(pe, f"{name}{t}_out")
                            for k in range(KD):
                                i = pe.matmul(bank, xnT[:, k, t * P:(t + 1) * P], w[:, n, k, :],
                                              start=k == 0, stop=k == KD - 1)
                            M.mark("pe", f"{name}{t}_done", i)
                            if name == "v":
                                M.wait(act, f"v{t}_done")
                                M.wait(act, "av15", ago=1)
                                M.mark("act", f"v{t}_out", act.copy(v[:, t, :], bank))
                                continue
                            tag = f"{name}{t}"
                            ta = tmp[0].take(dve, tag + "_rot")
                            tb = tmp[1].take(dve, tag + "_rot")
                            M.wait(dve, tag + "_done")
                            half = [P, D // (DA // 2), DA // 2]
                            dve.tensor_tensor(ta[:, :].rearrange("p (h d) -> p h d", d=DA // 2),
                                              bank.rearrange("p (h d) -> p h d", d=DA // 2),
                                              bc(rot[:, 0, t, :], half, 1), ALU.mult)
                            b4 = bank.rearrange("p (h e d) -> p h e d", e=2, d=DA // 2)
                            t4 = tb[:, :].rearrange("p (h e d) -> p h e d", e=2, d=DA // 2)
                            quarter = [P, HA, DA // 2]
                            dve.tensor_tensor(t4[:, :, 0, :], b4[:, :, 1, :], bc(rot[:, 1, t, :], quarter, 1), ALU.mult)
                            M.mark("dve", tag + "_out", dve.tensor_tensor(
                                t4[:, :, 1, :], b4[:, :, 0, :], bc(rot[:, 2, t, :], quarter, 1), ALU.mult))
                            M.wait(pool, tag + "_out")
                            M.wait(pool, f"{name}T{t}_P", ago=1)
                            M.mark("pool", tag + "_rot", pool.tensor_tensor(qk[n][:, t, :], ta[:, :], tb[:, :], ALU.add))
                    for t in range(TT):
                        for n, name in enumerate("qk"):
                            M.wait(pe, f"{name}{t}_rot")
                            bank = banks.take(pe, f"{name}T{t}")
                            for k in range(KD):
                                i = pe.transpose(bank[:, k * P:(k + 1) * P], qk[n][:, t, k * P:(k + 1) * P], ident[:, :])
                            M.mark("pe", f"{name}T{t}_P", i)
                            M.wait(act, f"{name}T{t}_P")
                            M.mark("act", f"{name}T{t}", act.copy(
                                qkT[n][:, :, t * P:(t + 1) * P], bank.rearrange("p (k c) -> p k c", k=KD)))
                    qT, kT = qkT

                    decayed, pending = {}, {}

                    def scores(h):
                        m, i0 = h // HG, DA * (h % HG)
                        r = slice(i0, i0 + DA)
                        bank = banks.take(pe, f"dec{h}")
                        M.wait(pe, "qT1", "kT1")
                        pe.matmul(bank[:, 0:S], kT[r, m, 0:P], qT[r, m, :], start=True, stop=True)
                        M.mark("pe", f"s{h}", pe.matmul(bank[:, S:S + P], kT[r, m, P:S], qT[r, m, P:S],
                                                       start=True, stop=True))
                        buf = decayed[h] = dec.take(dve, f"av{h}")
                        M.wait(dve, f"s{h}")
                        M.mark("dve", f"dec{h}", dve.tensor_tensor(buf[:, :], bank[:, 0:3 * P], dmask[:, h, :], ALU.mult))

                    def values(h):
                        m, i0 = h // HG, DA * (h % HG)
                        if h % HG == 0:
                            pending[m] = banks.take(pe, f"sq{m}")
                        out, buf = pending[m], decayed[h]
                        M.wait(pe, f"dec{h}", "v0_out", "v1_out")
                        c = slice(h * DA, (h + 1) * DA)
                        pe.matmul(out[i0:i0 + DA, 0:S], v[:, 0, c], buf[:, 0:S], start=True, stop=False,
                                  skip_group_check=True)
                        M.mark("pe", f"av{h}", pe.matmul(out[i0:i0 + DA, P:S], v[:, 1, c], buf[:, S:S + P],
                                                        start=False, stop=True, skip_group_check=True))
                        if h % HG == HG - 1:
                            M.wait(act, f"av{h}")
                            M.wait(act, "o1_done", ago=1)
                            M.wait(act, "sq2b", ago=1)
                            act.activation(oT[:, m, :], out[:, 0:S], ACT.Copy, scale=rmsw[:, m:m + 1])
                            M.mark("act", f"sq{m}", act.activation(sq[:, m, :], out[:, 0:S], ACT.Square))

                    for h in range(HA + 2):
                        if h < HA:
                            scores(h)
                        if h >= 2:
                            values(h - 2)

                    M.wait(pe, "sq3")
                    projected = []
                    for t in range(TT):
                        bank = banks.take(pe, f"x1_{t}")
                        projected.append(bank)
                        for k in range(KD):
                            i = pe.matmul(bank, oT[:, k, t * P:(t + 1) * P], w[:, 3, k, :], start=k == 0, stop=k == KD - 1)
                        M.mark("pe", f"o{t}_done", i)
                    M.wait(dve, "sq3")
                    M.wait(dve, "ss_done", ago=1)
                    M.mark("dve", "sq2a", dve.tensor_tensor(sq2[:, :, :], sq[:, 0:2, :], sq[:, 2:4, :], ALU.add))
                    M.wait(dve, "sq2a")
                    M.mark("dve", "sq2b", dve.tensor_tensor(sq2[:, 0, :], sq2[:, 0, :], sq2[:, 1, :], ALU.add))
                    M.wait(pe, "sq2b")
                    bank = banks.take(pe, "ss")
                    for t in range(TT):
                        i = pe.matmul(bank[:, t:t + 1], sq2[:, 0, t * P:(t + 1) * P], ones[:, 0:1], start=True, stop=True)
                    M.mark("pe", "ss_done", i)
                    M.wait(dve, "ss_done")
                    M.mark("dve", "ss", dve.tensor_scalar(ss[:, :], bank[:, 0:TT], 1.0 / D, LN_EPS, ALU.mult, ALU.add))
                    M.wait(pool, "ss")
                    M.mark("pool", "rr", pool.tensor_tensor(rr[:, :], ss[:, :], mhalf[:, :], ALU.pow))
                    M.wait(dve, "rr")
                    M.wait(dve, "x1_st", ago=1)
                    for t in range(TT):
                        M.wait(dve, f"o{t}_done")
                        M.mark("dve", f"x1_{t}", dve.scalar_tensor_tensor(
                            x1[:, t, :], projected[t], rr[:, t:t + 1], xin[:, t, :], ALU.mult, ALU.add))
                    M.wait(sp, "x1_1")
                    M.mark("d_x1", "x1_st", sp.dma_start(tokens(x1_d)[b], x1[:, :, :]), 16)

                    M.wait(dve, "x1_1", "xn_P1")
                    layer_norm("ln2", x1, xn)

                    def put_q2(t, bank):
                        M.wait(act, f"q2_P{t}")
                        M.mark("act", f"q2_T{t}", act.copy(q2T[:, :, b, t * P:(t + 1) * P], bank))
                    turn("q2", xn, lambda t: f"ln2_n{t}", put_q2)
            nc.all_engine_barrier()

            with ExitStack() as st:
                toep = [sb(st, f"toep{u}", [P, D]) for u in range(2)]
                kv = [sb(st, f"kv{u}", [P, KD * B, NPAIR]) for u in range(2)]
                z = [sb(st, f"z{u}", [P, KD, B, DC, DC]) for u in range(2)]
                starts = [sum(DC - e for e in range(d)) for d in range(DC)]
                with M.loop(HC // 2) as hh:
                    for u in range(2):
                        M.wait(sp, f"y{u}_done", ago=1)
                        M.mark(f"d_toep{u}", f"toep{u}", sp.dma_start(
                            toep[u][:, :], bass.AP(kpad_d.tensor, (hh * 2 + u) * (P + D) + 1, [[1, P], [1, D]])), 16)
                    for u in range(2):
                        s0 = (hh * 2 + u) * DC
                        flat = ctxT[:, :, :, :].rearrange("p k b s -> p (k b) s")
                        M.wait(pool, f"y{u}_done", ago=1)
                        for d in range(DC):
                            n = DC - d
                            i = pool.tensor_tensor(kv[u][:, :, starts[d]:starts[d] + n],
                                                   flat[:, :, bass.ds(s0, n)], flat[:, :, bass.ds(s0 + d, n)], ALU.mult)
                        M.mark("pool", f"kv{u}", i)
                    for u in range(2):
                        M.wait(pe, f"kv{u}", f"toep{u}")
                        M.wait(pe, f"z{u}", ago=1)
                        for lt in range(KD):
                            for mt in range(lt + 1):
                                i = pe.matmul(psum[:, 4 * u + lt, 0:B * NPAIR], toep[u][:, (lt - mt) * P:(lt - mt + 1) * P],
                                              kv[u][:, mt * B:(mt + 1) * B, :], start=mt == 0, stop=mt == lt)
                        M.mark("pe", f"y{u}_done", i)
                    for u in range(2):
                        s0 = (hh * 2 + u) * DC
                        M.wait(dve, f"y{u}_done")
                        y = psum[:, 4 * u:4 * u + 4, 0:B * NPAIR].rearrange("p l (b n) -> p l b n", b=B)
                        zf = z[u][:, :, :, :, :].rearrange("p l b j i -> p l b (j i)")
                        for d in range(DC):
                            n = DC - d
                            pair = y[:, :, :, starts[d]:starts[d] + n]
                            i = dve.tensor_tensor(zf[:, :, :, d * DC:d * DC + (n - 1) * (DC + 1) + 1:DC + 1], pair,
                                                  q2T[:, :, :, bass.ds(s0, n)], ALU.mult)
                            if d:
                                i = dve.tensor_tensor(zf[:, :, :, d:d + (n - 1) * (DC + 1) + 1:DC + 1], pair,
                                                      q2T[:, :, :, bass.ds(s0 + d, n)], ALU.mult)
                        M.mark("dve", f"z{u}", i)
                        wait_apart(dve, f"z{u}")
                        M.mark("dve", f"acc{u}", dve.tensor_reduce(
                            q2T[:, :, :, bass.ds(s0, DC)].rearrange("p k b s -> p (k b) s"),
                            z[u][:, :, :, :, :].rearrange("p l b j i -> p (l b) j i"), AX, ALU.add))
            nc.all_engine_barrier()

            with ExitStack() as st:
                gate_up = sb(st, "gate_up", [P, KD, 2 * FS + NE])
                down = sb(st, "down", [P, len(SJ), D])
                logits = sb(st, "logits", [P, NT, NE])
                convT = sb(st, "convT", [P, KD, S])
                x1b = sb(st, "x1b", [P, TT, D])
                x2 = sb(st, "x2", [P, TT, D])
                xn3 = sb(st, "xn3", [P, TT, D])
                x3T = sb(st, "x3T", [P, KD, S])
                silu = Ring(M, "silu", [sb(st, f"silu{k}", [P, S]) for k in range(2)])
                hT = sb(st, "hT", [P, len(SJ), S])
                lgT = sb(st, "lgT", [P, S])
                x2s = sb(st, "x2s", [P, TT, D])
                M.mark("d_gu", "gate_up", sp.dma_start(gate_up[:, :, :], rows(io["shared_gate_up"])), 16)
                full = FS // P
                M.mark("d_dn", "down0", sp.dma_start(down[:, 0:full, :], rows(io["shared_down"][0:full * P, :])), 16)
                M.mark("d_dn", "down1", sp.dma_start(down[0:FS - full * P, full, :], io["shared_down"][full * P:FS, :]), 16)
                M.wait(pe, "gate_up", "down1")
                with M.loop(B) as b:
                    M.wait(sp, "x2_1", ago=1)
                    M.mark("d_x1b", "x1b", sp.dma_start(x1b[:, :, :], tokens(x1_d)[b]), 16)
                    M.wait(act, "conv_P1", ago=1)
                    M.mark("act", "convT", act.copy(convT[:, :, :], q2T[:, :, b, :]))
                    M.wait(pe, "convT")
                    M.wait(dve, "x1b")
                    M.wait(dve, "x2s_1", "xn3_st", ago=1)
                    for t in range(TT):
                        bank = banks.take(pe, f"x2_{t}")
                        for k in range(KD):
                            i = pe.transpose(bank[:, k * P:(k + 1) * P], convT[:, k, t * P:(t + 1) * P], ident[:, :])
                        M.mark("pe", f"conv_P{t}", i)
                        M.wait(dve, f"conv_P{t}")
                        M.mark("dve", f"x2_{t}", dve.tensor_tensor(x2[:, t, :], bank, x1b[:, t, :], ALU.add))
                    M.wait(dve, "x2_1")
                    layer_norm("ln3", x2, xn3)
                    M.wait(sp, "ln3_n1")
                    M.mark("d_xn3", "xn3_st", sp.dma_start(
                        xn3_d.rearrange("(b t p) d -> b p t d", t=TT, p=P)[b], xn3[:, :, :]), 16)

                    def put_x3T(t, bank):
                        M.wait(act, f"x3_P{t}")
                        M.wait(act, "up5", ago=1)
                        M.mark("act", f"x3_T{t}", act.copy(x3T[:, :, t * P:(t + 1) * P], bank))
                    turn("x3", xn3, lambda t: f"ln3_n{t}", put_x3T)

                    M.wait(pe, "x3_T1")
                    for j, (f0, fn) in enumerate(SJ):
                        last = j == len(SJ) - 1
                        gn = fn + NE if last else fn
                        bank_g = banks.take(pe, "lgT" if last else f"silu{j}")
                        for k in range(KD):
                            i = pe.matmul(bank_g[0:gn, 0:S], gate_up[:, k, f0:f0 + gn], x3T[:, k, :],
                                          start=k == 0, stop=k == KD - 1)
                        M.mark("pe", f"gate{j}", i)
                        bank_u = banks.take(pe, f"h{j}")
                        for k in range(KD):
                            i = pe.matmul(bank_u[0:fn, 0:S], gate_up[:, k, FS + NE + f0:FS + NE + f0 + fn], x3T[:, k, :],
                                          start=k == 0, stop=k == KD - 1)
                        M.mark("pe", f"up{j}", i)
                        buf = silu.take(act, f"h{j}")
                        M.wait(act, f"gate{j}")
                        M.mark("act", f"silu{j}", act.activation(buf[0:fn, :], bank_g[0:fn, 0:S], ACT.Silu))
                        if last:
                            M.wait(act, "lg_P1", ago=1)
                            M.mark("act", "lgT", act.copy(lgT[fn:gn, :], bank_g[fn:gn, 0:S]))
                        M.wait(dve, f"silu{j}", f"up{j}")
                        M.wait(dve, "dn1", ago=1)
                        M.mark("dve", f"h{j}", dve.tensor_tensor(hT[0:fn, j, :], buf[0:fn, :], bank_u[0:fn, 0:S], ALU.mult))
                    M.wait(pe, "lgT", f"h{len(SJ) - 1}")
                    for t in range(TT):
                        bank = banks.take(pe, f"x2s_{t}")
                        for j, (f0, fn) in enumerate(SJ):
                            i = pe.matmul(bank, hT[0:fn, j, t * P:(t + 1) * P], down[0:fn, j, :],
                                          start=j == 0, stop=j == len(SJ) - 1)
                        M.mark("pe", f"dn{t}", i)
                        M.wait(dve, f"dn{t}")
                        M.wait(dve, "x2s_st", ago=1)
                        M.mark("dve", f"x2s_{t}", dve.tensor_tensor(x2s[:, t, :], bank, x2[:, t, :], ALU.add))
                    bank = banks.take(pe, "logits")
                    f0, f1 = SJ[-1][1], SJ[-1][1] + NE
                    for t in range(TT):
                        i = pe.transpose(bank[:, t * NE:(t + 1) * NE], lgT[f0:f1, t * P:(t + 1) * P], ident[f0:f1, f0:f1])
                        M.mark("pe", f"lg_P{t}", i)
                    M.wait(dve, "lg_P1")
                    M.mark("dve", "logits", dve.tensor_copy(
                        logits[:, :, :].rearrange("p (b t) e -> p b (t e)", t=TT)[:, b, :], bank[:, 0:TT * NE]))
                    M.wait(sp, "x2s_1")
                    M.mark("d_x2s", "x2s_st", sp.dma_start(tokens(x2s_d)[b], x2s[:, :, :]), 16)
                M.wait(sp, "x2s_st", "xn3_st", "ctxT_d")
                route(logits)
            nc.all_engine_barrier()

        with ExitStack() as st:
            UN = 3
            wgu = sb(st, "wgu", [P, NE, KD, 2 * FE])
            wdn = sb(st, "wdn", [P, NE, len(FJ), D])
            idx = [sb(st, f"idx{u}", [P, 1], U32) for u in range(UN)]
            xg = [sb(st, f"xg{u}", [P, D]) for u in range(UN)]
            xgT = Ring(M, "xgT", [sb(st, f"xgT{u}", [P, KD, P]) for u in range(2)])
            sg = Ring(M, "sg", [sb(st, f"sg{u}", [P, FE]) for u in range(2)])
            hh_ = Ring(M, "hh", [sb(st, f"hh{u}", [P, FE]) for u in range(2)])
            hhT = Ring(M, "hhT", [sb(st, f"hhT{u}", [P, len(FJ), P]) for u in range(2)])
            ys = Ring(M, "ys", [sb(st, f"ys{u}", [P, D]) for u in range(2)])
            for e in range(NE):
                M.mark("d_wgu", f"wgu{e}", sp.dma_start(wgu[:, e, :, :], rows(io["exp_gate_up"][e])), 16)
                M.mark("d_wdn", f"wdn{e}a", sp.dma_start(wdn[:, e, 0:2, :], rows(io["exp_down"][e, 0:2 * P, :])), 16)
                M.mark("d_wdn", f"wdn{e}b", sp.dma_start(wdn[0:FE - 2 * P, e, 2, :], io["exp_down"][e, 2 * P:FE, :]), 16)
            M.wait(pe, f"wgu{NE - 1}", f"wdn{NE - 1}b")
            with M.loop(SLOTS // UN) as n:
                for u in range(UN):
                    M.wait(sp, f"xg_P{u}", ago=1)
                    M.mark(f"d_idx{u}", f"idx{u}", sp.dma_start(
                        idx[u][:, :], slot_token_d.rearrange("(n u p) o -> n u p o", u=UN, p=P)[n, u]), 16)
                    M.wait(pool, f"xg_P{u}", ago=1)
                    wait_apart(pool, f"idx{u}")
                    M.mark(f"g_xg{u}", f"xg{u}", pool.indirect_dma_start(
                        out=xg[u][:, :], out_offset=None, in_=xn3_d,
                        in_offset=bass.IndirectOffsetOnAxis(ap=idx[u][:, 0:1], axis=0)), 16)
                hidden, expert = {}, {}

                def tokens_in(u):
                    M.wait(pe, f"xg{u}")
                    bank = banks.take(pe, f"xgT{u}")
                    for k in range(KD):
                        i = pe.transpose(bank[:, k * P:(k + 1) * P], xg[u][:, k * P:(k + 1) * P], ident[:, :])
                    M.mark("pe", f"xg_P{u}", i)
                    buf = xgT.take(act, f"eu{u}")
                    M.wait(act, f"xg_P{u}")
                    M.mark("act", f"xgT{u}", act.copy(buf[:, :, :], bank.rearrange("p (k c) -> p k c", k=KD)))
                    return buf

                def gate_and_up(u, buf):
                    expert[u] = e = pe.value_load(tile_expert[0:1, bass.ds(n * UN + u, 1)], min_val=0, max_val=NE - 1)
                    M.wait(pe, f"xgT{u}")
                    bank_g, bank_u = banks.take(pe, f"sg{u}"), banks.take(pe, f"hh{u}")
                    for k in range(KD):
                        i = pe.matmul(bank_g[:, 0:FE], buf[:, k, :], wgu[:, e, k, 0:FE], start=k == 0, stop=k == KD - 1)
                    M.mark("pe", f"eg{u}", i)
                    for k in range(KD):
                        i = pe.matmul(bank_u[:, 0:FE], buf[:, k, :], wgu[:, e, k, FE:2 * FE], start=k == 0, stop=k == KD - 1)
                    M.mark("pe", f"eu{u}", i)
                    s, h = sg.take(act, f"hh{u}"), hh_.take(dve, f"hh_P{u}")
                    M.wait(act, f"eg{u}")
                    M.mark("act", f"sg{u}", act.activation(s[:, :], bank_g[:, 0:FE], ACT.Silu))
                    M.wait(dve, f"sg{u}", f"eu{u}")
                    M.mark("dve", f"hh{u}", dve.tensor_tensor(h[:, :], s[:, :], bank_u[:, 0:FE], ALU.mult))
                    hidden[u] = h

                def hidden_in(u):
                    M.wait(pe, f"hh{u}")
                    bank = banks.take(pe, f"hhT{u}")
                    for j, (f0, fn) in enumerate(FJ):
                        i = pe.transpose(bank[0:fn, j * P:(j + 1) * P], hidden[u][:, f0:f0 + fn], ident[:, :])
                    M.mark("pe", f"hh_P{u}", i)
                    buf = hhT.take(dve, f"ed{u}")
                    M.wait(dve, f"hh_P{u}")
                    b3 = bank[:, 0:3 * P].rearrange("p (j c) -> p j c", j=3)
                    dve.tensor_copy(buf[:, 0:2, :], b3[:, 0:2, :])
                    M.mark("dve", f"hhT{u}", dve.tensor_copy(buf[0:FJ[2][1], 2, :], b3[0:FJ[2][1], 2, :]))
                    return buf

                def down_out(u, buf):
                    M.wait(pe, f"hhT{u}")
                    bank = banks.take(pe, f"ys{u}")
                    for j, (f0, fn) in enumerate(FJ):
                        i = pe.matmul(bank, buf[0:fn, j, :], wdn[0:fn, expert[u], j, :], start=j == 0, stop=j == 2)
                    M.mark("pe", f"ed{u}", i)
                    y = ys.take(act, f"ys_st{u}")
                    M.wait(act, f"ed{u}")
                    M.mark("act", f"ys{u}", act.copy(y[:, :], bank))
                    M.wait(sp, f"ys{u}")
                    M.mark(f"d_ys{u}", f"ys_st{u}", sp.dma_start(
                        ys_d.rearrange("(n u p) d -> n u p d", u=UN, p=P)[n, u], y[:, :]), 16)

                b0 = tokens_in(0)
                b1 = tokens_in(1)
                gate_and_up(0, b0)
                gate_and_up(1, b1)
                b2 = tokens_in(2)
                c0 = hidden_in(0)
                gate_and_up(2, b2)
                down_out(0, c0)
                c1 = hidden_in(1)
                down_out(1, c1)
                c2 = hidden_in(2)
                down_out(2, c2)
            M.wait(sp, *[f"ys_st{u}" for u in range(UN)])
        nc.all_engine_barrier()
        with ExitStack() as st:
            ring6 = Ring(M, "bank6", [psum[:, k, :] for k in range(6)])
            outs = Ring(M, "bank_out", [psum[:, k, :] for k in (6, 7)])
            load = {}
            for name, shape in (("w_qkv", [KD, 3 * D]), ("w_out", [KD, D]), ("xq", [KD, D]), ("xkz", [KD, 4 * P]),
                                ("xv", [KD, P]), ("xfc", [KD, D]), ("w_base", [KD, D]), ("low_in", [KD, RW + NR])):
                load[name] = sb(st, "w5_" + name, [P] + shape)
                M.mark("d_w5", "w5_" + name, sp.dma_start(load[name][:, :, :], rows(io[name])), 16)
            low_out = sb(st, "low_out", [RW, D])
            M.mark("d_w5", "w5_low_out", sp.dma_start(low_out[:, :], io["low_out"]), 16)
            bias = sb(st, "bias", [P, 3, D])
            rbias = sb(st, "rbias", [P, NR])
            for n, name in enumerate(("b_out", "b_fc", "b_base")):
                M.mark("d_w5", "w5_" + name, sp.dma_start(bias[:, n, :], io[name].broadcast_to([P, D])), 16)
            M.mark("d_w5", "w5_b_router", sp.dma_start(rbias[:, :], io["b_router"].broadcast_to([P, NR])), 16)
            rank6 = sb(st, "rank6", [P, NR])
            M.mark("d_w5", "w5_rank6", sp.dma_start(rank6[:, :], io["rank6"]), 16)

            idx5 = sb(st, "idx5", [P, 2, TT], U32)
            wy = sb(st, "wy", [P, 2, TT])
            yg = sb(st, "yg", [P, 2, TT, D])
            xa = sb(st, "xa", [P, TT, D])
            xb = sb(st, "xb", [P, TT, D])
            xn5 = sb(st, "xn5", [P, TT, D])
            xT5 = sb(st, "xT5", [P, KD, S])
            cT5 = sb(st, "cT5", [P, KD, S])
            qT5 = sb(st, "qT5", [P, KD, S])
            kT5 = sb(st, "kT5", [P, KD, S])
            v5 = sb(st, "v5", [P, TT, D])
            vz = sb(st, "vz", [P, TT, GX, 3 * DX])
            oT5 = sb(st, "oT5", [P, KD, S])
            prob = Ring(M, "prob", [sb(st, f"prob{k}", [P, TT, S]) for k in range(4)])
            probT = Ring(M, "probT", [sb(st, f"probT{k}", [P, TT, S]) for k in range(3)])
            stat = Ring(M, "stat", [sb(st, f"stat{k}", [P, 7, TT * TT]) for k in range(5)])
            low = sb(st, "low", [P, TT, RW + NR])
            lowT = sb(st, "lowT", [RW, S])
            g_, ge, gk, gm = (sb(st, "g" + n, [P, TT, NR]) for n in "gekm")
            gr = sb(st, "gr", [P, 4, TT])
            M.mark("dve", "vz0", dve.memset(vz[:, :, :, :], 0.0))
            M.wait(pe, "w5_rank6")
            M.wait(pool, "w5_rank6")
            M.wait(dve, "w5_rank6")
            M.wait(act, "vz0")

            def project(tag, b_of, src_ready, lhs, rhs, n, release, free=None):
                M.wait(pe, *src_ready)
                bank = ring6.take(pe, release)
                for k in range(KD):
                    i = pe.matmul(bank[:, 0:n], lhs(k), rhs(k), start=k == 0, stop=k == KD - 1)
                M.mark("pe", tag, i)
                return bank

            def turn5(tag, src, ready, dst, free):
                for t in range(TT):
                    M.wait(pe, ready(t))
                    bank = ring6.take(pe, f"{tag}_T{t}")
                    for k in range(KD):
                        i = pe.transpose(bank[:, k * P:(k + 1) * P], src[:, t, k * P:(k + 1) * P], ident[:, :])
                    M.mark("pe", f"{tag}_P{t}", i)
                    M.wait(act, f"{tag}_P{t}")
                    M.wait(act, free[0], ago=free[1])
                    M.mark("act", f"{tag}_T{t}", act.copy(dst[:, :, t * P:(t + 1) * P],
                                                         bank.rearrange("p (k c) -> p k c", k=KD)))

            def attend(tag, heads, ready, oT_free, blocked, skew=2):
                buf, opened = {}, {}
                n_heads = len(heads)
                per = n_heads // KD

                def scores(h):
                    q, k, _, _, _, _ = heads[h]
                    M.wait(pe, *ready)
                    bank = ring6.take(pe, f"{tag}e{h}")
                    for t in range(TT):
                        i = pe.matmul(bank[:, t * S:(t + 1) * S], q(t), k, start=True, stop=True)
                    M.mark("pe", f"{tag}s{h}", i)
                    if blocked:
                        block_softmax(h, bank)
                    else:
                        row_softmax(h, bank)

                def row_softmax(h, bank):
                    s3 = stat.take(dve, f"{tag}n{h}")
                    M.wait(dve, f"{tag}s{h}")
                    M.mark("dve", f"{tag}m{h}", dve.tensor_reduce(
                        s3[:, 0, 0:TT], bank.rearrange("p (t k) -> p t k", t=TT), AX, ALU.max, negate=True))
                    p = buf[h] = prob.take(act, f"{tag}pt{h}")
                    M.wait(act, f"{tag}m{h}")
                    for t in range(TT):
                        i = act.activation(p[:, t, :], bank[:, t * S:(t + 1) * S], ACT.Exp,
                                           bias=s3[:, 0, t:t + 1], accum_out=s3[:, 1, t:t + 1])
                    M.mark("act", f"{tag}e{h}", i)
                    M.wait(dve, f"{tag}e{h}")
                    M.mark("dve", f"{tag}r{h}", dve.reciprocal(s3[:, 2, 0:TT], s3[:, 1, 0:TT]))
                    M.wait(dve, f"{tag}r{h}")
                    for t in range(TT):
                        i = dve.tensor_scalar(p[:, t, :], p[:, t, :], s3[:, 2, t:t + 1], None, ALU.mult)
                    M.mark("dve", f"{tag}n{h}", i)

                def block_softmax(h, bank):
                    s3 = stat.take(dve, f"{tag}n{h}")
                    pairs = lambda n: s3[:, n, :].rearrange("p (t j) -> p t j", j=TT)
                    over_j = lambda n: bc(s3[:, n, 0:TT], [P, TT, TT], 2)
                    M.wait(dve, f"{tag}s{h}")
                    M.mark("dve", f"{tag}m{h}", dve.tensor_reduce(
                        s3[:, 0, :], bank.rearrange("p (t k) -> p t k", k=P), AX, ALU.max, negate=True))
                    M.wait(dve, f"{tag}m{h}")
                    M.mark("dve", f"{tag}ma{h}", dve.tensor_reduce(s3[:, 1, 0:TT], pairs(0), AX, ALU.min))
                    M.wait(dve, f"{tag}ma{h}")
                    M.mark("dve", f"{tag}mb{h}", dve.tensor_tensor(pairs(2), over_j(1), pairs(0), ALU.subtract))
                    p = buf[h] = prob.take(act, f"{tag}pt{h}")
                    M.wait(act, f"{tag}m{h}")
                    for n in range(TT * TT):
                        t, j = n // TT, n % TT
                        act.activation(p[:, t, j * P:(j + 1) * P], bank[:, n * P:(n + 1) * P], ACT.Exp,
                                       bias=s3[:, 0, n:n + 1], accum_out=s3[:, 4, n:n + 1])
                    M.wait(act, f"{tag}mb{h}")
                    M.mark("act", f"{tag}e{h}", act.activation(s3[:, 3, :], s3[:, 2, :], ACT.Exp))
                    M.wait(dve, f"{tag}e{h}")
                    M.mark("dve", f"{tag}ra{h}", dve.tensor_tensor(s3[:, 5, :], s3[:, 3, :], s3[:, 4, :], ALU.mult))
                    M.wait(dve, f"{tag}ra{h}")
                    M.mark("dve", f"{tag}rb{h}", dve.tensor_reduce(s3[:, 6, 0:TT], pairs(5), AX, ALU.add))
                    M.wait(dve, f"{tag}rb{h}")
                    M.mark("dve", f"{tag}rc{h}", dve.reciprocal(s3[:, 1, 0:TT], s3[:, 6, 0:TT]))
                    M.wait(dve, f"{tag}rc{h}")
                    M.mark("dve", f"{tag}rd{h}", dve.tensor_tensor(pairs(2), pairs(5), over_j(1), ALU.mult))
                    M.wait(dve, f"{tag}rd{h}")
                    for n in range(TT * TT):
                        t, j = n // TT, n % TT
                        i = dve.tensor_scalar(p[:, t, j * P:(j + 1) * P], p[:, t, j * P:(j + 1) * P],
                                              s3[:, 2, n:n + 1], None, ALU.mult)
                    M.mark("dve", f"{tag}n{h}", i)

                def flip(h):
                    M.wait(pe, f"{tag}n{h}")
                    bank = ring6.take(pe, f"{tag}pT{h}")
                    for kt in range(TT):
                        for t in range(TT):
                            i = pe.transpose(bank[:, kt * S + t * P:kt * S + (t + 1) * P],
                                             buf[h][:, t, kt * P:(kt + 1) * P], ident[:, :])
                    M.mark("pe", f"{tag}pt{h}", i)
                    e, key = (act, "act") if h % 4 else (dve, "dve")
                    b = buf[h] = probT.take(e, f"{tag}pv{h}")
                    M.wait(e, f"{tag}pt{h}")
                    copy = e.copy if e is act else e.tensor_copy
                    M.mark(key, f"{tag}pT{h}", copy(b[:, :, :], bank.rearrange("p (t k) -> p t k", t=TT)))

                def values(h):
                    _, _, v, quad, opens, closes = heads[h]
                    m = h // per
                    if h % per == 0:
                        opened[m] = outs.take(pe, f"{tag}o{m}")
                    M.wait(pe, f"{tag}pT{h}")
                    for kt in range(TT):
                        i = pe.matmul(opened[m][quad:quad + DA, 0:S], v(kt), buf[h][:, kt, :],
                                      start=opens and kt == 0, stop=closes and kt == TT - 1, skip_group_check=True)
                    M.mark("pe", f"{tag}pv{h}", i)
                    if h % per == per - 1:
                        M.wait(act, f"{tag}pv{h}")
                        M.wait(act, oT_free[0], ago=oT_free[1])
                        M.mark("act", f"{tag}o{m}", act.copy(oT5[:, m, :], opened[m][:, 0:S]))

                for n in range(n_heads + skew + 1):
                    if n < n_heads:
                        scores(n)
                    if skew <= n < n_heads + skew:
                        flip(n - skew)
                    if n >= skew + 1:
                        values(n - skew - 1)

            with M.loop(B) as b:
                pick = lambda t: t[:, :, :].rearrange("p c (b t) -> p c b t", t=TT)[:, :, b, :]
                M.wait(dve, "g1_1", ago=1)
                M.mark("dve", "idx5", dve.tensor_copy(idx5[:, :, :], pick(slot_of)))
                M.mark("dve", "wy", dve.tensor_copy(wy[:, :, :], pick(w_of)))
                M.wait(pool, "x3_1", ago=1)
                wait_apart(pool, "idx5")
                for c in range(2):
                    for t in range(TT):
                        M.mark("g_yg", f"g{c}_{t}", pool.indirect_dma_start(
                            out=yg[:, c, t, :], out_offset=None, in_=ys_d,
                            in_offset=bass.IndirectOffsetOnAxis(ap=idx5[:, c, t:t + 1], axis=0)), 16)
                M.wait(sp, "out_st", ago=1)
                M.mark("d_xa", "xa", sp.dma_start(xa[:, :, :], tokens(x2s_d)[b]), 16)
                M.wait(sp, "xv_1", ago=1)
                M.mark("d_cT5", "cT5", sp.dma_start(cT5[:, :, :], ctxT_d[b]), 16)
                M.wait(dve, "xa", "g1_1", "wy")
                for c in range(2):
                    for t in range(TT):
                        M.mark("dve", f"x3_{t}" if c else f"x3a_{t}", dve.scalar_tensor_tensor(
                            xa[:, t, :], yg[:, c, t, :], wy[:, c, t:t + 1], xa[:, t, :], ALU.mult, ALU.add))
                    M.wait(dve, f"x3_{TT - 1}" if c else f"x3a_{TT - 1}")

                layer_norm("ln4", xa, xn5)
                turn5("x4", xn5, lambda t: f"ln4_n{t}", xT5, ("ffn1", 1))
                for t in range(TT):
                    M.wait(pool, f"ln4_n{t}")
                    M.wait(pool, "out_st", ago=1)
                    M.mark("pool", f"xb4_{t}", pool.tensor_tensor(xb[:, t, :], xa[:, t, :], bias[:, 0, :], ALU.add))
                w = load["w_qkv"]
                for m in range(KD):
                    for n, dst in ((0, qT5), (1, kT5)):
                        bank = project(f"P{n}_{m}", None, ["x4_T1"], lambda k: w[:, k, n * D + m * P:n * D + (m + 1) * P],
                                       lambda k: xT5[:, k, :], S, f"q{n}_{m}")
                        M.wait(act, f"P{n}_{m}")
                        M.wait(act, f"X{'pv' if n else 's'}{HX - 1}", ago=1)
                        M.mark("act", f"q{n}_{m}", act.activation(dst[:, m, :], bank[:, 0:S], ACT.Copy,
                                                                 scale=1.0 if n else float(DA) ** -0.5))
                for t in range(TT):
                    bank = project(f"Pv_{t}", None, ["x4_T1"], lambda k: xT5[:, k, t * P:(t + 1) * P],
                                   lambda k: w[:, k, 2 * D:3 * D], D, f"v5_{t}")
                    M.wait(dve, f"Pv_{t}")
                    M.wait(dve, f"Apv{HA - 1}", ago=1)
                    M.mark("dve", f"v5_{t}", dve.tensor_copy(v5[:, t, :], bank))

                def head4(h):
                    m, r = h // HG, slice(DA * (h % HG), DA * (h % HG) + DA)
                    return (lambda t: qT5[r, m, t * P:(t + 1) * P], kT5[r, m, :],
                            lambda kt: v5[:, kt, h * DA:(h + 1) * DA], DA * (h % HG), True, True)
                attend("A", [head4(h) for h in range(HA)], [f"q1_{KD - 1}", "v5_0", "v5_1"], ("Xout1", 1), True)
                for t in range(TT):
                    bank = project(f"Aout{t}", None, [f"Ao{KD - 1}"], lambda k: oT5[:, k, t * P:(t + 1) * P],
                                   lambda k: load["w_out"][:, k, :], D, f"x4r_{t}")
                    M.wait(dve, f"Aout{t}", f"xb4_{t}")
                    M.mark("dve", f"x4r_{t}", dve.tensor_tensor(xa[:, t, :], bank, xb[:, t, :], ALU.add))
                M.wait(dve, "x4r_1")

                M.wait(dve, "x4_P1")
                layer_norm("ln5", xa, xn5)
                turn5("x5", xn5, lambda t: f"ln5_n{t}", xT5, ("Pv_1", 0))
                for t in range(TT):
                    M.wait(pool, f"ln5_n{t}")
                    M.mark("pool", f"xb5_{t}", pool.tensor_tensor(xb[:, t, :], xa[:, t, :], bias[:, 1, :], ALU.add))
                for m in range(KD):
                    bank = project(f"Pxk_{m}", None, ["cT5"], lambda k: load["xkz"][:, k, m * P:(m + 1) * P],
                                   lambda k: cT5[:, k, :], S, f"xk_{m}")
                    M.wait(act, f"Pxk_{m}", f"As{HA - 1}")
                    M.mark("act", f"xk_{m}", act.copy(kT5[:, m, :], bank[:, 0:S]))
                for t in range(TT):
                    bank = project(f"xv_{t}", None, ["cT5"], lambda k: cT5[:, k, t * P:(t + 1) * P],
                                   lambda k: load["xv"][:, k, :], P, f"vz_{t}")
                    M.wait(act, f"xv_{t}")
                    M.wait(act, f"Xpv{HX - 1}", ago=1)
                    M.mark("act", f"vz_{t}", act.copy(vz[:, t, :, DX:2 * DX],
                                                     bank[:, 0:P].rearrange("p (g d) -> p g d", g=GX)))
                for m in range(KD):
                    bank = project(f"Pxq_{m}", None, ["x5_T1"], lambda k: load["xq"][:, k, m * P:(m + 1) * P],
                                   lambda k: xT5[:, k, :], S, f"xq_{m}")
                    M.wait(act, f"Pxq_{m}")
                    M.mark("act", f"xq_{m}", act.activation(qT5[:, m, :], bank[:, 0:S], ACT.Copy, scale=float(DX) ** -0.5))

                def head5(h):
                    m, i, a = h // 8, h // 2 % 4, h % 2
                    half = m // 2
                    r = slice(DA * i, DA * i + DA)
                    g = 4 * half + i
                    return (lambda t: qT5[r, m, t * P:(t + 1) * P], kT5[r, 2 * half + a, :],
                            lambda kt: vz[:, kt, g, DX * (1 - a):DX * (3 - a)], DA * i, a == 0, a == 1)
                attend("X", [head5(h) for h in range(HX)], [f"xq_{KD - 1}", "xk_3", "vz_1"], ("Aout1", 0), False)
                for t in range(TT):
                    bank = project(f"Xout{t}", None, [f"Xo{KD - 1}"], lambda k: oT5[:, k, t * P:(t + 1) * P],
                                   lambda k: load["xfc"][:, k, :], D, f"x5r_{t}")
                    M.wait(dve, f"Xout{t}", f"xb5_{t}")
                    M.mark("dve", f"x5r_{t}", dve.tensor_tensor(xa[:, t, :], bank, xb[:, t, :], ALU.add))
                M.wait(dve, "x5r_1")

                M.wait(dve, "x5_P1")
                layer_norm("ln6", xa, xn5)
                turn5("x6", xn5, lambda t: f"ln6_n{t}", xT5, (f"Pxq_{KD - 1}", 0))
                for t in range(TT):
                    M.wait(pool, f"ln6_n{t}")
                    M.mark("pool", f"xb6_{t}", pool.tensor_tensor(xb[:, t, :], xa[:, t, :], bias[:, 2, :], ALU.add))
                for t in range(TT):
                    bank = project(f"Plow_{t}", None, ["x6_T1"], lambda k: xT5[:, k, t * P:(t + 1) * P],
                                   lambda k: load["low_in"][:, k, :], RW + NR, f"low_{t}")
                    M.wait(act, f"Plow_{t}")
                    M.wait(act, "low_P1", ago=1)
                    M.mark("act", f"low_{t}", act.copy(low[:, t, :], bank[:, 0:RW + NR]))
                base = []
                for t in range(TT):
                    bank = ring6.take(pe, f"x6r_{t}")
                    for k in range(KD):
                        pe.matmul(bank, xT5[:, k, t * P:(t + 1) * P], load["w_base"][:, k, :], start=k == 0, stop=False)
                    base.append(bank)
                each = lambda n: bc(gr[:, n, :], [P, TT, NR], 2)

                def V(name, ins):
                    M.mark("dve", name, ins)
                    M.wait(dve, name)

                M.wait(dve, "low_1")
                V("g0", dve.tensor_tensor(g_[:, :, :], low[:, :, RW:], bc(rbias[:, :], [P, TT, NR], 1), ALU.add))
                V("g1", dve.tensor_reduce(gr[:, 0, :], g_[:, :, :], AX, ALU.max))
                V("g2", dve.tensor_tensor(g_[:, :, :], g_[:, :, :], each(0), ALU.subtract))
                M.wait(act, "g2")
                M.mark("act", "gexp", act.activation(ge[:, :, :], g_[:, :, :], ACT.Exp))
                M.wait(dve, "gexp")
                V("g3", dve.tensor_reduce(gr[:, 1, :], ge[:, :, :], AX, ALU.add))
                V("g4", dve.reciprocal(gr[:, 2, :], gr[:, 1, :]))
                V("g5", dve.tensor_tensor(ge[:, :, :], ge[:, :, :], each(2), ALU.mult))
                V("g6", dve.tensor_copy(g_[:, :, :], ge[:, :, :]))
                V("g7", dve.memset(gm[:, :, :], 0.0))
                for c in range(2):
                    V(f"g8{c}", dve.tensor_reduce(gr[:, 0, :], g_[:, :, :], AX, ALU.max))
                    V(f"g9{c}", dve.tensor_tensor(gk[:, :, :], g_[:, :, :], each(0), ALU.is_equal))
                    V(f"ga{c}", dve.tensor_tensor(gk[:, :, :], gk[:, :, :], bc(rank6[:, :], [P, TT, NR], 1), ALU.mult))
                    V(f"gb{c}", dve.tensor_reduce(gr[:, 3, :], gk[:, :, :], AX, ALU.max))
                    V(f"gc{c}", dve.tensor_tensor(gk[:, :, :], gk[:, :, :], each(3), ALU.is_equal))
                    V(f"gd{c}", dve.tensor_tensor(gm[:, :, :], gm[:, :, :], gk[:, :, :], ALU.add))
                    if c == 0:
                        V("ge", dve.scalar_tensor_tensor(g_[:, :, :], gk[:, :, :], -2.0, g_[:, :, :], ALU.mult, ALU.add))
                V("gf", dve.tensor_tensor(gm[:, :, :], gm[:, :, :], ge[:, :, :], ALU.mult))
                lowv = low[:, :, 0:RR * NR].rearrange("p t (e r) -> p t e r", r=RR)
                for t in range(TT):
                    i = dve.tensor_tensor(lowv[:, t, :, :], lowv[:, t, :, :], bc(gm[:, t, :], [P, NR, RR], 2), ALU.mult)
                M.mark("dve", "gated", i)
                M.wait(pe, "gated")
                bank = ring6.take(pe, "lowT")
                for t in range(TT):
                    i = pe.transpose(bank[0:RW, t * P:(t + 1) * P], low[:, t, 0:RW], ident[:, :])
                    M.mark("pe", f"low_P{t}", i)
                M.wait(act, "low_P1")
                M.wait(act, "ffn1", ago=1)
                M.mark("act", "lowT", act.copy(lowT[:, :], bank[0:RW, 0:S]))
                M.wait(pe, "lowT")
                for t in range(TT):
                    M.mark("pe", f"ffn{t}", pe.matmul(base[t], lowT[:, t * P:(t + 1) * P], low_out[:, :], start=False, stop=True))
                    M.wait(dve, f"ffn{t}", f"xb6_{t}")
                    M.mark("dve", f"x6r_{t}", dve.tensor_tensor(xb[:, t, :], base[t], xb[:, t, :], ALU.add))
                M.wait(sp, "x6r_1")
                M.mark("d_out", "out_st", sp.dma_start(tokens(io["out"])[b], xb[:, :, :]), 16)
            M.wait(sp, "out_st")
        M.close()
        return M


def _tables():
    ident = np.eye(P, dtype=np.float32)
    slopes = np.float32(2.0 ** (-2.0 ** (-(np.log2(HA) - 3)))) ** np.arange(1, HA + 1)
    start = 2.0 ** (-2.0 ** (-(np.log2(HA) - 3)))
    slopes = np.array([start * start ** i for i in range(HA)])
    pos = np.arange(S)
    dist = pos[None, :] - np.arange(P)[:, None]
    full = np.where(dist[:, None, :] >= 0, np.exp(-slopes[None, :, None] * np.maximum(dist, 0)[:, None, :]), 0.0)
    dmask = np.concatenate([full, full[:, :, :P]], axis=2).astype(np.float32)
    quarter = DA // 4
    freq = np.concatenate([(1.0 / 1024.0) ** np.linspace(0.0, 1.0, quarter, dtype=np.float32),
                           np.zeros(quarter, np.float32)]).astype(np.float32)
    theta = (pos.astype(np.float32)[:, None] * freq[None, :]).astype(np.float32).astype(np.float64)
    rot = np.stack([np.cos(theta), np.sin(theta), -np.sin(theta)]).astype(np.float32)
    rot = rot.reshape(3, TT, P, DA // 2).transpose(2, 0, 1, 3)
    tri = np.triu(np.ones((P, P), np.float32), 1)
    rconst = np.tile(np.concatenate([NE - np.arange(NE), P * np.arange(NT), np.arange(SLOTS)]).astype(np.float32), (P, 1))
    token_ids = (np.arange(NT)[None, :] * P + np.arange(P)[:, None]).astype(np.uint32)
    return {"ident": ident, "dmask": dmask, "rot": rot, "tri": tri, "rconst": rconst, "token_ids": token_ids}


def kernel(**inputs):
    import concourse.bacc as bacc
    from concourse.bass_utils import run_bass_kernel_spmd as run

    a = {k: np.asarray(v) for k, v in inputs.items()}
    flip = lambda w, axis: np.flip(w.reshape(w.shape[:axis] + (KD, P) + w.shape[axis + 1:]), axis + 1).reshape(w.shape)
    laid = dict(_tables())
    laid.update({
        "x": a["x"],
        "ctx": flip(a["ctx_2048"], 2),
        "wq": a["L0_attn_Wq"], "wk": a["L0_attn_Wk"], "wv": a["L0_attn_Wv"], "wo": a["L0_attn_Wo"],
        "rms_w": a["L0_attn_rms_w"].reshape(KD, P).T,
        "ssm_kernel": a["L0_xattn_ssm_kernel"],
        "skip": a["L0_xattn_D"].reshape(HC, 1),
        "shared_gate_up": np.concatenate([a["L0_ffn_shared_wg"], a["L0_ffn_gate_w"], a["L0_ffn_shared_wu"]]).T,
        "shared_down": a["L0_ffn_shared_wd"].T,
        "exp_gate_up": np.concatenate([a["L0_ffn_exp_wg"], a["L0_ffn_exp_wu"]], axis=1).transpose(0, 2, 1),
        "exp_down": a["L0_ffn_exp_wd"].transpose(0, 2, 1),
    })
    qkv = a["L1_attn_w_qkv"].T
    order = np.arange(D).reshape(2, 4, 2, 2, DX).transpose(0, 2, 1, 3, 4).reshape(D)
    xk = flip(a["L1_xattn_Wk"].T, 0).reshape(D, 2, 4, DX)
    xkz = np.zeros((D, 2, 2, 4, 2, DX), np.float32)
    for v in range(2):
        xkz[:, :, v, :, v, :] = xk
    laid.update({
        "w_qkv": qkv, "w_out": a["L1_attn_w_out"].T, "b_out": a["L1_attn_b_out"].reshape(1, D),
        "xq": a["L1_xattn_Wq"].T[:, order], "xkz": xkz.reshape(D, 4 * P), "xv": flip(a["L1_xattn_Wv"].T, 0),
        "xfc": a["L1_xattn_Wfc"].T[order, :], "b_fc": a["L1_xattn_bfc"].reshape(1, D),
        "w_base": a["L1_ffn_W_base"], "b_base": a["L1_ffn_b_base"].reshape(1, D),
        "low_in": np.concatenate([a["L1_ffn_A_r"].transpose(1, 0, 2).reshape(D, NR * RR), a["L1_ffn_A_s"],
                                  a["L1_ffn_W_router"]], axis=1),
        "low_out": np.concatenate([a["L1_ffn_B_r"].reshape(NR * RR, D), a["L1_ffn_B_s"]]),
        "b_router": a["L1_ffn_b_router"].reshape(1, NR),
        "rank6": np.tile(NR - np.arange(NR, dtype=np.float32), (P, 1)),
    })
    laid = {k: np.ascontiguousarray(v) for k, v in laid.items()}

    def program(known):
        nc = bacc.Bacc("TRN2", target_bir_lowering=False, num_devices=1)
        io = {k: nc.dram_tensor("in_" + k, v.shape, mybir.dt.from_np(v.dtype), kind="ExternalInput").ap()
              for k, v in laid.items()}
        io["out"] = nc.dram_tensor("out_0_dram", (B, S, D), F32, kind="ExternalOutput").ap()
        return nc, build(nc, io, known)

    _, counted = program(None)
    nc, _ = program(counted)
    r = run(nc, [{"in_" + k: v for k, v in laid.items()}], core_ids=[0])
    return r.results[0]["out_0_dram"]
```

```python
from contextlib import ExitStack, contextmanager

import numpy as np
import concourse.bass as bass
from concourse import mybir
from concourse.alu_op_type import AluOpType as ALU

F32 = mybir.dt.float32
U32 = mybir.dt.uint32
I32 = mybir.dt.int32
ACT = mybir.ActivationFunctionType
AX = mybir.AxisListType.X

P = 128
B, S, D = 8, 256, 512
TT = S // P
NT = B * TT
KD = D // P
HA = 16
DA = D // HA
HG = P // DA
HC, DC = 32, 8
NPAIR = DC * (DC + 1) // 2
NE, FE, FS = 8, 352, 704
FJ = [(0, 128), (128, 128), (256, 96)]
SJ = [(j * P, min(P, FS - j * P)) for j in range(-(-FS // P))]
SLOTS = 2 * B * S // P + NE - 1
ROUTE_SCALE = 2.5
HX, DX, GX = 32, 16, 8
NR, RR = 6, 16
RW = RR * (NR + 1)
LN_EPS = 1e-5
PAD = 4096


class Marks:

    def __init__(self, nc, stack, known):
        self.nc, self.stack, self.known = nc, stack, known
        self.sems, self.base, self.here, self.names, self.per = {}, {}, {}, {}, {}
        self.rings = {}
        self.scope, self.turn, self.turns, self.seen = 0, None, 1, {}
        self.prefix = ""

    def sem(self, key):
        if key not in self.sems:
            self.sems[key] = self.stack.enter_context(self.nc.semaphore(key))
        return self.sems[key]

    def start(self):
        for key in (self.known or self).base:
            if self.pad(key):
                self.nc.sync.sem_inc(self.sem(key), self.pad(key))

    @staticmethod
    def pad(key):
        return 0 if key.startswith("g_") else PAD

    def mark(self, key, name, instruction, by=1):
        instruction.then_inc(self.sem(key), by)
        self.here[key] = self.here.get(key, 0) + by
        name = self.prefix + name
        assert name not in self.names, name
        self.names[name] = (key, self.scope, self.here[key])

    def wait(self, eng, *names, ago=0):
        if self.known is None:
            return
        if ago and self.turn is None:
            return
        for name in names:
            name = self.prefix + name
            key, scope, k = self.known.names[name]
            assert ago or name in self.names, name
            base, per, turns = self.known.per[scope][key]
            who = (id(eng), key)
            if scope == self.scope and self.turn is not None:
                now = k - ago * per
                if self.seen.get((who, scope), -10**9) >= now:
                    continue
                self.seen[(who, scope)] = now
                eng.wait_ge(self.sem(key), self.turn * per + (self.pad(key) + base + now))
            else:
                now = base + (turns - 1) * per + k
                if self.seen.get(who, -1) >= now:
                    continue
                if self.turn is None:
                    self.seen[who] = now
                eng.wait_ge(self.sem(key), self.pad(key) + now)

    def close(self):
        self.per[self.scope] = {k: (self.base.get(k, 0), n, self.turns) for k, n in self.here.items()}
        for k, n in self.here.items():
            self.base[k] = self.base.get(k, 0) + n * self.turns
        self.scope, self.here, self.turn, self.turns = self.scope + 1, {}, None, 1

    @contextmanager
    def loop(self, turns):
        self.close()
        self.turns = turns
        with self.nc.Fori(0, turns) as i:
            self.turn = i
            yield i
        self.close()


class Ring:

    def __init__(self, marks, name, buffers):
        self.marks, self.name, self.buffers = marks, name, buffers
        self.scope, self.uses = None, []

    def take(self, eng, released):
        m = self.marks
        if self.scope != m.scope:
            self.scope, self.uses = m.scope, []
            m.rings[(self.name, self.scope)] = self.uses
        n, size = len(self.uses), len(self.buffers)
        self.uses.append(released)
        if n >= size:
            m.wait(eng, self.uses[n - size])
        elif m.turn is not None and m.known is not None:
            before = m.known.rings[(self.name, self.scope)]
            last = [r for k, r in enumerate(before) if k % size == n]
            m.wait(eng, last[-1], ago=1)
        return self.buffers[n % size]


def together(*threads):
    spent = [0.0] * len(threads)
    alive = list(range(len(threads)))
    while alive:
        k = min(alive, key=lambda n: spent[n] / threads[n][1])
        step = next(threads[k][0], None)
        if step is None:
            alive.remove(k)
        else:
            spent[k] += step


def bc(ap, shape, at):
    return ap.unsqueeze(at).broadcast_to(shape)


def build(nc, io, known):
    pe, act, dve, pool, sp = nc.tensor, nc.scalar, nc.vector, nc.gpsimd, nc.sync
    with ExitStack() as whole:
        M = Marks(nc, whole, known)
        sb = lambda st, name, shape, dt=F32: st.enter_context(nc.sbuf_tensor(name, shape, dt))
        dram = lambda name, shape, dt=F32: nc.dram_tensor(name, shape, dt, kind="Internal").ap()
        psum = whole.enter_context(nc.psum_tensor("psum", [P, 8, 512], F32))
        banks = Ring(M, "bank", [psum[:, k, :] for k in range(8)])
        M.start()

        ident = sb(whole, "ident", [P, P])
        ones = sb(whole, "ones", [P, P])
        mhalf = sb(whole, "mhalf", [P, TT])
        ln_st = sb(whole, "ln_st", [P, TT, 6])
        ln_mv = sb(whole, "ln_mv", [P, TT, 2])
        ln_ve = sb(whole, "ln_ve", [P, TT])
        ln_rs = sb(whole, "ln_rs", [P, TT])
        slot_of = sb(whole, "slot_of", [P, 2, NT], U32)
        w_of = sb(whole, "w_of", [P, 2, NT])

        tile_expert = sb(whole, "tile_expert", [P, SLOTS], I32)

        x1_d = dram("x1_d", [B, S, D])
        x2s_d = dram("x2s_d", [B, S, D])
        xn3_d = dram("xn3_d", [B * S, D])
        ctxT_d = dram("ctxT_d", [B, P, KD, S])
        kpad_d = dram("kpad_d", [HC, P + D])
        slot_token_d = dram("slot_token_d", [SLOTS * P, 1], U32)
        ys_d = dram("ys_d", [SLOTS * P, D])

        tokens = lambda ap: ap.rearrange("b (t p) d -> b p t d", p=P)
        rows = lambda ap: ap.rearrange("(k p) n -> p k n", p=P)

        M.mark("d_const", "ident", sp.dma_start(ident[:, :], io["ident"]), 16)
        M.mark("dve", "ones", dve.memset(ones[:, :], 1.0))
        M.mark("dve", "mhalf", dve.memset(mhalf[:, :], -0.5))
        M.wait(pe, "ident", "ones")
        M.wait(pool, "mhalf")
        M.wait(dve, "ones")

        spare = {n: Ring(M, "spare_" + n, [sb(whole, f"spare_{n}{k}", [P, 1]) for k in range(2)]) for n in ("dve", "pool")}

        def wait_apart(eng, name):
            key = "dve" if eng is dve else "pool"
            column = spare[key].take(eng, "apart_" + name)
            M.wait(eng, name)
            M.mark(key, "apart_" + name, eng.tensor_tensor(column[:, :], ones[:, 0:1], ones[:, 0:1], ALU.mult))

        def layer_norm(tag, src, dst):
            for t in range(TT):
                i = dve.bn_stats(ln_st[:, t, :], src[:, t, :])
            M.mark("dve", tag + "_st", i)
            wait_apart(dve, tag + "_st")
            for t in range(TT):
                i = dve.bn_aggr(ln_mv[:, t, :], ln_st[:, t, :])
            M.mark("dve", tag + "_mv", i)
            M.wait(dve, tag + "_mv")
            M.mark("dve", tag + "_ve", dve.tensor_scalar(ln_ve[:, :], ln_mv[:, :, 1], LN_EPS, None, ALU.add))
            M.wait(pool, tag + "_ve")
            M.mark("pool", tag + "_rs", pool.tensor_tensor(ln_rs[:, :], ln_ve[:, :], mhalf[:, :], ALU.pow))
            M.wait(dve, tag + "_rs")
            for t in range(TT):
                M.mark("dve", f"{tag}_n{t}", dve.tensor_scalar(
                    dst[:, t, :], src[:, t, :], ln_mv[:, t, 0:1], ln_rs[:, t:t + 1], ALU.subtract, ALU.mult))

        def turn(tag, src, ready, write):
            for t in range(TT):
                M.wait(pe, ready(t))
                bank = banks.take(pe, f"{tag}_T{t}")
                for k in range(KD):
                    i = pe.transpose(bank[:, k * P:(k + 1) * P], src[:, t, k * P:(k + 1) * P], ident[:, :])
                M.mark("pe", f"{tag}_P{t}", i)
                write(t, bank.rearrange("p (k c) -> p k c", k=KD))

        def route(logits):
            with ExitStack() as st:
                step = [0]

                def done(key, eng, ins):
                    step[0] += 1
                    M.mark(key, f"route{step[0]}", ins)
                    M.wait(eng, f"route{step[0]}")
                    return f"route{step[0]}"

                def V(ins):
                    return done("dve", dve, ins)

                full = lambda name: sb(st, name, [P, NT, NE])
                few = lambda name: sb(st, name, [P, NT])
                score, eq, h1, h2, a2, pre, tot, run, run2 = (full("r_" + n) for n in (
                    "score", "eq", "h1", "h2", "a2", "pre", "tot", "run", "run2"))
                m1, m2, key, den = (few("r_" + n) for n in ("m1", "m2", "key", "den"))
                tri = sb(st, "tri", [P, P])
                rconst = sb(st, "rconst", [P, NE + NT + SLOTS])
                cnt = sb(st, "cnt", [P, NE, NT])
                tiles, first, first2 = (sb(st, "r_" + n, [P, NE]) for n in ("tiles", "first", "first2"))
                et = sb(st, "et", [P, SLOTS, NE])
                etf = sb(st, "etf", [P, SLOTS])
                ids = sb(st, "ids", [P, NT], U32)
                zero = sb(st, "zero", [P, SLOTS], U32)
                at = sb(st, "at", [P, 2 * NT, 1], U32)
                M.mark("d_tri", "tri", sp.dma_start(tri[:, :], io["tri"]), 16)
                M.mark("d_rconst", "rconst", sp.dma_start(rconst[:, :], io["rconst"]), 16)
                M.mark("d_ids", "ids", sp.dma_start(ids[:, :], io["token_ids"]), 16)
                M.mark("dve", "zero", dve.memset(zero[:, :], 0))
                M.wait(sp, "zero")
                M.mark("d_zero", "slots0", sp.dma_start(slot_token_d.rearrange("(p n) o -> p (n o)", p=P), zero[:, :]), 16)
                M.wait(act, "logits")
                M.mark("act", "score", act.activation(score[:, :, :], logits[:, :, :], ACT.Sigmoid))
                M.wait(dve, "score", "rconst")
                rank8 = bc(rconst[:, 0:NE], [P, NT, NE], 1)
                by_e = lambda t: bc(t[:, :], [P, NT, NE], 2)
                for m, hot in ((m1, h1), (m2, h2)):
                    V(dve.tensor_reduce(m[:, :], score[:, :, :], AX, ALU.max))
                    V(dve.tensor_tensor(eq[:, :, :], score[:, :, :], by_e(m), ALU.is_equal))
                    V(dve.tensor_tensor(eq[:, :, :], eq[:, :, :], rank8, ALU.mult))
                    V(dve.tensor_reduce(key[:, :], eq[:, :, :], AX, ALU.max))
                    V(dve.tensor_tensor(hot[:, :, :], eq[:, :, :], by_e(key), ALU.is_equal))
                    if m is m1:
                        V(dve.scalar_tensor_tensor(score[:, :, :], hot[:, :, :], -2.0, score[:, :, :], ALU.mult, ALU.add))
                V(dve.tensor_tensor(den[:, :], m1[:, :], m2[:, :], ALU.add))
                V(dve.tensor_scalar(den[:, :], den[:, :], 1e-20, None, ALU.add))
                V(dve.reciprocal(den[:, :], den[:, :]))
                for c, m in enumerate((m1, m2)):
                    V(dve.scalar_tensor_tensor(w_of[:, c, :], m[:, :], ROUTE_SCALE, den[:, :], ALU.mult, ALU.mult))
                at_a2 = V(dve.tensor_tensor(a2[:, :, :], h1[:, :, :], h2[:, :, :], ALU.add))
                M.wait(pe, at_a2, "tri")
                flat = a2[:, :, :].rearrange("p t e -> p (t e)")
                bank_p, bank_t = banks.take(pe, "r_tot"), banks.take(pe, "r_tot ")
                pe.matmul(bank_p[:, 0:NT * NE], tri[:, :], flat, start=True, stop=True)
                M.mark("pe", "r_counts", pe.matmul(bank_t[:, 0:NT * NE], ones[:, :], flat, start=True, stop=True))
                M.wait(dve, "r_counts")
                dve.tensor_copy(pre[:, :, :].rearrange("p t e -> p (t e)"), bank_p[:, 0:NT * NE])
                dve.tensor_copy(tot[:, :, :].rearrange("p t e -> p (t e)"), bank_t[:, 0:NT * NE])
                V(dve.tensor_copy(run[:, :, :].rearrange("p t e -> p (t e)"), bank_t[:, 0:NT * NE]))
                M.names["r_tot"] = M.names["r_tot "] = M.names[f"route{step[0]}"]
                src, dst, d = run, run2, 1
                while d < NT:
                    dve.tensor_copy(dst[:, 0:d, :], src[:, 0:d, :])
                    V(dve.tensor_tensor(dst[:, d:, :], src[:, d:, :], src[:, 0:NT - d, :], ALU.add))
                    src, dst, d = dst, src, 2 * d
                V(dve.tensor_tensor(cnt[:, :, :], bc(src[:, NT - 1, :], [P, NE, NT], 2),
                                    bc(rconst[:, NE:NE + NT], [P, NE, NT], 1), ALU.is_gt))
                V(dve.tensor_reduce(tiles[:, :], cnt[:, :, :], AX, ALU.add))
                V(dve.tensor_copy(first[:, :], tiles[:, :]))
                fs, fd, d = first, first2, 1
                while d < NE:
                    dve.tensor_copy(fd[:, 0:d], fs[:, 0:d])
                    V(dve.tensor_tensor(fd[:, d:], fs[:, d:], fs[:, 0:NE - d], ALU.add))
                    fs, fd, d = fd, fs, 2 * d
                V(dve.tensor_tensor(fs[:, :], fs[:, :], tiles[:, :], ALU.subtract))
                V(dve.tensor_tensor(et[:, :, :], bc(rconst[:, NE + NT:], [P, SLOTS, NE], 2),
                                    bc(fs[:, :], [P, SLOTS, NE], 1), ALU.is_ge))
                V(dve.tensor_reduce(etf[:, :], et[:, :, :], AX, ALU.add))
                V(dve.tensor_scalar(tile_expert[:, :], etf[:, :], -1.0, None, ALU.add))
                V(dve.tensor_tensor(pre[:, :, :], pre[:, :, :], src[:, :, :], ALU.add))
                V(dve.tensor_tensor(pre[:, :, :], pre[:, :, :], tot[:, :, :], ALU.subtract))
                V(dve.tensor_scalar(fd[:, :], fs[:, :], float(P), None, ALU.mult))
                V(dve.tensor_tensor(pre[:, :, :], pre[:, :, :], bc(fd[:, :], [P, NT, NE], 1), ALU.add))
                for c, hot in enumerate((h1, h2)):
                    V(dve.tensor_tensor(eq[:, :, :], pre[:, :, :], hot[:, :, :], ALU.mult))
                    V(dve.tensor_reduce(key[:, :], eq[:, :, :], AX, ALU.add))
                    V(dve.tensor_copy(slot_of[:, c, :], key[:, :]))
                    last = V(dve.tensor_copy(at[:, c * NT:(c + 1) * NT, 0], key[:, :]))
                M.wait(pool, last, "ids", "slots0")
                for c in range(2):
                    for t in range(NT):
                        i = pool.indirect_dma_start(
                            out=slot_token_d, out_offset=bass.IndirectOffsetOnAxis(ap=at[:, c * NT + t, :], axis=0),
                            in_=ids[:, t:t + 1], in_offset=None)
                        M.mark("g_scatter", f"scatter{c}_{t}", i, 16)
                M.wait(pool, f"scatter1_{NT - 1}")

        with ExitStack() as st12:
            ctxT = sb(st12, "ctxT", [P, KD, B, S])
            q2T = sb(st12, "q2T", [P, KD, B, S])
            with ExitStack() as st:
                w = sb(st, "w", [P, 4, KD, D])
                dmask = sb(st, "dmask", [P, HA, 3 * P])
                rot = sb(st, "rot", [P, 3, TT, DA // 2])
                rmsw = sb(st, "rmsw", [P, KD])
                kpad = sb(st, "kpad", [HC, P + D])
                skip = sb(st, "skip", [HC, 1])
                xin = sb(st, "xin", [P, TT, D])
                cin = sb(st, "cin", [P, TT, D])
                xn = sb(st, "xn", [P, TT, D])
                xnT = sb(st, "xnT", [P, KD, S])
                qk = [sb(st, f"qk{n}", [P, TT, D]) for n in range(2)]
                qkT = [sb(st, f"qkT{n}", [P, KD, S]) for n in range(2)]
                v = sb(st, "v", [P, TT, D])
                tmp = [Ring(M, f"rot{n}", [sb(st, f"rot{n}{k}", [P, D]) for k in range(2)]) for n in range(2)]
                dec = Ring(M, "dec", [sb(st, f"dec{k}", [P, 3 * P]) for k in range(4)])
                oT = sb(st, "oT", [P, KD, S])
                sq = sb(st, "sq", [P, KD, S])
                sq2 = sb(st, "sq2", [P, 2, S])
                ss = sb(st, "ss", [P, TT])
                rr = sb(st, "rr", [P, TT])
                x1 = sb(st, "x1", [P, TT, D])

                M.mark("dve", "kpad0", dve.memset(kpad[:, :], 0.0))
                M.wait(sp, "kpad0")
                M.mark("d_kpad", "kpad_in", sp.dma_start(kpad[:, P:P + D], io["ssm_kernel"]), 16)
                M.mark("d_skip", "skip_in", sp.dma_start(skip[:, :], io["skip"]), 16)
                M.wait(dve, "kpad_in", "skip_in")
                M.mark("dve", "kpad", dve.tensor_tensor(kpad[:, P:P + 1], kpad[:, P:P + 1], skip[:, :], ALU.add))
                M.wait(sp, "kpad")
                M.mark("d_kpadout", "kpad_d", sp.dma_start(kpad_d, kpad[:, :]), 16)

                for n, name in enumerate(("rot", "wq", "wk", "wv", "dmask", "rms_w", "wo")):
                    dst = {"rot": rot[:, :, :, :], "dmask": dmask[:, :, :], "rms_w": rmsw[:, :]}.get(name)
                    if dst is None:
                        j = ("wq", "wk", "wv", "wo").index(name)
                        M.mark("d_" + name, name, sp.dma_start(w[:, j, :, :], rows(io[name])), 16)
                    else:
                        M.mark("d_" + name, name, sp.dma_start(dst, io[name]), 16)
                M.wait(pe, "wq", "wk", "wv", "wo")
                M.wait(dve, "rot", "dmask")
                M.wait(act, "rms_w")

                with M.loop(B) as b:
                    M.wait(sp, "x1_1", ago=1)
                    M.mark("d_x", "x", sp.dma_start(xin[:, :, :], tokens(io["x"])[b]), 16)
                    M.wait(sp, "ctx_P1", ago=1)
                    M.mark("d_c", "ctx", sp.dma_start(cin[:, :, :], tokens(io["ctx"])[b]), 16)

                    def put_ctx(t, bank):
                        M.wait(act, f"ctx_P{t}")
                        M.mark("act", f"ctx_T{t}", act.copy(ctxT[:, :, b, t * P:(t + 1) * P], bank))
                    turn("ctx", cin, lambda t: "ctx", put_ctx)
                    M.wait(sp, "ctx_T1")
                    M.mark("d_ctxT", "ctxT_d", sp.dma_start(ctxT_d[b], ctxT[:, :, b, :]), 16)

                    M.wait(dve, "x")
                    M.wait(dve, "q2_P1", ago=1)
                    layer_norm("ln1", xin, xn)
                    M.wait(act, "v1_done", ago=1)

                    def put_xnT(t, bank):
                        M.wait(act, f"xn_P{t}")
                        M.mark("act", f"xn_T{t}", act.copy(xnT[:, :, t * P:(t + 1) * P], bank))
                    turn("xn", xn, lambda t: f"ln1_n{t}", put_xnT)

                    for t in range(TT):
                        M.wait(pe, f"xn_T{t}")
                        for n, name in enumerate("qkv"):
                            bank = banks.take(pe, f"{name}{t}_out")
                            for k in range(KD):
                                i = pe.matmul(bank, xnT[:, k, t * P:(t + 1) * P], w[:, n, k, :],
                                              start=k == 0, stop=k == KD - 1)
                            M.mark("pe", f"{name}{t}_done", i)
                            if name == "v":
                                M.wait(act, f"v{t}_done")
                                M.wait(act, "av15", ago=1)
                                M.mark("act", f"v{t}_out", act.copy(v[:, t, :], bank))
                                continue
                            tag = f"{name}{t}"
                            ta = tmp[0].take(dve, tag + "_rot")
                            tb = tmp[1].take(dve, tag + "_rot")
                            M.wait(dve, tag + "_done")
                            half = [P, D // (DA // 2), DA // 2]
                            dve.tensor_tensor(ta[:, :].rearrange("p (h d) -> p h d", d=DA // 2),
                                              bank.rearrange("p (h d) -> p h d", d=DA // 2),
                                              bc(rot[:, 0, t, :], half, 1), ALU.mult)
                            b4 = bank.rearrange("p (h e d) -> p h e d", e=2, d=DA // 2)
                            t4 = tb[:, :].rearrange("p (h e d) -> p h e d", e=2, d=DA // 2)
                            quarter = [P, HA, DA // 2]
                            dve.tensor_tensor(t4[:, :, 0, :], b4[:, :, 1, :], bc(rot[:, 1, t, :], quarter, 1), ALU.mult)
                            M.mark("dve", tag + "_out", dve.tensor_tensor(
                                t4[:, :, 1, :], b4[:, :, 0, :], bc(rot[:, 2, t, :], quarter, 1), ALU.mult))
                            M.wait(pool, tag + "_out")
                            M.wait(pool, f"{name}T{t}_P", ago=1)
                            M.mark("pool", tag + "_rot", pool.tensor_tensor(qk[n][:, t, :], ta[:, :], tb[:, :], ALU.add))
                    for t in range(TT):
                        for n, name in enumerate("qk"):
                            M.wait(pe, f"{name}{t}_rot")
                            bank = banks.take(pe, f"{name}T{t}")
                            for k in range(KD):
                                i = pe.transpose(bank[:, k * P:(k + 1) * P], qk[n][:, t, k * P:(k + 1) * P], ident[:, :])
                            M.mark("pe", f"{name}T{t}_P", i)
                            M.wait(act, f"{name}T{t}_P")
                            M.mark("act", f"{name}T{t}", act.copy(
                                qkT[n][:, :, t * P:(t + 1) * P], bank.rearrange("p (k c) -> p k c", k=KD)))
                    qT, kT = qkT

                    decayed, pending = {}, {}

                    def scores(h):
                        m, i0 = h // HG, DA * (h % HG)
                        r = slice(i0, i0 + DA)
                        bank = banks.take(pe, f"dec{h}")
                        M.wait(pe, "qT1", "kT1")
                        pe.matmul(bank[:, 0:S], kT[r, m, 0:P], qT[r, m, :], start=True, stop=True)
                        M.mark("pe", f"s{h}", pe.matmul(bank[:, S:S + P], kT[r, m, P:S], qT[r, m, P:S],
                                                       start=True, stop=True))
                        buf = decayed[h] = dec.take(dve, f"av{h}")
                        M.wait(dve, f"s{h}")
                        M.mark("dve", f"dec{h}", dve.tensor_tensor(buf[:, :], bank[:, 0:3 * P], dmask[:, h, :], ALU.mult))

                    def values(h):
                        m, i0 = h // HG, DA * (h % HG)
                        if h % HG == 0:
                            pending[m] = banks.take(pe, f"sq{m}")
                        out, buf = pending[m], decayed[h]
                        M.wait(pe, f"dec{h}", "v0_out", "v1_out")
                        c = slice(h * DA, (h + 1) * DA)
                        pe.matmul(out[i0:i0 + DA, 0:S], v[:, 0, c], buf[:, 0:S], start=True, stop=False,
                                  skip_group_check=True)
                        M.mark("pe", f"av{h}", pe.matmul(out[i0:i0 + DA, P:S], v[:, 1, c], buf[:, S:S + P],
                                                        start=False, stop=True, skip_group_check=True))
                        if h % HG == HG - 1:
                            M.wait(act, f"av{h}")
                            M.wait(act, "o1_done", ago=1)
                            M.wait(act, "sq2b", ago=1)
                            act.activation(oT[:, m, :], out[:, 0:S], ACT.Copy, scale=rmsw[:, m:m + 1])
                            M.mark("act", f"sq{m}", act.activation(sq[:, m, :], out[:, 0:S], ACT.Square))

                    for h in range(HA + 2):
                        if h < HA:
                            scores(h)
                        if h >= 2:
                            values(h - 2)

                    M.wait(pe, "sq3")
                    projected = []
                    for t in range(TT):
                        bank = banks.take(pe, f"x1_{t}")
                        projected.append(bank)
                        for k in range(KD):
                            i = pe.matmul(bank, oT[:, k, t * P:(t + 1) * P], w[:, 3, k, :], start=k == 0, stop=k == KD - 1)
                        M.mark("pe", f"o{t}_done", i)
                    M.wait(dve, "sq3")
                    M.wait(dve, "ss_done", ago=1)
                    M.mark("dve", "sq2a", dve.tensor_tensor(sq2[:, :, :], sq[:, 0:2, :], sq[:, 2:4, :], ALU.add))
                    M.wait(dve, "sq2a")
                    M.mark("dve", "sq2b", dve.tensor_tensor(sq2[:, 0, :], sq2[:, 0, :], sq2[:, 1, :], ALU.add))
                    M.wait(pe, "sq2b")
                    bank = banks.take(pe, "ss")
                    for t in range(TT):
                        i = pe.matmul(bank[:, t:t + 1], sq2[:, 0, t * P:(t + 1) * P], ones[:, 0:1], start=True, stop=True)
                    M.mark("pe", "ss_done", i)
                    M.wait(dve, "ss_done")
                    M.mark("dve", "ss", dve.tensor_scalar(ss[:, :], bank[:, 0:TT], 1.0 / D, LN_EPS, ALU.mult, ALU.add))
                    M.wait(pool, "ss")
                    M.mark("pool", "rr", pool.tensor_tensor(rr[:, :], ss[:, :], mhalf[:, :], ALU.pow))
                    M.wait(dve, "rr")
                    M.wait(dve, "x1_st", ago=1)
                    for t in range(TT):
                        M.wait(dve, f"o{t}_done")
                        M.mark("dve", f"x1_{t}", dve.scalar_tensor_tensor(
                            x1[:, t, :], projected[t], rr[:, t:t + 1], xin[:, t, :], ALU.mult, ALU.add))
                    M.wait(sp, "x1_1")
                    M.mark("d_x1", "x1_st", sp.dma_start(tokens(x1_d)[b], x1[:, :, :]), 16)

                    M.wait(dve, "x1_1", "xn_P1")
                    layer_norm("ln2", x1, xn)

                    def put_q2(t, bank):
                        M.wait(act, f"q2_P{t}")
                        M.mark("act", f"q2_T{t}", act.copy(q2T[:, :, b, t * P:(t + 1) * P], bank))
                    turn("q2", xn, lambda t: f"ln2_n{t}", put_q2)
            nc.all_engine_barrier()

            with ExitStack() as st:
                toep = [sb(st, f"toep{u}", [P, D]) for u in range(2)]
                kv = [sb(st, f"kv{u}", [P, KD * B, NPAIR]) for u in range(2)]
                z = [sb(st, f"z{u}", [P, KD, B, DC, DC]) for u in range(2)]
                starts = [sum(DC - e for e in range(d)) for d in range(DC)]
                with M.loop(HC // 2) as hh:
                    for u in range(2):
                        M.wait(sp, f"y{u}_done", ago=1)
                        M.mark(f"d_toep{u}", f"toep{u}", sp.dma_start(
                            toep[u][:, :], bass.AP(kpad_d.tensor, (hh * 2 + u) * (P + D) + 1, [[1, P], [1, D]])), 16)
                    for u in range(2):
                        s0 = (hh * 2 + u) * DC
                        flat = ctxT[:, :, :, :].rearrange("p k b s -> p (k b) s")
                        M.wait(pool, f"y{u}_done", ago=1)
                        for d in range(DC):
                            n = DC - d
                            i = pool.tensor_tensor(kv[u][:, :, starts[d]:starts[d] + n],
                                                   flat[:, :, bass.ds(s0, n)], flat[:, :, bass.ds(s0 + d, n)], ALU.mult)
                        M.mark("pool", f"kv{u}", i)
                    for u in range(2):
                        M.wait(pe, f"kv{u}", f"toep{u}")
                        M.wait(pe, f"z{u}", ago=1)
                        for lt in range(KD):
                            for mt in range(lt + 1):
                                i = pe.matmul(psum[:, 4 * u + lt, 0:B * NPAIR], toep[u][:, (lt - mt) * P:(lt - mt + 1) * P],
                                              kv[u][:, mt * B:(mt + 1) * B, :], start=mt == 0, stop=mt == lt)
                        M.mark("pe", f"y{u}_done", i)
                    for u in range(2):
                        s0 = (hh * 2 + u) * DC
                        M.wait(dve, f"y{u}_done")
                        y = psum[:, 4 * u:4 * u + 4, 0:B * NPAIR].rearrange("p l (b n) -> p l b n", b=B)
                        zf = z[u][:, :, :, :, :].rearrange("p l b j i -> p l b (j i)")
                        for d in range(DC):
                            n = DC - d
                            pair = y[:, :, :, starts[d]:starts[d] + n]
                            i = dve.tensor_tensor(zf[:, :, :, d * DC:d * DC + (n - 1) * (DC + 1) + 1:DC + 1], pair,
                                                  q2T[:, :, :, bass.ds(s0, n)], ALU.mult)
                            if d:
                                i = dve.tensor_tensor(zf[:, :, :, d:d + (n - 1) * (DC + 1) + 1:DC + 1], pair,
                                                      q2T[:, :, :, bass.ds(s0 + d, n)], ALU.mult)
                        M.mark("dve", f"z{u}", i)
                        wait_apart(dve, f"z{u}")
                        M.mark("dve", f"acc{u}", dve.tensor_reduce(
                            q2T[:, :, :, bass.ds(s0, DC)].rearrange("p k b s -> p (k b) s"),
                            z[u][:, :, :, :, :].rearrange("p l b j i -> p (l b) j i"), AX, ALU.add))
            nc.all_engine_barrier()

            with ExitStack() as st:
                gate_up = sb(st, "gate_up", [P, KD, 2 * FS + NE])
                down = sb(st, "down", [P, len(SJ), D])
                logits = sb(st, "logits", [P, NT, NE])
                convT = sb(st, "convT", [P, KD, S])
                x1b = sb(st, "x1b", [P, TT, D])
                x2 = sb(st, "x2", [P, TT, D])
                xn3 = sb(st, "xn3", [P, TT, D])
                x3T = sb(st, "x3T", [P, KD, S])
                silu = Ring(M, "silu", [sb(st, f"silu{k}", [P, S]) for k in range(2)])
                hT = sb(st, "hT", [P, len(SJ), S])
                lgT = sb(st, "lgT", [P, S])
                x2s = sb(st, "x2s", [P, TT, D])
                M.mark("d_gu", "gate_up", sp.dma_start(gate_up[:, :, :], rows(io["shared_gate_up"])), 16)
                full = FS // P
                M.mark("d_dn", "down0", sp.dma_start(down[:, 0:full, :], rows(io["shared_down"][0:full * P, :])), 16)
                M.mark("d_dn", "down1", sp.dma_start(down[0:FS - full * P, full, :], io["shared_down"][full * P:FS, :]), 16)
                M.wait(pe, "gate_up", "down1")
                with M.loop(B) as b:
                    M.wait(sp, "x2_1", ago=1)
                    M.mark("d_x1b", "x1b", sp.dma_start(x1b[:, :, :], tokens(x1_d)[b]), 16)
                    M.wait(act, "conv_P1", ago=1)
                    M.mark("act", "convT", act.copy(convT[:, :, :], q2T[:, :, b, :]))
                    M.wait(pe, "convT")
                    M.wait(dve, "x1b")
                    M.wait(dve, "x2s_1", "xn3_st", ago=1)
                    for t in range(TT):
                        bank = banks.take(pe, f"x2_{t}")
                        for k in range(KD):
                            i = pe.transpose(bank[:, k * P:(k + 1) * P], convT[:, k, t * P:(t + 1) * P], ident[:, :])
                        M.mark("pe", f"conv_P{t}", i)
                        M.wait(dve, f"conv_P{t}")
                        M.mark("dve", f"x2_{t}", dve.tensor_tensor(x2[:, t, :], bank, x1b[:, t, :], ALU.add))
                    M.wait(dve, "x2_1")
                    layer_norm("ln3", x2, xn3)
                    M.wait(sp, "ln3_n1")
                    M.mark("d_xn3", "xn3_st", sp.dma_start(
                        xn3_d.rearrange("(b t p) d -> b p t d", t=TT, p=P)[b], xn3[:, :, :]), 16)

                    def put_x3T(t, bank):
                        M.wait(act, f"x3_P{t}")
                        M.wait(act, "up5", ago=1)
                        M.mark("act", f"x3_T{t}", act.copy(x3T[:, :, t * P:(t + 1) * P], bank))
                    turn("x3", xn3, lambda t: f"ln3_n{t}", put_x3T)

                    M.wait(pe, "x3_T1")
                    for j, (f0, fn) in enumerate(SJ):
                        last = j == len(SJ) - 1
                        gn = fn + NE if last else fn
                        bank_g = banks.take(pe, "lgT" if last else f"silu{j}")
                        for k in range(KD):
                            i = pe.matmul(bank_g[0:gn, 0:S], gate_up[:, k, f0:f0 + gn], x3T[:, k, :],
                                          start=k == 0, stop=k == KD - 1)
                        M.mark("pe", f"gate{j}", i)
                        bank_u = banks.take(pe, f"h{j}")
                        for k in range(KD):
                            i = pe.matmul(bank_u[0:fn, 0:S], gate_up[:, k, FS + NE + f0:FS + NE + f0 + fn], x3T[:, k, :],
                                          start=k == 0, stop=k == KD - 1)
                        M.mark("pe", f"up{j}", i)
                        buf = silu.take(act, f"h{j}")
                        M.wait(act, f"gate{j}")
                        M.mark("act", f"silu{j}", act.activation(buf[0:fn, :], bank_g[0:fn, 0:S], ACT.Silu))
                        if last:
                            M.wait(act, "lg_P1", ago=1)
                            M.mark("act", "lgT", act.copy(lgT[fn:gn, :], bank_g[fn:gn, 0:S]))
                        M.wait(dve, f"silu{j}", f"up{j}")
                        M.wait(dve, "dn1", ago=1)
                        M.mark("dve", f"h{j}", dve.tensor_tensor(hT[0:fn, j, :], buf[0:fn, :], bank_u[0:fn, 0:S], ALU.mult))
                    M.wait(pe, "lgT", f"h{len(SJ) - 1}")
                    for t in range(TT):
                        bank = banks.take(pe, f"x2s_{t}")
                        for j, (f0, fn) in enumerate(SJ):
                            i = pe.matmul(bank, hT[0:fn, j, t * P:(t + 1) * P], down[0:fn, j, :],
                                          start=j == 0, stop=j == len(SJ) - 1)
                        M.mark("pe", f"dn{t}", i)
                        M.wait(dve, f"dn{t}")
                        M.wait(dve, "x2s_st", ago=1)
                        M.mark("dve", f"x2s_{t}", dve.tensor_tensor(x2s[:, t, :], bank, x2[:, t, :], ALU.add))
                    bank = banks.take(pe, "logits")
                    f0, f1 = SJ[-1][1], SJ[-1][1] + NE
                    for t in range(TT):
                        i = pe.transpose(bank[:, t * NE:(t + 1) * NE], lgT[f0:f1, t * P:(t + 1) * P], ident[f0:f1, f0:f1])
                        M.mark("pe", f"lg_P{t}", i)
                    M.wait(dve, "lg_P1")
                    M.mark("dve", "logits", dve.tensor_copy(
                        logits[:, :, :].rearrange("p (b t) e -> p b (t e)", t=TT)[:, b, :], bank[:, 0:TT * NE]))
                    M.wait(sp, "x2s_1")
                    M.mark("d_x2s", "x2s_st", sp.dma_start(tokens(x2s_d)[b], x2s[:, :, :]), 16)
                M.wait(sp, "x2s_st", "xn3_st", "ctxT_d")
                route(logits)
            nc.all_engine_barrier()

        with ExitStack() as st:
            UN = 3
            wgu = sb(st, "wgu", [P, NE, KD, 2 * FE])
            wdn = sb(st, "wdn", [P, NE, len(FJ), D])
            idx = [sb(st, f"idx{u}", [P, 1], U32) for u in range(UN)]
            xg = [sb(st, f"xg{u}", [P, D]) for u in range(UN)]
            xgT = Ring(M, "xgT", [sb(st, f"xgT{u}", [P, KD, P]) for u in range(2)])
            sg = Ring(M, "sg", [sb(st, f"sg{u}", [P, FE]) for u in range(2)])
            hh_ = Ring(M, "hh", [sb(st, f"hh{u}", [P, FE]) for u in range(2)])
            hhT = Ring(M, "hhT", [sb(st, f"hhT{u}", [P, len(FJ), P]) for u in range(2)])
            ys = Ring(M, "ys", [sb(st, f"ys{u}", [P, D]) for u in range(2)])
            for e in range(NE):
                M.mark("d_wgu", f"wgu{e}", sp.dma_start(wgu[:, e, :, :], rows(io["exp_gate_up"][e])), 16)
                M.mark("d_wdn", f"wdn{e}a", sp.dma_start(wdn[:, e, 0:2, :], rows(io["exp_down"][e, 0:2 * P, :])), 16)
                M.mark("d_wdn", f"wdn{e}b", sp.dma_start(wdn[0:FE - 2 * P, e, 2, :], io["exp_down"][e, 2 * P:FE, :]), 16)
            M.wait(pe, f"wgu{NE - 1}", f"wdn{NE - 1}b")
            with M.loop(SLOTS // UN) as n:
                for u in range(UN):
                    M.wait(sp, f"xg_P{u}", ago=1)
                    M.mark(f"d_idx{u}", f"idx{u}", sp.dma_start(
                        idx[u][:, :], slot_token_d.rearrange("(n u p) o -> n u p o", u=UN, p=P)[n, u]), 16)
                    M.wait(pool, f"xg_P{u}", ago=1)
                    wait_apart(pool, f"idx{u}")
                    M.mark(f"g_xg{u}", f"xg{u}", pool.indirect_dma_start(
                        out=xg[u][:, :], out_offset=None, in_=xn3_d,
                        in_offset=bass.IndirectOffsetOnAxis(ap=idx[u][:, 0:1], axis=0)), 16)
                hidden, expert = {}, {}

                def tokens_in(u):
                    M.wait(pe, f"xg{u}")
                    bank = banks.take(pe, f"xgT{u}")
                    for k in range(KD):
                        i = pe.transpose(bank[:, k * P:(k + 1) * P], xg[u][:, k * P:(k + 1) * P], ident[:, :])
                    M.mark("pe", f"xg_P{u}", i)
                    buf = xgT.take(act, f"eu{u}")
                    M.wait(act, f"xg_P{u}")
                    M.mark("act", f"xgT{u}", act.copy(buf[:, :, :], bank.rearrange("p (k c) -> p k c", k=KD)))
                    return buf

                def gate_and_up(u, buf):
                    expert[u] = e = pe.value_load(tile_expert[0:1, bass.ds(n * UN + u, 1)], min_val=0, max_val=NE - 1)
                    M.wait(pe, f"xgT{u}")
                    bank_g, bank_u = banks.take(pe, f"sg{u}"), banks.take(pe, f"hh{u}")
                    for k in range(KD):
                        i = pe.matmul(bank_g[:, 0:FE], buf[:, k, :], wgu[:, e, k, 0:FE], start=k == 0, stop=k == KD - 1)
                    M.mark("pe", f"eg{u}", i)
                    for k in range(KD):
                        i = pe.matmul(bank_u[:, 0:FE], buf[:, k, :], wgu[:, e, k, FE:2 * FE], start=k == 0, stop=k == KD - 1)
                    M.mark("pe", f"eu{u}", i)
                    s, h = sg.take(act, f"hh{u}"), hh_.take(dve, f"hh_P{u}")
                    M.wait(act, f"eg{u}")
                    M.mark("act", f"sg{u}", act.activation(s[:, :], bank_g[:, 0:FE], ACT.Silu))
                    M.wait(dve, f"sg{u}", f"eu{u}")
                    M.mark("dve", f"hh{u}", dve.tensor_tensor(h[:, :], s[:, :], bank_u[:, 0:FE], ALU.mult))
                    hidden[u] = h

                def hidden_in(u):
                    M.wait(pe, f"hh{u}")
                    bank = banks.take(pe, f"hhT{u}")
                    for j, (f0, fn) in enumerate(FJ):
                        i = pe.transpose(bank[0:fn, j * P:(j + 1) * P], hidden[u][:, f0:f0 + fn], ident[:, :])
                    M.mark("pe", f"hh_P{u}", i)
                    buf = hhT.take(dve, f"ed{u}")
                    M.wait(dve, f"hh_P{u}")
                    b3 = bank[:, 0:3 * P].rearrange("p (j c) -> p j c", j=3)
                    dve.tensor_copy(buf[:, 0:2, :], b3[:, 0:2, :])
                    M.mark("dve", f"hhT{u}", dve.tensor_copy(buf[0:FJ[2][1], 2, :], b3[0:FJ[2][1], 2, :]))
                    return buf

                def down_out(u, buf):
                    M.wait(pe, f"hhT{u}")
                    bank = banks.take(pe, f"ys{u}")
                    for j, (f0, fn) in enumerate(FJ):
                        i = pe.matmul(bank, buf[0:fn, j, :], wdn[0:fn, expert[u], j, :], start=j == 0, stop=j == 2)
                    M.mark("pe", f"ed{u}", i)
                    y = ys.take(act, f"ys_st{u}")
                    M.wait(act, f"ed{u}")
                    M.mark("act", f"ys{u}", act.copy(y[:, :], bank))
                    M.wait(sp, f"ys{u}")
                    M.mark(f"d_ys{u}", f"ys_st{u}", sp.dma_start(
                        ys_d.rearrange("(n u p) d -> n u p d", u=UN, p=P)[n, u], y[:, :]), 16)

                b0 = tokens_in(0)
                b1 = tokens_in(1)
                gate_and_up(0, b0)
                gate_and_up(1, b1)
                b2 = tokens_in(2)
                c0 = hidden_in(0)
                gate_and_up(2, b2)
                down_out(0, c0)
                c1 = hidden_in(1)
                down_out(1, c1)
                c2 = hidden_in(2)
                down_out(2, c2)
            M.wait(sp, *[f"ys_st{u}" for u in range(UN)])
        nc.all_engine_barrier()
        with ExitStack() as st:
            ring6 = Ring(M, "bank6", [psum[:, k, :] for k in range(6)])
            outs = {"A": Ring(M, "bank_A", [psum[:, 6, :]]), "X": Ring(M, "bank_X", [psum[:, 7, :]])}
            load = {}
            for name, shape in (("w_qkv", [KD, 3 * D]), ("w_out", [KD, D]), ("xq", [KD, D]), ("xkz", [KD, 4 * P]),
                                ("xv", [KD, P]), ("xfc", [KD, D]), ("w_base", [KD, D]), ("low_in", [KD, RW + NR])):
                load[name] = sb(st, "w5_" + name, [P] + shape)
                M.mark("d_w5", "w5_" + name, sp.dma_start(load[name][:, :, :], rows(io[name])), 16)
            low_out = sb(st, "low_out", [RW, D])
            M.mark("d_w5", "w5_low_out", sp.dma_start(low_out[:, :], io["low_out"]), 16)
            bias = sb(st, "bias", [P, 3, D])
            rbias = sb(st, "rbias", [P, NR])
            for n, name in enumerate(("b_out", "b_fc", "b_base")):
                M.mark("d_w5", "w5_" + name, sp.dma_start(bias[:, n, :], io[name].broadcast_to([P, D])), 16)
            M.mark("d_w5", "w5_b_router", sp.dma_start(rbias[:, :], io["b_router"].broadcast_to([P, NR])), 16)
            rank6 = sb(st, "rank6", [P, NR])
            M.mark("d_w5", "w5_rank6", sp.dma_start(rank6[:, :], io["rank6"]), 16)

            idx5 = sb(st, "idx5", [P, 2, TT], U32)
            wy = sb(st, "wy", [P, 2, TT])
            yg = sb(st, "yg", [P, 2, TT, D])
            xa1 = sb(st, "xa1", [P, TT, D])
            xb1 = sb(st, "xb1", [P, TT, D])
            xn1 = sb(st, "xn1", [P, TT, D])
            xT1 = sb(st, "xT1", [P, KD, S])
            qT1 = sb(st, "qT1", [P, KD, S])
            kT1 = sb(st, "kT1", [P, KD, S])
            v1 = sb(st, "v1", [P, TT, D])
            oT1 = sb(st, "oT1", [P, KD, S])
            x4 = sb(st, "x4", [P, TT, D])
            xa2 = sb(st, "xa2", [P, TT, D])
            xb2 = sb(st, "xb2", [P, TT, D])
            xn2 = sb(st, "xn2", [P, TT, D])
            xT2 = sb(st, "xT2", [P, KD, S])
            cT5 = sb(st, "cT5", [P, KD, S])
            qT2 = sb(st, "qT2", [P, KD, S])
            kT2 = sb(st, "kT2", [P, KD, S])
            vz = sb(st, "vz", [P, TT, GX, 3 * DX])
            oT2 = sb(st, "oT2", [P, KD, S])
            prob = {g: Ring(M, "prob" + g, [sb(st, f"prob{g}{k}", [P, TT, S]) for k in range(3)]) for g in "AX"}
            probT = {g: Ring(M, "probT" + g, [sb(st, f"probT{g}{k}", [P, TT, S]) for k in range(2)]) for g in "AX"}
            stat = {g: Ring(M, "stat" + g, [sb(st, f"stat{g}{k}", [P, 7, TT * TT]) for k in range(4)]) for g in "AX"}
            ln_of = {g: [sb(st, f"ln{g}_{n}", [P, TT] + e) for n, e in (("st", [6]), ("mv", [2]), ("ve", []), ("rs", []))]
                     for g in "AX"}
            low = sb(st, "low", [P, TT, RW + NR])
            lowT = sb(st, "lowT", [RW, S])
            g_, ge, gk, gm = (sb(st, "g" + n, [P, TT, NR]) for n in "gekm")
            gr = sb(st, "gr", [P, 4, TT])
            M.mark("dve", "vz0", dve.memset(vz[:, :, :, :], 0.0))
            M.wait(pe, "w5_rank6")
            M.wait(pool, "w5_rank6")
            M.wait(dve, "w5_rank6")
            M.wait(act, "vz0")

            def norm(g, tag, src, dst):
                ln_st, ln_mv, ln_ve, ln_rs = ln_of[g]
                for t in range(TT):
                    i = dve.bn_stats(ln_st[:, t, :], src[:, t, :])
                M.mark("dve", tag + "_st", i)
                yield 1000
                wait_apart(dve, tag + "_st")
                for t in range(TT):
                    i = dve.bn_aggr(ln_mv[:, t, :], ln_st[:, t, :])
                M.mark("dve", tag + "_mv", i)
                yield 500
                M.wait(dve, tag + "_mv")
                M.mark("dve", tag + "_ve", dve.tensor_scalar(ln_ve[:, :], ln_mv[:, :, 1], LN_EPS, None, ALU.add))
                M.wait(pool, tag + "_ve")
                M.mark("pool", tag + "_rs", pool.tensor_tensor(ln_rs[:, :], ln_ve[:, :], mhalf[:, :], ALU.pow))
                yield 1500
                M.wait(dve, tag + "_rs")
                for t in range(TT):
                    M.mark("dve", f"{tag}_n{t}", dve.tensor_scalar(
                        dst[:, t, :], src[:, t, :], ln_mv[:, t, 0:1], ln_rs[:, t:t + 1], ALU.subtract, ALU.mult))
                yield 1000

            def project(tag, src_ready, lhs, rhs, n, release):
                M.wait(pe, *src_ready)
                bank = ring6.take(pe, release)
                for k in range(KD):
                    i = pe.matmul(bank[:, 0:n], lhs(k), rhs(k), start=k == 0, stop=k == KD - 1)
                M.mark("pe", tag, i)
                return bank

            def turn5(tag, src, ready, dst, free):
                for t in range(TT):
                    M.wait(pe, ready(t))
                    bank = ring6.take(pe, f"{tag}_T{t}")
                    for k in range(KD):
                        i = pe.transpose(bank[:, k * P:(k + 1) * P], src[:, t, k * P:(k + 1) * P], ident[:, :])
                    M.mark("pe", f"{tag}_P{t}", i)
                    M.wait(act, f"{tag}_P{t}")
                    M.wait(act, free[0], ago=free[1])
                    M.mark("act", f"{tag}_T{t}", act.copy(dst[:, :, t * P:(t + 1) * P],
                                                         bank.rearrange("p (k c) -> p k c", k=KD)))
                    yield 1000

            def attend(g, heads, ready, oT, oT_free, blocked, skew=2):
                buf, opened = {}, {}
                n_heads = len(heads)
                per = n_heads // KD

                def scores(h):
                    q, k, _, _, _, _ = heads[h]
                    M.wait(pe, *ready)
                    bank = ring6.take(pe, f"{g}e{h}")
                    for t in range(TT):
                        i = pe.matmul(bank[:, t * S:(t + 1) * S], q(t), k, start=True, stop=True)
                    M.mark("pe", f"{g}s{h}", i)
                    if blocked:
                        block_softmax(h, bank)
                    else:
                        row_softmax(h, bank)

                def row_softmax(h, bank):
                    s3 = stat[g].take(dve, f"{g}n{h}")
                    M.wait(dve, f"{g}s{h}")
                    M.mark("dve", f"{g}m{h}", dve.tensor_reduce(
                        s3[:, 0, 0:TT], bank.rearrange("p (t k) -> p t k", t=TT), AX, ALU.max, negate=True))
                    p = buf[h] = prob[g].take(act, f"{g}pt{h}")
                    M.wait(act, f"{g}m{h}")
                    for t in range(TT):
                        i = act.activation(p[:, t, :], bank[:, t * S:(t + 1) * S], ACT.Exp,
                                           bias=s3[:, 0, t:t + 1], accum_out=s3[:, 1, t:t + 1])
                    M.mark("act", f"{g}e{h}", i)
                    later.append((h, s3, p))

                def row_scale(h, s3, p):
                    M.wait(dve, f"{g}e{h}")
                    M.mark("dve", f"{g}r{h}", dve.reciprocal(s3[:, 2, 0:TT], s3[:, 1, 0:TT]))
                    M.wait(dve, f"{g}r{h}")
                    for t in range(TT):
                        i = dve.tensor_scalar(p[:, t, :], p[:, t, :], s3[:, 2, t:t + 1], None, ALU.mult)
                    M.mark("dve", f"{g}n{h}", i)

                def block_softmax(h, bank):
                    s3 = stat[g].take(dve, f"{g}n{h}")
                    pairs = lambda n: s3[:, n, :].rearrange("p (t j) -> p t j", j=TT)
                    M.wait(dve, f"{g}s{h}")
                    M.mark("dve", f"{g}m{h}", dve.tensor_reduce(
                        s3[:, 0, :], bank.rearrange("p (t k) -> p t k", k=P), AX, ALU.max, negate=True))
                    M.wait(dve, f"{g}m{h}")
                    M.mark("dve", f"{g}ma{h}", dve.tensor_reduce(s3[:, 1, 0:TT], pairs(0), AX, ALU.min))
                    M.wait(dve, f"{g}ma{h}")
                    M.mark("dve", f"{g}mb{h}", dve.tensor_tensor(
                        pairs(2), bc(s3[:, 1, 0:TT], [P, TT, TT], 2), pairs(0), ALU.subtract))
                    p = buf[h] = prob[g].take(act, f"{g}pt{h}")
                    M.wait(act, f"{g}m{h}")
                    for n in range(TT * TT):
                        t, j = n // TT, n % TT
                        act.activation(p[:, t, j * P:(j + 1) * P], bank[:, n * P:(n + 1) * P], ACT.Exp,
                                       bias=s3[:, 0, n:n + 1], accum_out=s3[:, 4, n:n + 1])
                    M.wait(act, f"{g}mb{h}")
                    M.mark("act", f"{g}e{h}", act.activation(s3[:, 3, :], s3[:, 2, :], ACT.Exp))
                    later.append((h, s3, p))

                def block_scale(h, s3, p):
                    pairs = lambda n: s3[:, n, :].rearrange("p (t j) -> p t j", j=TT)
                    M.wait(dve, f"{g}e{h}")
                    M.mark("dve", f"{g}ra{h}", dve.tensor_tensor(s3[:, 5, :], s3[:, 3, :], s3[:, 4, :], ALU.mult))
                    M.wait(dve, f"{g}ra{h}")
                    M.mark("dve", f"{g}rb{h}", dve.tensor_reduce(s3[:, 6, 0:TT], pairs(5), AX, ALU.add))
                    M.wait(dve, f"{g}rb{h}")
                    M.mark("dve", f"{g}rc{h}", dve.reciprocal(s3[:, 1, 0:TT], s3[:, 6, 0:TT]))
                    M.wait(dve, f"{g}rc{h}")
                    M.mark("dve", f"{g}rd{h}", dve.tensor_tensor(
                        pairs(2), pairs(5), bc(s3[:, 1, 0:TT], [P, TT, TT], 2), ALU.mult))
                    M.wait(dve, f"{g}rd{h}")
                    for n in range(TT * TT):
                        t, j = n // TT, n % TT
                        i = dve.tensor_scalar(p[:, t, j * P:(j + 1) * P], p[:, t, j * P:(j + 1) * P],
                                              s3[:, 2, n:n + 1], None, ALU.mult)
                    M.mark("dve", f"{g}n{h}", i)

                def flip(h):
                    M.wait(pe, f"{g}n{h}")
                    bank = ring6.take(pe, f"{g}pT{h}")
                    for kt in range(TT):
                        for t in range(TT):
                            i = pe.transpose(bank[:, kt * S + t * P:kt * S + (t + 1) * P],
                                             buf[h][:, t, kt * P:(kt + 1) * P], ident[:, :])
                    M.mark("pe", f"{g}pt{h}", i)
                    e, key = (act, "act") if h % 2 else (dve, "dve")
                    b = buf[h] = probT[g].take(e, f"{g}pv{h}")
                    M.wait(e, f"{g}pt{h}")
                    copy = e.copy if e is act else e.tensor_copy
                    M.mark(key, f"{g}pT{h}", copy(b[:, :, :], bank.rearrange("p (t k) -> p t k", t=TT)))

                def values(h):
                    _, _, v, quad, opens, closes = heads[h]
                    m = h // per
                    if h % per == 0:
                        opened[m] = outs[g].take(pe, f"{g}o{m}")
                    M.wait(pe, f"{g}pT{h}")
                    for kt in range(TT):
                        i = pe.matmul(opened[m][quad:quad + DA, 0:S], v(kt), buf[h][:, kt, :],
                                      start=opens and kt == 0, stop=closes and kt == TT - 1, skip_group_check=True)
                    M.mark("pe", f"{g}pv{h}", i)
                    if h % per == per - 1:
                        M.wait(act, f"{g}pv{h}")
                        M.wait(act, oT_free, ago=1)
                        M.mark("act", f"{g}o{m}", act.copy(oT[:, m, :], opened[m][:, 0:S]))

                later = []
                for n in range(n_heads + skew + 1):
                    if later and n >= skew - 1:
                        (block_scale if blocked else row_scale)(*later.pop(0))
                    if n < n_heads:
                        scores(n)
                        yield 854
                    if skew <= n < n_heads + skew:
                        flip(n - skew)
                        yield 854
                    if n >= skew + 1:
                        values(n - skew - 1)
                        yield 854

            def self_attention(b, peeled):
                pick = lambda t: t[:, :, :].rearrange("p c (b t) -> p c b t", t=TT)[:, :, b, :]
                M.wait(dve, "g1_1", ago=1)
                M.mark("dve", "idx5", dve.tensor_copy(idx5[:, :, :], pick(slot_of)))
                M.mark("dve", "wy", dve.tensor_copy(wy[:, :, :], pick(w_of)))
                M.wait(pool, "x3_1", ago=1)
                wait_apart(pool, "idx5")
                for c in range(2):
                    for t in range(TT):
                        M.mark("g_yg", f"g{c}_{t}", pool.indirect_dma_start(
                            out=yg[:, c, t, :], out_offset=None, in_=ys_d,
                            in_offset=bass.IndirectOffsetOnAxis(ap=idx5[:, c, t:t + 1], axis=0)), 16)
                M.wait(sp, "xb4_1", "ln4_n1", ago=1)
                M.mark("d_xa", "xa", sp.dma_start(xa1[:, :, :], tokens(x2s_d)[b]), 16)
                yield 6000
                M.wait(dve, "xa", "g1_1", "wy")
                for c in range(2):
                    for t in range(TT):
                        M.mark("dve", f"x3_{t}" if c else f"x3a_{t}", dve.scalar_tensor_tensor(
                            xa1[:, t, :], yg[:, c, t, :], wy[:, c, t:t + 1], xa1[:, t, :], ALU.mult, ALU.add))
                    yield 1200
                    M.wait(dve, f"x3_{TT - 1}" if c else f"x3a_{TT - 1}")
                M.wait(dve, "x4_P1", ago=1)
                yield from norm("A", "ln4", xa1, xn1)
                yield from turn5("x4", xn1, lambda t: f"ln4_n{t}", xT1, ("Pv_1", 1))
                for t in range(TT):
                    M.wait(pool, f"ln4_n{t}")
                    M.wait(pool, "x4r_1", ago=1)
                    M.mark("pool", f"xb4_{t}", pool.tensor_tensor(xb1[:, t, :], xa1[:, t, :], bias[:, 0, :], ALU.add))
                w = load["w_qkv"]
                for m in range(KD):
                    for n, dst in ((0, qT1), (1, kT1)):
                        bank = project(f"P{n}_{m}", ["x4_T1"], lambda k: w[:, k, n * D + m * P:n * D + (m + 1) * P],
                                       lambda k: xT1[:, k, :], S, f"q{n}_{m}")
                        M.wait(act, f"P{n}_{m}")
                        M.wait(act, f"As{HA - 1}", ago=1)
                        M.mark("act", f"q{n}_{m}", act.activation(dst[:, m, :], bank[:, 0:S], ACT.Copy,
                                                                 scale=1.0 if n else float(DA) ** -0.5))
                        yield 1700
                for t in range(TT):
                    bank = project(f"Pv_{t}", ["x4_T1"], lambda k: xT1[:, k, t * P:(t + 1) * P],
                                   lambda k: w[:, k, 2 * D:3 * D], D, f"v5_{t}")
                    M.wait(dve, f"Pv_{t}")
                    M.wait(dve, f"Apv{HA - 1}", ago=1)
                    M.mark("dve", f"v5_{t}", dve.tensor_copy(v1[:, t, :], bank))
                    yield 3400

                def head4(h):
                    m, r = h // HG, slice(DA * (h % HG), DA * (h % HG) + DA)
                    return (lambda t: qT1[r, m, t * P:(t + 1) * P], kT1[r, m, :],
                            lambda kt: v1[:, kt, h * DA:(h + 1) * DA], DA * (h % HG), True, True)
                yield from attend("A", [head4(h) for h in range(HA)], [f"q1_{KD - 1}", "v5_0", "v5_1"], oT1, "Aout1", True)
                for t in range(TT):
                    bank = project(f"Aout{t}", [f"Ao{KD - 1}"], lambda k: oT1[:, k, t * P:(t + 1) * P],
                                   lambda k: load["w_out"][:, k, :], D, f"x4r_{t}")
                    M.wait(dve, f"Aout{t}", f"xb4_{t}")
                    if not peeled:
                        M.wait(dve, "xb5_1", "ln5_n1")
                    M.mark("dve", f"x4r_{t}", dve.tensor_tensor(x4[:, t, :], bank, xb1[:, t, :], ALU.add))
                    yield 3400

            def cross_attention_and_ffn(b):
                M.wait(sp, "xv_1", f"Pxk_{KD - 1}", ago=1)
                M.mark("d_cT5", "cT5", sp.dma_start(cT5[:, :, :], ctxT_d[b]), 16)
                M.wait(dve, "x4r_1", ago=1)
                M.wait(dve, "x6_P1", ago=1)
                yield from norm("X", "ln5", x4, xn2)
                for t in range(TT):
                    M.wait(pool, "x4r_1", "out_st", ago=1)
                    M.mark("pool", f"xb5_{t}", pool.tensor_tensor(xb2[:, t, :], x4[:, t, :], bias[:, 1, :], ALU.add))
                for m in range(KD):
                    bank = project(f"Pxk_{m}", ["cT5"], lambda k: load["xkz"][:, k, m * P:(m + 1) * P],
                                   lambda k: cT5[:, k, :], S, f"xk_{m}")
                    M.wait(act, f"Pxk_{m}")
                    M.wait(act, f"Xs{HX - 1}", ago=1)
                    M.mark("act", f"xk_{m}", act.copy(kT2[:, m, :], bank[:, 0:S]))
                    yield 1700
                yield from turn5("x5", xn2, lambda t: f"ln5_n{t}", xT2, ("ffn1", 1))
                for t in range(TT):
                    bank = project(f"xv_{t}", ["cT5"], lambda k: cT5[:, k, t * P:(t + 1) * P],
                                   lambda k: load["xv"][:, k, :], P, f"vz_{t}")
                    M.wait(act, f"xv_{t}")
                    M.wait(act, f"Xpv{HX - 1}", ago=1)
                    M.mark("act", f"vz_{t}", act.copy(vz[:, t, :, DX:2 * DX],
                                                     bank[:, 0:P].rearrange("p (g d) -> p g d", g=GX)))
                    yield 1700
                for m in range(KD):
                    bank = project(f"Pxq_{m}", ["x5_T1"], lambda k: load["xq"][:, k, m * P:(m + 1) * P],
                                   lambda k: xT2[:, k, :], S, f"xq_{m}")
                    M.wait(act, f"Pxq_{m}")
                    M.wait(act, f"Xs{HX - 1}", ago=1)
                    M.mark("act", f"xq_{m}", act.activation(qT2[:, m, :], bank[:, 0:S], ACT.Copy, scale=float(DX) ** -0.5))
                    yield 1700

                def head5(h):
                    m, i, a = h // 8, h // 2 % 4, h % 2
                    half = m // 2
                    r = slice(DA * i, DA * i + DA)
                    grp = 4 * half + i
                    return (lambda t: qT2[r, m, t * P:(t + 1) * P], kT2[r, 2 * half + a, :],
                            lambda kt: vz[:, kt, grp, DX * (1 - a):DX * (3 - a)], DA * i, a == 0, a == 1)
                yield from attend("X", [head5(h) for h in range(HX)], [f"xq_{KD - 1}", "xk_3", "vz_1"], oT2, "Xout1", False)
                for t in range(TT):
                    bank = project(f"Xout{t}", [f"Xo{KD - 1}"], lambda k: oT2[:, k, t * P:(t + 1) * P],
                                   lambda k: load["xfc"][:, k, :], D, f"x5r_{t}")
                    M.wait(dve, f"Xout{t}", f"xb5_{t}")
                    M.wait(dve, "xb6_1", ago=1)
                    M.mark("dve", f"x5r_{t}", dve.tensor_tensor(xa2[:, t, :], bank, xb2[:, t, :], ALU.add))
                    yield 3400
                M.wait(dve, "x5r_1")

                M.wait(dve, "x5_P1")
                yield from norm("X", "ln6", xa2, xn2)
                yield from turn5("x6", xn2, lambda t: f"ln6_n{t}", xT2, (f"Pxq_{KD - 1}", 0))
                for t in range(TT):
                    M.wait(pool, "x5r_1")
                    M.mark("pool", f"xb6_{t}", pool.tensor_tensor(xb2[:, t, :], xa2[:, t, :], bias[:, 2, :], ALU.add))
                for t in range(TT):
                    bank = project(f"Plow_{t}", ["x6_T1"], lambda k: xT2[:, k, t * P:(t + 1) * P],
                                   lambda k: load["low_in"][:, k, :], RW + NR, f"low_{t}")
                    M.wait(act, f"Plow_{t}")
                    M.wait(act, "low_P1", ago=1)
                    M.mark("act", f"low_{t}", act.copy(low[:, t, :], bank[:, 0:RW + NR]))
                    yield 1700
                each = lambda n: bc(gr[:, n, :], [P, TT, NR], 2)

                def V(name, ins):
                    M.mark("dve", name, ins)
                    M.wait(dve, name)

                M.wait(dve, "low_1")
                V("g0", dve.tensor_tensor(g_[:, :, :], low[:, :, RW:], bc(rbias[:, :], [P, TT, NR], 1), ALU.add))
                V("g1", dve.tensor_reduce(gr[:, 0, :], g_[:, :, :], AX, ALU.max))
                V("g2", dve.tensor_tensor(g_[:, :, :], g_[:, :, :], each(0), ALU.subtract))
                M.wait(act, "g2")
                M.mark("act", "gexp", act.activation(ge[:, :, :], g_[:, :, :], ACT.Exp))
                yield 1200
                M.wait(dve, "gexp")
                V("g3", dve.tensor_reduce(gr[:, 1, :], ge[:, :, :], AX, ALU.add))
                V("g4", dve.reciprocal(gr[:, 2, :], gr[:, 1, :]))
                V("g5", dve.tensor_tensor(ge[:, :, :], ge[:, :, :], each(2), ALU.mult))
                yield 600
                V("g6", dve.tensor_copy(g_[:, :, :], ge[:, :, :]))
                V("g7", dve.memset(gm[:, :, :], 0.0))
                for c in range(2):
                    V(f"g8{c}", dve.tensor_reduce(gr[:, 0, :], g_[:, :, :], AX, ALU.max))
                    V(f"g9{c}", dve.tensor_tensor(gk[:, :, :], g_[:, :, :], each(0), ALU.is_equal))
                    yield 600
                    V(f"ga{c}", dve.tensor_tensor(gk[:, :, :], gk[:, :, :], bc(rank6[:, :], [P, TT, NR], 1), ALU.mult))
                    V(f"gb{c}", dve.tensor_reduce(gr[:, 3, :], gk[:, :, :], AX, ALU.max))
                    yield 600
                    V(f"gc{c}", dve.tensor_tensor(gk[:, :, :], gk[:, :, :], each(3), ALU.is_equal))
                    V(f"gd{c}", dve.tensor_tensor(gm[:, :, :], gm[:, :, :], gk[:, :, :], ALU.add))
                    if c == 0:
                        V("ge", dve.scalar_tensor_tensor(g_[:, :, :], gk[:, :, :], -2.0, g_[:, :, :], ALU.mult, ALU.add))
                    yield 600
                V("gf", dve.tensor_tensor(gm[:, :, :], gm[:, :, :], ge[:, :, :], ALU.mult))
                lowv = low[:, :, 0:RR * NR].rearrange("p t (e r) -> p t e r", r=RR)
                for t in range(TT):
                    i = dve.tensor_tensor(lowv[:, t, :, :], lowv[:, t, :, :], bc(gm[:, t, :], [P, NR, RR], 2), ALU.mult)
                M.mark("dve", "gated", i)
                yield 1000
                M.wait(pe, "gated")
                bank = ring6.take(pe, "lowT")
                for t in range(TT):
                    i = pe.transpose(bank[0:RW, t * P:(t + 1) * P], low[:, t, 0:RW], ident[:, :])
                    M.mark("pe", f"low_P{t}", i)
                M.wait(act, "low_P1")
                M.wait(act, "ffn1", ago=1)
                M.mark("act", "lowT", act.copy(lowT[:, :], bank[0:RW, 0:S]))
                yield 1000
                for t in range(TT):
                    base = ring6.take(pe, f"x6r_{t}")
                    for k in range(KD):
                        pe.matmul(base, xT2[:, k, t * P:(t + 1) * P], load["w_base"][:, k, :], start=k == 0, stop=False)
                    M.wait(pe, "lowT")
                    M.mark("pe", f"ffn{t}", pe.matmul(base, lowT[:, t * P:(t + 1) * P], low_out[:, :], start=False, stop=True))
                    M.wait(dve, f"ffn{t}", f"xb6_{t}")
                    M.mark("dve", f"x6r_{t}", dve.tensor_tensor(xb2[:, t, :], base, xb2[:, t, :], ALU.add))
                    yield 4200
                M.wait(sp, "x6r_1")
                M.mark("d_out", "out_st", sp.dma_start(tokens(io["out"])[b], xb2[:, :, :]), 16)

            M.prefix = "first_"
            ahead = sum(self_attention(0, True))
            M.prefix = ""
            nc.all_engine_barrier()
            with M.loop(B - 1) as b:
                together((cross_attention_and_ffn(b), 1.6 * ahead), (self_attention(b + 1, False), ahead))
            M.wait(sp, "out_st")
            nc.all_engine_barrier()
            M.prefix = "last_"
            sum(cross_attention_and_ffn(B - 1))
            M.wait(sp, "out_st")
        M.close()
        return M


def _tables():
    ident = np.eye(P, dtype=np.float32)
    start = 2.0 ** (-2.0 ** (-(np.log2(HA) - 3)))
    slopes = np.array([start * start ** i for i in range(HA)])
    pos = np.arange(S)
    dist = pos[None, :] - np.arange(P)[:, None]
    full = np.where(dist[:, None, :] >= 0, np.exp(-slopes[None, :, None] * np.maximum(dist, 0)[:, None, :]), 0.0)
    dmask = np.concatenate([full, full[:, :, :P]], axis=2).astype(np.float32)
    quarter = DA // 4
    freq = np.concatenate([(1.0 / 1024.0) ** np.linspace(0.0, 1.0, quarter, dtype=np.float32),
                           np.zeros(quarter, np.float32)]).astype(np.float32)
    theta = (pos.astype(np.float32)[:, None] * freq[None, :]).astype(np.float32).astype(np.float64)
    rot = np.stack([np.cos(theta), np.sin(theta), -np.sin(theta)]).astype(np.float32)
    rot = rot.reshape(3, TT, P, DA // 2).transpose(2, 0, 1, 3)
    tri = np.triu(np.ones((P, P), np.float32), 1)
    rconst = np.tile(np.concatenate([NE - np.arange(NE), P * np.arange(NT), np.arange(SLOTS)]).astype(np.float32), (P, 1))
    token_ids = (np.arange(NT)[None, :] * P + np.arange(P)[:, None]).astype(np.uint32)
    return {"ident": ident, "dmask": dmask, "rot": rot, "tri": tri, "rconst": rconst, "token_ids": token_ids}


def kernel(**inputs):
    import concourse.bacc as bacc
    from concourse.bass_utils import run_bass_kernel_spmd as run

    a = {k: np.asarray(v) for k, v in inputs.items()}
    flip = lambda w, axis: np.flip(w.reshape(w.shape[:axis] + (KD, P) + w.shape[axis + 1:]), axis + 1).reshape(w.shape)
    laid = dict(_tables())
    laid.update({
        "x": a["x"],
        "ctx": flip(a["ctx_2048"], 2),
        "wq": a["L0_attn_Wq"], "wk": a["L0_attn_Wk"], "wv": a["L0_attn_Wv"], "wo": a["L0_attn_Wo"],
        "rms_w": a["L0_attn_rms_w"].reshape(KD, P).T,
        "ssm_kernel": a["L0_xattn_ssm_kernel"],
        "skip": a["L0_xattn_D"].reshape(HC, 1),
        "shared_gate_up": np.concatenate([a["L0_ffn_shared_wg"], a["L0_ffn_gate_w"], a["L0_ffn_shared_wu"]]).T,
        "shared_down": a["L0_ffn_shared_wd"].T,
        "exp_gate_up": np.concatenate([a["L0_ffn_exp_wg"], a["L0_ffn_exp_wu"]], axis=1).transpose(0, 2, 1),
        "exp_down": a["L0_ffn_exp_wd"].transpose(0, 2, 1),
    })
    qkv = a["L1_attn_w_qkv"].T
    order = np.arange(D).reshape(2, 4, 2, 2, DX).transpose(0, 2, 1, 3, 4).reshape(D)
    xk = flip(a["L1_xattn_Wk"].T, 0).reshape(D, 2, 4, DX)
    xkz = np.zeros((D, 2, 2, 4, 2, DX), np.float32)
    for v in range(2):
        xkz[:, :, v, :, v, :] = xk
    laid.update({
        "w_qkv": qkv, "w_out": a["L1_attn_w_out"].T, "b_out": a["L1_attn_b_out"].reshape(1, D),
        "xq": a["L1_xattn_Wq"].T[:, order], "xkz": xkz.reshape(D, 4 * P), "xv": flip(a["L1_xattn_Wv"].T, 0),
        "xfc": a["L1_xattn_Wfc"].T[order, :], "b_fc": a["L1_xattn_bfc"].reshape(1, D),
        "w_base": a["L1_ffn_W_base"], "b_base": a["L1_ffn_b_base"].reshape(1, D),
        "low_in": np.concatenate([a["L1_ffn_A_r"].transpose(1, 0, 2).reshape(D, NR * RR), a["L1_ffn_A_s"],
                                  a["L1_ffn_W_router"]], axis=1),
        "low_out": np.concatenate([a["L1_ffn_B_r"].reshape(NR * RR, D), a["L1_ffn_B_s"]]),
        "b_router": a["L1_ffn_b_router"].reshape(1, NR),
        "rank6": np.tile(NR - np.arange(NR, dtype=np.float32), (P, 1)),
    })
    laid = {k: np.ascontiguousarray(v) for k, v in laid.items()}

    def program(known):
        nc = bacc.Bacc("TRN2", target_bir_lowering=False, num_devices=1)
        io = {k: nc.dram_tensor("in_" + k, v.shape, mybir.dt.from_np(v.dtype), kind="ExternalInput").ap()
              for k, v in laid.items()}
        io["out"] = nc.dram_tensor("out_0_dram", (B, S, D), F32, kind="ExternalOutput").ap()
        return nc, build(nc, io, known)

    _, counted = program(None)
    nc, _ = program(counted)
    r = run(nc, [{"in_" + k: v for k, v in laid.items()}], core_ids=[0])
    return r.results[0]["out_0_dram"]
```

```python
from contextlib import ExitStack, contextmanager

import numpy as np
import concourse.bass as bass
from concourse import mybir
from concourse.alu_op_type import AluOpType as ALU

F32 = mybir.dt.float32
F32R = mybir.dt.float32r
U32 = mybir.dt.uint32
I32 = mybir.dt.int32
ACT = mybir.ActivationFunctionType
AX = mybir.AxisListType.X

P = 128
B, S, D = 8, 256, 512
TT = S // P
NT = B * TT
KD = D // P
HA = 16
DA = D // HA
HG = P // DA
HC, DC = 32, 8
NPAIR = DC * (DC + 1) // 2
NE, FE, FS = 8, 352, 704
FJ = [(0, 128), (128, 128), (256, 96)]
SJ = [(j * P, min(P, FS - j * P)) for j in range(-(-FS // P))]
SLOTS = 2 * B * S // P + NE - 1
ROUTE_SCALE = 2.5
HX, DX, GX = 32, 16, 8
HPT = P // DX
NR, RR = 6, 16
RW = RR * (NR + 1)
LN_EPS = 1e-5
PAD = 4096


class Marks:

    def __init__(self, nc, stack, known):
        self.nc, self.stack, self.known = nc, stack, known
        self.sems, self.base, self.here, self.names, self.per = {}, {}, {}, {}, {}
        self.rings = {}
        self.scope, self.turn, self.turns, self.seen = 0, None, 1, {}
        self.prefix = ""

    def sem(self, key):
        if key not in self.sems:
            self.sems[key] = self.stack.enter_context(self.nc.semaphore(key))
        return self.sems[key]

    def start(self):
        for key in (self.known or self).base:
            if self.pad(key):
                self.nc.sync.sem_inc(self.sem(key), self.pad(key))

    @staticmethod
    def pad(key):
        return 0 if key.startswith("g_") else PAD

    def mark(self, key, name, instruction, by=1):
        instruction.then_inc(self.sem(key), by)
        self.here[key] = self.here.get(key, 0) + by
        name = self.prefix + name
        assert name not in self.names, name
        self.names[name] = (key, self.scope, self.here[key])

    def wait(self, eng, *names, ago=0):
        if self.known is None:
            return
        if ago and self.turn is None:
            return
        for name in names:
            if self.prefix + name in self.known.names:
                name = self.prefix + name
            key, scope, k = self.known.names[name]
            assert ago or name in self.names, name
            base, per, turns = self.known.per[scope][key]
            who = (id(eng), key)
            if scope == self.scope and self.turn is not None:
                now = k - ago * per
                if self.seen.get((who, scope), -10**9) >= now:
                    continue
                self.seen[(who, scope)] = now
                eng.wait_ge(self.sem(key), self.turn * per + (self.pad(key) + base + now))
            else:
                now = base + (turns - 1) * per + k
                if self.seen.get(who, -1) >= now:
                    continue
                if self.turn is None:
                    self.seen[who] = now
                eng.wait_ge(self.sem(key), self.pad(key) + now)

    def close(self):
        self.per[self.scope] = {k: (self.base.get(k, 0), n, self.turns) for k, n in self.here.items()}
        for k, n in self.here.items():
            self.base[k] = self.base.get(k, 0) + n * self.turns
        self.scope, self.here, self.turn, self.turns = self.scope + 1, {}, None, 1

    @contextmanager
    def loop(self, turns):
        self.close()
        self.turns = turns
        with self.nc.Fori(0, turns) as i:
            self.turn = i
            yield i
        self.close()


class Ring:

    def __init__(self, marks, name, buffers):
        self.marks, self.name, self.buffers = marks, name, buffers
        self.scope, self.uses = None, []

    def take(self, eng, released):
        m = self.marks
        if self.scope != m.scope:
            self.scope, self.uses = m.scope, []
            m.rings[(self.name, self.scope)] = self.uses
        n, size = len(self.uses), len(self.buffers)
        self.uses.append(released)
        if n >= size:
            m.wait(eng, self.uses[n - size])
        elif m.turn is not None and m.known is not None:
            before = m.known.rings[(self.name, self.scope)]
            last = [r for k, r in enumerate(before) if k % size == n]
            m.wait(eng, last[-1], ago=1)
        return self.buffers[n % size]


def together(*threads):
    clock, spent, ready = 0.0, [0.0] * len(threads), [0.0] * len(threads)
    alive = list(range(len(threads)))
    while alive:
        now = [k for k in alive if ready[k] <= clock]
        if not now:
            clock = min(ready[k] for k in alive)
            continue
        k = min(now, key=lambda n: spent[n] / threads[n][1])
        step = next(threads[k][0], None)
        if step is None:
            alive.remove(k)
        else:
            clock += step[0]
            spent[k] += step[0]
            ready[k] = clock + step[1]


def side_by_side(main, side, start):
    clock = ready = 0.0
    for n, step in enumerate(main):
        yield step
        clock += sum(step)
        if n >= start and clock >= ready:
            more = next(side, None)
            if more is not None:
                yield more[0], 0
                clock += more[0]
                ready = clock + more[1]
    yield from side


def alone(thread):
    return sum(step[0] for step in thread)


def bc(ap, shape, at):
    return ap.unsqueeze(at).broadcast_to(shape)


def build(nc, io, known):
    pe, act, dve, pool, sp = nc.tensor, nc.scalar, nc.vector, nc.gpsimd, nc.sync
    with ExitStack() as whole:
        M = Marks(nc, whole, known)
        sb = lambda st, name, shape, dt=F32: st.enter_context(nc.sbuf_tensor(name, shape, dt))
        sb_top = lambda st, name, shape: st.enter_context(nc.sbuf_tensor(name, shape, F32, side="right"))
        dram = lambda name, shape, dt=F32: nc.dram_tensor(name, shape, dt, kind="Internal").ap()
        psum = whole.enter_context(nc.psum_tensor("psum", [P, 8, 512], F32))
        banks = Ring(M, "bank", [psum[:, k, :] for k in range(8)])
        M.start()

        ident = sb(whole, "ident", [P, P])
        ones = sb(whole, "ones", [P, P])
        mhalf = sb(whole, "mhalf", [P, TT])
        minus1 = sb(whole, "minus1", [P, TT])
        ln_st = sb(whole, "ln_st", [P, TT, 6])
        ln_mv = sb(whole, "ln_mv", [P, TT, 2])
        ln_ve = sb(whole, "ln_ve", [P, TT])
        ln_rs = sb(whole, "ln_rs", [P, TT])
        ln_bufs = (ln_st, ln_mv, ln_ve, ln_rs)
        slot_of = sb(whole, "slot_of", [P, 2, NT], U32)
        w_of = sb(whole, "w_of", [P, 2, NT])

        logits = sb(whole, "logits", [P, NT, NE])
        ids = sb(whole, "ids", [P, NT], U32)
        at = sb(whole, "at", [P, 2 * NT, 1], U32)
        tile_expert = sb(whole, "tile_expert", [P, SLOTS], I32)

        x1_d = dram("x1_d", [B, S, D])
        x2s_d = dram("x2s_d", [B, S, D])
        xn3_d = dram("xn3_d", [B * S, D])
        ctxT_d = dram("ctxT_d", [B, P, KD, S])
        kpad_d = dram("kpad_d", [HC, P + D])
        slot_token_d = dram("slot_token_d", [SLOTS * P, 1], U32)
        q_parts_d = dram("q_parts_d", [2, D, S])
        k_parts_d = dram("k_parts_d", [2, P, S])
        ys_d = dram("ys_d", [SLOTS * P, D])

        tokens = lambda ap: ap.rearrange("b (t p) d -> b p t d", p=P)
        rows = lambda ap: ap.rearrange("(k p) n -> p k n", p=P)

        rows3 = lambda ap: ap.rearrange("e (k p) n -> e p k n", p=P)

        M.mark("d_const", "ident", sp.dma_start(ident[:, :], io["ident"]), 16)
        M.mark("dve", "ones", dve.memset(ones[:, :], 1.0))
        dve.memset(minus1[:, :], -1.0)
        M.mark("dve", "mhalf", dve.memset(mhalf[:, :], -0.5))
        M.wait(pe, "ident", "ones")
        M.wait(pool, "mhalf")
        M.wait(dve, "ones")

        spare = {n: Ring(M, "spare_" + n, [sb(whole, f"spare_{n}{k}", [P, 1]) for k in range(2)]) for n in ("dve", "pool")}

        def wait_apart(eng, name, ago=0):
            key = "dve" if eng is dve else "pool"
            column = spare[key].take(eng, "apart_" + name)
            M.wait(eng, name, ago=ago)
            M.mark(key, "apart_" + name, eng.tensor_tensor(column[:, :], ones[:, 0:1], ones[:, 0:1], ALU.mult))

        def norm(bufs, tag, src, dst):
            ln_st, ln_mv, ln_ve, ln_rs = bufs
            for t in range(TT):
                i = dve.bn_stats(ln_st[:, t, :], src[:, t, :])
            M.mark("dve", tag + "_st", i)
            yield 0, 1500
            wait_apart(dve, tag + "_st")
            for t in range(TT):
                i = dve.bn_aggr(ln_mv[:, t, :], ln_st[:, t, :])
            M.mark("dve", tag + "_mv", i)
            yield 0, 600
            M.wait(dve, tag + "_mv")
            M.mark("dve", tag + "_ve", dve.tensor_scalar(ln_ve[:, :], ln_mv[:, :, 1], LN_EPS, None, ALU.add))
            M.wait(pool, tag + "_ve")
            M.mark("pool", tag + "_rs", pool.tensor_tensor(ln_rs[:, :], ln_ve[:, :], mhalf[:, :], ALU.pow))
            yield 0, 1200
            M.wait(dve, tag + "_rs")
            for t in range(TT):
                M.mark("dve", f"{tag}_n{t}", dve.tensor_scalar(
                    dst[:, t, :], src[:, t, :], ln_mv[:, t, 0:1], ln_rs[:, t:t + 1], ALU.subtract, ALU.mult))
            yield 0, 1200

        def route(st, ring, logits):
            step = [0]

            def done(key, eng, ins):
                step[0] += 1
                name = f"route{step[0]}"
                M.mark(key, name, ins)
                M.wait(eng, name)
                return name

            def V(ins):
                return done("dve", dve, ins)

            full = lambda name: sb(st, name, [P, NT, NE])
            few = lambda name: sb(st, name, [P, NT])
            score, eq, h1, h2, a2, pre, tot, run, run2 = (full("r_" + n) for n in (
                "score", "eq", "h1", "h2", "a2", "pre", "tot", "run", "run2"))
            m1, m2, key, den = (few("r_" + n) for n in ("m1", "m2", "key", "den"))
            tri = sb(st, "tri", [P, P])
            rconst = sb(st, "rconst", [P, NE + NT + SLOTS])
            cnt = sb(st, "cnt", [P, NE, NT])
            tiles, first, first2 = (sb(st, "r_" + n, [P, NE]) for n in ("tiles", "first", "first2"))
            et = sb(st, "et", [P, SLOTS, NE])
            etf = sb(st, "etf", [P, SLOTS])
            zero = sb(st, "zero", [P, SLOTS], U32)
            M.mark("d_tri", "tri", sp.dma_start(tri[:, :], io["tri"]), 16)
            M.mark("d_rconst", "rconst", sp.dma_start(rconst[:, :], io["rconst"]), 16)
            M.mark("d_ids", "ids", sp.dma_start(ids[:, :], io["token_ids"]), 16)
            M.mark("dve", "zero", dve.memset(zero[:, :], 0))
            M.wait(sp, "zero")
            M.mark("d_zero", "slots0", sp.dma_start(slot_token_d.rearrange("(p n) o -> p (n o)", p=P), zero[:, :]), 16)
            M.wait(act, "logits")
            M.mark("act", "score", act.activation(score[:, :, :], logits[:, :, :], ACT.Sigmoid))
            M.wait(dve, "score", "rconst")
            rank8 = bc(rconst[:, 0:NE], [P, NT, NE], 1)
            by_e = lambda t: bc(t[:, :], [P, NT, NE], 2)
            for m, hot in ((m1, h1), (m2, h2)):
                V(dve.tensor_reduce(m[:, :], score[:, :, :], AX, ALU.max))
                V(dve.tensor_tensor(eq[:, :, :], score[:, :, :], by_e(m), ALU.is_equal))
                V(dve.tensor_tensor(eq[:, :, :], eq[:, :, :], rank8, ALU.mult))
                V(dve.tensor_reduce(key[:, :], eq[:, :, :], AX, ALU.max))
                V(dve.tensor_tensor(hot[:, :, :], eq[:, :, :], by_e(key), ALU.is_equal))
                if m is m1:
                    V(dve.scalar_tensor_tensor(score[:, :, :], hot[:, :, :], -2.0, score[:, :, :], ALU.mult, ALU.add))
            V(dve.tensor_tensor(den[:, :], m1[:, :], m2[:, :], ALU.add))
            V(dve.tensor_scalar(den[:, :], den[:, :], 1e-20, None, ALU.add))
            V(dve.reciprocal(den[:, :], den[:, :]))
            for c, m in enumerate((m1, m2)):
                V(dve.scalar_tensor_tensor(w_of[:, c, :], m[:, :], ROUTE_SCALE, den[:, :], ALU.mult, ALU.mult))
            at_a2 = V(dve.tensor_tensor(a2[:, :, :], h1[:, :, :], h2[:, :, :], ALU.add))
            M.wait(pe, at_a2, "tri")
            flat = a2[:, :, :].rearrange("p t e -> p (t e)")
            bank_p, bank_t = ring.take(pe, "r_tot"), ring.take(pe, "r_tot ")
            pe.matmul(bank_p[:, 0:NT * NE], tri[:, :], flat, start=True, stop=True)
            M.mark("pe", "r_counts", pe.matmul(bank_t[:, 0:NT * NE], ones[:, :], flat, start=True, stop=True))
            M.wait(dve, "r_counts")
            dve.tensor_copy(pre[:, :, :].rearrange("p t e -> p (t e)"), bank_p[:, 0:NT * NE])
            dve.tensor_copy(tot[:, :, :].rearrange("p t e -> p (t e)"), bank_t[:, 0:NT * NE])
            V(dve.tensor_copy(run[:, :, :].rearrange("p t e -> p (t e)"), bank_t[:, 0:NT * NE]))
            for name in ("r_tot", "r_tot "):
                M.names[M.prefix + name] = M.names[M.prefix + f"route{step[0]}"]
            src, dst, d = run, run2, 1
            while d < NT:
                dve.tensor_copy(dst[:, 0:d, :], src[:, 0:d, :])
                V(dve.tensor_tensor(dst[:, d:, :], src[:, d:, :], src[:, 0:NT - d, :], ALU.add))
                src, dst, d = dst, src, 2 * d
            V(dve.tensor_tensor(cnt[:, :, :], bc(src[:, NT - 1, :], [P, NE, NT], 2),
                                bc(rconst[:, NE:NE + NT], [P, NE, NT], 1), ALU.is_gt))
            V(dve.tensor_reduce(tiles[:, :], cnt[:, :, :], AX, ALU.add))
            V(dve.tensor_copy(first[:, :], tiles[:, :]))
            fs, fd, d = first, first2, 1
            while d < NE:
                dve.tensor_copy(fd[:, 0:d], fs[:, 0:d])
                V(dve.tensor_tensor(fd[:, d:], fs[:, d:], fs[:, 0:NE - d], ALU.add))
                fs, fd, d = fd, fs, 2 * d
            V(dve.tensor_tensor(fs[:, :], fs[:, :], tiles[:, :], ALU.subtract))
            V(dve.tensor_tensor(pre[:, :, :], pre[:, :, :], src[:, :, :], ALU.add))
            V(dve.tensor_tensor(pre[:, :, :], pre[:, :, :], tot[:, :, :], ALU.subtract))
            V(dve.tensor_scalar(fd[:, :], fs[:, :], float(P), None, ALU.mult))
            V(dve.tensor_tensor(pre[:, :, :], pre[:, :, :], bc(fd[:, :], [P, NT, NE], 1), ALU.add))
            for c, hot in enumerate((h1, h2)):
                V(dve.tensor_tensor(eq[:, :, :], pre[:, :, :], hot[:, :, :], ALU.mult))
                V(dve.tensor_reduce(key[:, :], eq[:, :, :], AX, ALU.add))
                V(dve.tensor_copy(slot_of[:, c, :], key[:, :]))
                last = V(dve.tensor_copy(at[:, c * NT:(c + 1) * NT, 0], key[:, :]))
                M.wait(pool, last, "ids", "slots0")
                for t in range(NT):
                    i = pool.indirect_dma_start(
                        out=slot_token_d, out_offset=bass.IndirectOffsetOnAxis(ap=at[:, c * NT + t, :], axis=0),
                        in_=ids[:, t:t + 1], in_offset=None)
                    M.mark("g_scatter", f"scatter{c}_{t}", i, 16)
            V(dve.tensor_tensor(et[:, :, :], bc(rconst[:, NE + NT:], [P, SLOTS, NE], 2),
                                bc(fs[:, :], [P, SLOTS, NE], 1), ALU.is_ge))
            V(dve.tensor_reduce(etf[:, :], et[:, :, :], AX, ALU.add))
            last = V(dve.tensor_scalar(tile_expert[:, :], etf[:, :], -1.0, None, ALU.add))
            M.names[M.prefix + "routed"] = M.names[M.prefix + last]

        of_experts, of_attention = ExitStack(), ExitStack()
        assert B == NE

        with ExitStack() as st12:
            q2T = sb(st12, "q2T", [P, KD, B, S])
            of_ctx = ExitStack()
            ctxT = sb(of_ctx, "ctxT", [P, KD, B, S])
            with ExitStack() as st:
                w = sb(st, "w", [P, 4, KD, D])
                dmask = sb(st, "dmask", [P, HA, 3 * P])
                rot = sb(st, "rot", [P, 3, TT, DA // 2])
                rmsw = sb(st, "rmsw", [P, KD])
                kpad = sb(st, "kpad", [HC, P + D])
                skip = sb(st, "skip", [HC, 1])
                xin = sb(st, "xin", [P, TT, D])
                cin = sb(st, "cin", [P, TT, D])
                xn = sb(st, "xn", [P, TT, D])
                xn2 = sb(st, "xn_2", [P, TT, D])
                xres = sb(st, "xres", [P, TT, D])
                xnT = sb(st, "xnT", [P, KD, S])
                qk = [sb(st, f"qk{n}", [P, TT, D]) for n in range(2)]
                qkT = [sb(st, f"qkT{n}", [P, KD, S]) for n in range(2)]
                v = sb(st, "v", [P, TT, D])
                tmp = [Ring(M, f"rot{n}", [sb(st, f"rot{n}{k}", [P, D]) for k in range(2)]) for n in range(2)]
                dec = Ring(M, "dec", [sb(st, f"dec{k}", [P, 3 * P]) for k in range(4)])
                oT = sb(st, "oT", [P, KD, S])
                sq = sb(st, "sq", [P, KD, S])
                sq2 = sb(st, "sq2", [P, 2, S])
                ss = sb(st, "ss", [P, TT])
                rr = sb(st, "rr", [P, TT])
                x1 = sb(st, "x1", [P, TT, D])

                M.mark("dve", "kpad0", dve.memset(kpad[:, :], 0.0))
                M.wait(sp, "kpad0")
                M.mark("d_kpad", "kpad_in", sp.dma_start(kpad[:, P:P + D], io["ssm_kernel"]), 16)
                M.mark("d_skip", "skip_in", sp.dma_start(skip[:, :], io["skip"]), 16)
                M.wait(dve, "kpad_in", "skip_in")
                M.mark("dve", "kpad", dve.tensor_tensor(kpad[:, P:P + 1], kpad[:, P:P + 1], skip[:, :], ALU.add))
                M.wait(sp, "kpad")
                M.mark("d_kpadout", "kpad_d", sp.dma_start(kpad_d, kpad[:, :]), 16)

                ring1 = {"main": Ring(M, "banks_main", [psum[:, k, :] for k in range(6)]),
                         "side": Ring(M, "banks_side", [psum[:, k, :] for k in (6, 7)])}
                def turned(tag, src, ready, put):
                    for t in range(TT):
                        M.wait(pe, ready(t))
                        bank = ring1["side"].take(pe, f"{tag}_T{t}")
                        for k in range(KD):
                            i = pe.transpose(bank[:, k * P:(k + 1) * P], src[:, t, k * P:(k + 1) * P], ident[:, :])
                        M.mark("pe", f"{tag}_P{t}", i)
                        M.wait(act, f"{tag}_P{t}")
                        put(t, bank.rearrange("p (k c) -> p k c", k=KD))
                        yield 850, 0

                def prepare(b, beside=True):
                    M.wait(sp, "ln1_n1", ago=1)
                    M.mark("d_x", "x", sp.dma_start(xin[:, :, :], tokens(io["x"])[b]), 16)
                    M.wait(sp, "ctx_P1", ago=1)
                    M.mark("d_c", "ctx", sp.dma_start(cin[:, :, :], tokens(io["ctx"])[b]), 16)
                    yield 0, 16000
                    M.wait(dve, "x")
                    M.wait(dve, "xn_P1", ago=1)
                    yield from norm(ln_bufs, "ln1", xin, xn)

                    def put_ctx(t, bank):
                        M.mark("act", f"ctx_T{t}", act.copy(ctxT[:, :, b, t * P:(t + 1) * P], bank))
                    M.wait(act, "ctxT_d", ago=1)
                    yield from turned("ctx", cin, lambda t: "ctx", put_ctx)
                    M.wait(sp, "ctx_T1")
                    M.mark("d_ctxT", "ctxT_d", sp.dma_start(ctxT_d[b], ctxT[:, :, b, :]), 16)

                    def put_xnT(t, bank):
                        if beside:
                            M.wait(act, "v1_done")
                        M.mark("act", f"xn_T{t}", act.copy(xnT[:, :, t * P:(t + 1) * P], bank))
                    yield from turned("xn", xn, lambda t: f"ln1_n{t}", put_xnT)

                def queries(b):
                    M.wait(dve, "x1_1", "q2_P1", ago=1)
                    yield from norm(ln_bufs, "ln2", x1, xn2)

                    def put_q2(t, bank):
                        M.mark("act", f"q2_T{t}", act.copy(q2T[:, :, b, t * P:(t + 1) * P], bank))
                    yield from turned("q2", xn2, lambda t: f"ln2_n{t}", put_q2)

                def linear_attention(b, peeled):
                    M.wait(sp, "x1_1", ago=1)
                    M.mark("d_xres", "xres", sp.dma_start(xres[:, :, :], tokens(io["x"])[b]), 16)
                    M.wait(pe, "xn_T1", ago=1)
                    for t in range(TT):
                        for n, name in enumerate("qkv"):
                            bank = ring1["main"].take(pe, f"{name}{t}_out")
                            if peeled:
                                M.wait(pe, "w" + name)
                                M.wait(dve, "rot")
                            for k in range(KD):
                                i = pe.matmul(bank, xnT[:, k, t * P:(t + 1) * P], w[:, n, k, :],
                                              start=k == 0, stop=k == KD - 1)
                            M.mark("pe", f"{name}{t}_done", i)
                            if name == "v":
                                M.wait(act, f"v{t}_done")
                                if peeled and t == 0:
                                    M.wait(pe, "wo")
                                    M.wait(dve, "dmask")
                                    M.wait(act, "rms_w")
                                M.wait(act, "av15", ago=1)
                                M.mark("act", f"v{t}_out", act.copy(v[:, t, :], bank))
                                yield 3400, 0
                                continue
                            tag = f"{name}{t}"
                            ta = tmp[0].take(dve, tag + "_rot")
                            tb = tmp[1].take(dve, tag + "_rot")
                            M.wait(dve, tag + "_done")
                            half = [P, D // (DA // 2), DA // 2]
                            dve.tensor_tensor(ta[:, :].rearrange("p (h d) -> p h d", d=DA // 2),
                                              bank.rearrange("p (h d) -> p h d", d=DA // 2),
                                              bc(rot[:, 0, t, :], half, 1), ALU.mult)
                            b4 = bank.rearrange("p (h e d) -> p h e d", e=2, d=DA // 2)
                            t4 = tb[:, :].rearrange("p (h e d) -> p h e d", e=2, d=DA // 2)
                            quarter = [P, HA, DA // 2]
                            dve.tensor_tensor(t4[:, :, 0, :], b4[:, :, 1, :], bc(rot[:, 1, t, :], quarter, 1), ALU.mult)
                            M.mark("dve", tag + "_out", dve.tensor_tensor(
                                t4[:, :, 1, :], b4[:, :, 0, :], bc(rot[:, 2, t, :], quarter, 1), ALU.mult))
                            M.wait(pool, tag + "_out")
                            M.wait(pool, f"{name}T{t}_P", ago=1)
                            M.mark("pool", tag + "_rot", pool.tensor_tensor(qk[n][:, t, :], ta[:, :], tb[:, :], ALU.add))
                            yield 3400, 0
                    for t in range(TT):
                        for n, name in enumerate("qk"):
                            M.wait(pe, f"{name}{t}_rot")
                            bank = ring1["main"].take(pe, f"{name}T{t}")
                            for k in range(KD):
                                i = pe.transpose(bank[:, k * P:(k + 1) * P], qk[n][:, t, k * P:(k + 1) * P], ident[:, :])
                            M.mark("pe", f"{name}T{t}_P", i)
                            M.wait(act, f"{name}T{t}_P")
                            M.mark("act", f"{name}T{t}", act.copy(
                                qkT[n][:, :, t * P:(t + 1) * P], bank.rearrange("p (k c) -> p k c", k=KD)))
                            yield 850, 0
                    qT, kT = qkT

                    decayed, pending = {}, {}

                    def scores(h):
                        m, i0 = h // HG, DA * (h % HG)
                        r = slice(i0, i0 + DA)
                        bank = ring1["main"].take(pe, f"dec{h}")
                        M.wait(pe, "qT1", "kT1")
                        pe.matmul(bank[:, 0:S], kT[r, m, 0:P], qT[r, m, :], start=True, stop=True)
                        M.mark("pe", f"s{h}", pe.matmul(bank[:, S:S + P], kT[r, m, P:S], qT[r, m, P:S],
                                                       start=True, stop=True))
                        buf = decayed[h] = dec.take(dve, f"av{h}")
                        M.wait(dve, f"s{h}")
                        M.mark("dve", f"dec{h}", dve.tensor_tensor(buf[:, :], bank[:, 0:3 * P], dmask[:, h, :], ALU.mult))

                    def values(h):
                        m, i0 = h // HG, DA * (h % HG)
                        if h % HG == 0:
                            pending[m] = ring1["main"].take(pe, f"sq{m}")
                        out, buf = pending[m], decayed[h]
                        M.wait(pe, f"dec{h}", "v0_out", "v1_out")
                        c = slice(h * DA, (h + 1) * DA)
                        pe.matmul(out[i0:i0 + DA, 0:S], v[:, 0, c], buf[:, 0:S], start=True, stop=False,
                                  skip_group_check=True)
                        M.mark("pe", f"av{h}", pe.matmul(out[i0:i0 + DA, P:S], v[:, 1, c], buf[:, S:S + P],
                                                        start=False, stop=True, skip_group_check=True))
                        if h % HG == HG - 1:
                            M.wait(act, f"av{h}")
                            M.wait(act, "o1_done", ago=1)
                            M.wait(act, "sq2b", ago=1)
                            act.activation(oT[:, m, :], out[:, 0:S], ACT.Copy, scale=rmsw[:, m:m + 1])
                            M.mark("act", f"sq{m}", act.activation(sq[:, m, :], out[:, 0:S], ACT.Square))

                    for h in range(HA + 2):
                        if h < HA:
                            scores(h)
                            yield 640, 0
                        if h >= 2:
                            values(h - 2)
                            yield 640, 0

                    M.wait(dve, "sq3")
                    M.wait(dve, "ss_done", ago=1)
                    M.mark("dve", "sq2a", dve.tensor_tensor(sq2[:, :, :], sq[:, 0:2, :], sq[:, 2:4, :], ALU.add))
                    M.wait(dve, "sq2a")
                    M.mark("dve", "sq2b", dve.tensor_tensor(sq2[:, 0, :], sq2[:, 0, :], sq2[:, 1, :], ALU.add))
                    M.wait(pe, "sq3")
                    for t in range(TT):
                        bank = ring1["main"].take(pe, f"x1_{t}")
                        for k in range(KD):
                            i = pe.matmul(bank, oT[:, k, t * P:(t + 1) * P], w[:, 3, k, :], start=k == 0, stop=k == KD - 1)
                        M.mark("pe", f"o{t}_done", i)
                        if t == 0:
                            M.wait(pe, "sq2b")
                            bank_s = ring1["main"].take(pe, "ss")
                            for u in range(TT):
                                i = pe.matmul(bank_s[:, u:u + 1], sq2[:, 0, u * P:(u + 1) * P], ones[:, 0:1], start=True, stop=True)
                            M.mark("pe", "ss_done", i)
                            M.wait(dve, "ss_done")
                            M.mark("dve", "ss", dve.tensor_scalar(ss[:, :], bank_s[:, 0:TT], 1.0 / D, LN_EPS, ALU.mult, ALU.add))
                            M.wait(pool, "ss")
                            M.mark("pool", "rr", pool.tensor_tensor(rr[:, :], ss[:, :], mhalf[:, :], ALU.pow))
                            M.wait(dve, "rr", "xres")
                            M.wait(dve, "x1_st", ago=1)
                            if not peeled:
                                M.wait(dve, "ln2_n1")
                        M.wait(dve, f"o{t}_done")
                        M.mark("dve", f"x1_{t}", dve.scalar_tensor_tensor(
                            x1[:, t, :], bank, rr[:, t:t + 1], xres[:, t, :], ALU.mult, ALU.add))
                        yield 3400, 0
                    M.wait(sp, "x1_1")
                    M.mark("d_x1", "x1_st", sp.dma_start(tokens(x1_d)[b], x1[:, :, :]), 16)

                def one_after_another(*threads):
                    for thread in threads:
                        yield from thread

                M.prefix = "zeroth_"
                alone(prepare(0, beside=False))
                M.prefix = ""
                for n, name in enumerate(("rot", "wq", "wk", "wv", "dmask", "rms_w", "wo")):
                    dst = {"rot": rot[:, :, :, :], "dmask": dmask[:, :, :], "rms_w": rmsw[:, :]}.get(name)
                    if dst is None:
                        j = ("wq", "wk", "wv", "wo").index(name)
                        M.mark("d_" + name, name, sp.dma_start(w[:, j, :, :], rows(io[name])), 16)
                    else:
                        M.mark("d_" + name, name, sp.dma_start(dst, io[name]), 16)
                nc.all_engine_barrier()
                M.close()
                M.prefix = "first_"
                together((linear_attention(0, True), 61000), (prepare(1), 6800))
                M.wait(sp, "x1_st", "ctxT_d")
                M.prefix = ""
                nc.all_engine_barrier()
                with M.loop(B - 1) as b:
                    together((linear_attention(b + 1, False), 61000),
                             (one_after_another(queries(b), prepare((b + 2) % B)), 6800))
                M.wait(sp, "x1_st", "ctxT_d")
                nc.all_engine_barrier()
                M.prefix = "last_"
                alone(queries(B - 1))
                M.close()
                M.prefix = ""
            nc.all_engine_barrier()

            with ExitStack() as st:
                toep = [sb(st, f"toep{u}", [P, D]) for u in range(2)]
                kv = [sb(st, f"kv{u}", [P, KD * B, NPAIR]) for u in range(2)]
                z = [sb(st, f"z{u}", [P, KD, B, DC, DC]) for u in range(2)]
                starts = [sum(DC - e for e in range(d)) for d in range(DC)]
                with M.loop(HC // 2) as hh:
                    for u in range(2):
                        M.wait(sp, f"y{u}_done", ago=1)
                        M.mark(f"d_toep{u}", f"toep{u}", sp.dma_start(
                            toep[u][:, :], bass.AP(kpad_d.tensor, (hh * 2 + u) * (P + D) + 1, [[1, P], [1, D]])), 16)
                    for u in range(2):
                        s0 = (hh * 2 + u) * DC
                        flat = ctxT[:, :, :, :].rearrange("p k b s -> p (k b) s")
                        M.wait(pool, f"y{u}_done", ago=1)
                        for d in range(DC):
                            n = DC - d
                            i = pool.tensor_tensor(kv[u][:, :, starts[d]:starts[d] + n],
                                                   flat[:, :, bass.ds(s0, n)], flat[:, :, bass.ds(s0 + d, n)], ALU.mult)
                        M.mark("pool", f"kv{u}", i)
                    for u in range(2):
                        M.wait(pe, f"kv{u}", f"toep{u}")
                        M.wait(pe, f"z{u}", ago=1)
                        for lt in range(KD):
                            for mt in range(lt + 1):
                                i = pe.matmul(psum[:, 4 * u + lt, 0:B * NPAIR], toep[u][:, (lt - mt) * P:(lt - mt + 1) * P],
                                              kv[u][:, mt * B:(mt + 1) * B, :], start=mt == 0, stop=mt == lt)
                        M.mark("pe", f"y{u}_done", i)
                    for u in range(2):
                        s0 = (hh * 2 + u) * DC
                        M.wait(dve, f"y{u}_done")
                        y = psum[:, 4 * u:4 * u + 4, 0:B * NPAIR].rearrange("p l (b n) -> p l b n", b=B)
                        zf = z[u][:, :, :, :, :].rearrange("p l b j i -> p l b (j i)")
                        for d in range(DC):
                            n = DC - d
                            pair = y[:, :, :, starts[d]:starts[d] + n]
                            i = dve.tensor_tensor(zf[:, :, :, d * DC:d * DC + (n - 1) * (DC + 1) + 1:DC + 1], pair,
                                                  q2T[:, :, :, bass.ds(s0, n)], ALU.mult)
                            if d:
                                i = dve.tensor_tensor(zf[:, :, :, d:d + (n - 1) * (DC + 1) + 1:DC + 1], pair,
                                                      q2T[:, :, :, bass.ds(s0 + d, n)], ALU.mult)
                        M.mark("dve", f"z{u}", i)
                        wait_apart(dve, f"z{u}")
                        M.mark("dve", f"acc{u}", dve.tensor_reduce(
                            q2T[:, :, :, bass.ds(s0, DC)].rearrange("p k b s -> p (k b) s"),
                            z[u][:, :, :, :, :].rearrange("p l b j i -> p (l b) j i"), AX, ALU.add))
            of_ctx.close()
            nc.all_engine_barrier()

            wgu = sb_top(of_experts, "wgu", [P, NE, KD, 2 * FE])
            with ExitStack() as st:
                gate_up = sb(st, "gate_up", [P, KD, 2 * FS + NE])
                x2r = sb(st, "x2r", [P, TT, D])
                down = sb(st, "down", [P, len(SJ), D])
                convT = sb(st, "convT", [P, KD, S])
                x1b = sb(st, "x1b", [P, TT, D])
                x2 = sb(st, "x2", [P, TT, D])
                xn3 = sb(st, "xn3", [P, TT, D])
                x3T = sb(st, "x3T", [P, KD, S])
                silu = Ring(M, "silu", [sb(st, f"silu{k}", [P, S]) for k in range(2)])
                hT = sb(st, "hT", [P, len(SJ), S])
                lgT = sb(st, "lgT", [P, S])
                x2s = sb(st, "x2s", [P, TT, D])
                ring3 = {"main": Ring(M, "banks_ffn", [psum[:, k, :] for k in range(5)]),
                         "side": Ring(M, "banks_prep", [psum[:, k, :] for k in (5, 6, 7)])}

                def load_shared():
                    M.mark("d_gu", "gate_up", sp.dma_start(gate_up[:, :, :], rows(io["shared_gate_up"])), 16)
                    full = FS // P
                    M.mark("d_dn", "down0", sp.dma_start(down[:, 0:full, :], rows(io["shared_down"][0:full * P, :])), 16)
                    M.mark("d_dn", "down1", sp.dma_start(down[0:FS - full * P, full, :], io["shared_down"][full * P:FS, :]), 16)

                def prepare3(b, beside=True):
                    M.wait(sp, "x2_1", ago=1)
                    M.mark("d_x1b", "x1b", sp.dma_start(x1b[:, :, :], tokens(x1_d)[b]), 16)
                    if not beside:
                        load_shared()
                    M.wait(act, "conv_P1", ago=1)
                    M.mark("act", "convT", act.copy(convT[:, :, :], q2T[:, :, b, :]))
                    yield 0, 3000
                    M.wait(dve, "x1b")
                    M.wait(pe, "convT")
                    if beside:
                        M.wait(dve, "x2r")
                    for t in range(TT):
                        bank = ring3["side"].take(pe, f"x2_{t}")
                        for k in range(KD):
                            i = pe.transpose(bank[:, k * P:(k + 1) * P], convT[:, k, t * P:(t + 1) * P], ident[:, :])
                        M.mark("pe", f"conv_P{t}", i)
                        M.wait(dve, f"conv_P{t}")
                        M.mark("dve", f"x2_{t}", dve.tensor_tensor(x2[:, t, :], bank, x1b[:, t, :], ALU.add))
                        yield 850, 600 * t
                    M.wait(dve, "x2_1")
                    M.wait(dve, "xn3_st", "x3_P1", ago=1)
                    yield from norm(ln_bufs, "ln3", x2, xn3)
                    M.wait(sp, "ln3_n1")
                    M.mark("d_xn3", "xn3_st", sp.dma_start(
                        xn3_d.rearrange("(b t p) d -> b p t d", t=TT, p=P)[b], xn3[:, :, :]), 16)
                    for t in range(TT):
                        M.wait(pe, f"ln3_n{t}")
                        bank = ring3["side"].take(pe, f"x3_T{t}")
                        for k in range(KD):
                            i = pe.transpose(bank[:, k * P:(k + 1) * P], xn3[:, t, k * P:(k + 1) * P], ident[:, :])
                        M.mark("pe", f"x3_P{t}", i)
                        M.wait(act, f"x3_P{t}")
                        if beside and t == 0:
                            yield 0, 0
                            while M.prefix + f"up{len(SJ) - 1}" not in M.names:
                                yield 0, 2000
                            M.wait(act, f"up{len(SJ) - 1}")
                        M.mark("act", f"x3_T{t}", act.copy(x3T[:, :, t * P:(t + 1) * P], bank.rearrange("p (k c) -> p k c", k=KD)))
                        yield 850, 500 * t
                    M.wait(pe, "x3_T1")
                    if not beside:
                        M.wait(pe, "gate_up", "down1")
                    bank = ring3["side"].take(pe, "lgT")
                    for k in range(KD):
                        i = pe.matmul(bank[0:NE, 0:S], gate_up[:, k, 2 * FS:2 * FS + NE], x3T[:, k, :], start=k == 0, stop=k == KD - 1)
                    M.mark("pe", "lg", i)
                    M.wait(act, "lg")
                    M.wait(act, "lg_P1", ago=1)
                    M.mark("act", "lgT", act.copy(lgT[0:NE, :], bank[0:NE, 0:S]))
                    yield 1700, 500
                    M.wait(pe, "lgT")
                    bank = ring3["side"].take(pe, "logits")
                    for t in range(TT):
                        i = pe.matmul(bank[:, t * NE:(t + 1) * NE], lgT[0:NE, t * P:(t + 1) * P], ident[0:NE, 0:NE],
                                      start=True, stop=True)
                        M.mark("pe", f"lg_P{t}", i)
                    M.wait(dve, "lg_P1")
                    M.mark("dve", "logits", dve.tensor_copy(
                        logits[:, :, :].rearrange("p (b t) e -> p b (t e)", t=TT)[:, b, :], bank[:, 0:TT * NE]))
                    yield 200, 0

                def shared_expert(b):
                    M.mark("d_wgu", "wgu", sp.dma_start(wgu[:, b, :, :], rows3(io["exp_gate_up"])[b]), 16)
                    wait_apart(pool, "x2s_1", ago=1)
                    M.mark("pool", "x2r", pool.tensor_copy(x2r[:, :, :], x2[:, :, :]))
                    M.wait(pe, "x3_T1", ago=1)
                    for j, (f0, fn) in enumerate(SJ):
                        bank_g = ring3["main"].take(pe, f"silu{j}")
                        for k in range(KD):
                            i = pe.matmul(bank_g[0:fn, 0:S], gate_up[:, k, f0:f0 + fn], x3T[:, k, :],
                                          start=k == 0, stop=k == KD - 1)
                        M.mark("pe", f"gate{j}", i)
                        bank_u = ring3["main"].take(pe, f"h{j}")
                        for k in range(KD):
                            i = pe.matmul(bank_u[0:fn, 0:S], gate_up[:, k, FS + f0:FS + f0 + fn], x3T[:, k, :],
                                          start=k == 0, stop=k == KD - 1)
                        M.mark("pe", f"up{j}", i)
                        buf = silu.take(act, f"h{j}")
                        M.wait(act, f"gate{j}")
                        M.mark("act", f"silu{j}", act.activation(buf[0:fn, :], bank_g[0:fn, 0:S], ACT.Silu))
                        M.wait(dve, f"silu{j}", f"up{j}")
                        M.wait(dve, "dn1", ago=1)
                        M.mark("dve", f"h{j}", dve.tensor_tensor(hT[0:fn, j, :], buf[0:fn, :], bank_u[0:fn, 0:S], ALU.mult))
                        yield 3400, 0
                    for t in range(TT):
                        bank = ring3["main"].take(pe, f"x2s_{t}")
                        for j, (f0, fn) in enumerate(SJ):
                            M.wait(pe, f"h{j}")
                            i = pe.matmul(bank, hT[0:fn, j, t * P:(t + 1) * P], down[0:fn, j, :],
                                          start=j == 0, stop=j == len(SJ) - 1)
                        M.mark("pe", f"dn{t}", i)
                        M.wait(dve, f"dn{t}", "x2r")
                        M.wait(dve, "x2s_st", ago=1)
                        M.mark("dve", f"x2s_{t}", dve.tensor_tensor(x2s[:, t, :], bank, x2r[:, t, :], ALU.add))
                        yield 5100, 0
                    M.wait(sp, "x2s_1")
                    M.mark("d_x2s", "x2s_st", sp.dma_start(tokens(x2s_d)[b], x2s[:, :, :]), 16)

                M.prefix = "zeroth_"
                alone(prepare3(0, beside=False))
                M.prefix = ""
                nc.all_engine_barrier()
                with M.loop(B - 1) as b:
                    together((shared_expert(b), 31000), (prepare3(b + 1), 6000))
                M.wait(sp, "x2s_st", "xn3_st")
                nc.all_engine_barrier()
                M.prefix = "last_"
                last_expert = shared_expert(B - 1)
                next(last_expert)
                route(st, ring3["side"], logits)
                alone(last_expert)
                M.wait(sp, "x2s_st", "x2s_1", "routed")
                M.prefix = ""
            st12.close()
            wdn = sb_top(of_experts, "wdn", [P, NE, len(FJ), D])
            load = {}
            for name, shape in (("w_qkv", [KD, 3 * D]), ("w_out", [KD, D])):
                load[name] = of_attention.enter_context(nc.sbuf_tensor("w5_" + name, [P] + shape, F32))

            def load_weights():
                for e in range(NE):
                    M.mark("d_wdn", f"wdn{e}a", sp.dma_start(wdn[:, e, 0:2, :], rows(io["exp_down"][e, 0:2 * P, :])), 16)
                    M.mark("d_wdn", f"wdn{e}b", sp.dma_start(wdn[0:FE - 2 * P, e, 2, :], io["exp_down"][e, 2 * P:FE, :]), 16)
            load_weights()
            M.wait(pool, f"last_scatter1_{NT - 1}")
            nc.all_engine_barrier()

        with ExitStack() as st:
            UN = 3
            idx = [sb(st, f"idx{u}", [P, 1], U32) for u in range(UN)]
            xg = [sb(st, f"xg{u}", [P, D]) for u in range(UN)]
            xgT = [sb(st, f"xgT{u}", [P, KD, P]) for u in range(UN)]
            sg = Ring(M, "sg", [sb(st, f"sg{u}", [P, FE]) for u in range(2)])
            hh_ = Ring(M, "hh", [sb(st, f"hh{u}", [P, FE]) for u in range(2)])
            hhT = Ring(M, "hhT", [sb(st, f"hhT{u}", [P, len(FJ), P]) for u in range(2)])
            ys = Ring(M, "ys", [sb(st, f"ys{u}", [P, D]) for u in range(2)])
            M.wait(pe, "last_wgu")
            turns = SLOTS // UN
            hidden, expert = {}, {}

            def gather(u, n):
                M.mark(f"d_idx{u}", f"idx{u}", sp.dma_start(
                    idx[u][:, :], slot_token_d.rearrange("(n u p) o -> n u p o", u=UN, p=P)[n, u]), 16)
                wait_apart(pool, f"idx{u}")
                M.mark(f"g_xg{u}", f"xg{u}", pool.indirect_dma_start(
                    out=xg[u][:, :], out_offset=None, in_=xn3_d,
                    in_offset=bass.IndirectOffsetOnAxis(ap=idx[u][:, 0:1], axis=0)), 16)

            def tokens_in(u, peeled=False):
                if peeled:
                    M.wait(pe, f"xg{u}")
                else:
                    M.wait(pe, f"xg{u}", ago=1)
                bank = banks.take(pe, f"xgT{u}")
                for k in range(KD):
                    i = pe.transpose(bank[:, k * P:(k + 1) * P], xg[u][:, k * P:(k + 1) * P], ident[:, :])
                M.mark("pe", f"xg_P{u}", i)
                M.wait(act, f"xg_P{u}")
                if not peeled:
                    M.wait(act, f"eu{u}")
                M.mark("act", f"xgT{u}", act.copy(xgT[u][:, :, :], bank.rearrange("p (k c) -> p k c", k=KD)))

            M.prefix = "zeroth_"
            for u in range(UN):
                gather(u, 0)
            for u in range(UN):
                tokens_in(u, peeled=True)
            nc.all_engine_barrier()
            M.close()
            M.prefix = "first_"
            for u in range(UN):
                gather(u, 1)
            M.prefix = ""
            M.wait(sp, f"first_xg{UN - 1}")
            for name, dst in load.items():
                M.mark("d_w4", "w5_" + name, sp.dma_start(dst[:, :, :], rows(io[name])), 16)
            nc.all_engine_barrier()
            with M.loop(turns) as n:
                def gate_and_up(u):
                    expert[u] = e = pe.value_load(tile_expert[0:1, bass.ds(n * UN + u, 1)], min_val=0, max_val=NE - 1)
                    M.wait(pe, f"xgT{u}", ago=1)
                    bank_g, bank_u = banks.take(pe, f"sg{u}"), banks.take(pe, f"hh{u}")
                    for k in range(KD):
                        i = pe.matmul(bank_g[:, 0:FE], xgT[u][:, k, :], wgu[:, e, k, 0:FE], start=k == 0, stop=k == KD - 1)
                    M.mark("pe", f"eg{u}", i)
                    for k in range(KD):
                        i = pe.matmul(bank_u[:, 0:FE], xgT[u][:, k, :], wgu[:, e, k, FE:2 * FE], start=k == 0, stop=k == KD - 1)
                    M.mark("pe", f"eu{u}", i)
                    s, h = sg.take(act, f"hh{u}"), hh_.take(dve, f"hh_P{u}")
                    M.wait(act, f"eg{u}")
                    M.mark("act", f"sg{u}", act.activation(s[:, :], bank_g[:, 0:FE], ACT.Silu))
                    M.wait(dve, f"sg{u}", f"eu{u}")
                    M.mark("dve", f"hh{u}", dve.tensor_tensor(h[:, :], s[:, :], bank_u[:, 0:FE], ALU.mult))
                    hidden[u] = h

                def hidden_in(u):
                    M.wait(pe, f"hh{u}")
                    bank = banks.take(pe, f"hhT{u}")
                    for j, (f0, fn) in enumerate(FJ):
                        i = pe.transpose(bank[0:fn, j * P:(j + 1) * P], hidden[u][:, f0:f0 + fn], ident[:, :])
                    M.mark("pe", f"hh_P{u}", i)
                    buf = hhT.take(dve, f"ed{u}")
                    M.wait(dve, f"hh_P{u}")
                    b3 = bank[:, 0:3 * P].rearrange("p (j c) -> p j c", j=3)
                    dve.tensor_copy(buf[:, 0:2, :], b3[:, 0:2, :])
                    M.mark("dve", f"hhT{u}", dve.tensor_copy(buf[0:FJ[2][1], 2, :], b3[0:FJ[2][1], 2, :]))
                    return buf

                def down_out(u, buf):
                    M.wait(pe, f"hhT{u}", f"wdn{NE - 1}b")
                    bank = banks.take(pe, f"ys{u}")
                    for j, (f0, fn) in enumerate(FJ):
                        i = pe.matmul(bank, buf[0:fn, j, :], wdn[0:fn, expert[u], j, :], start=j == 0, stop=j == 2)
                    M.mark("pe", f"ed{u}", i)
                    y = ys.take(act, f"ys_st{u}")
                    M.wait(act, f"ed{u}")
                    M.mark("act", f"ys{u}", act.copy(y[:, :], bank))
                    M.wait(sp, f"ys{u}")
                    M.mark(f"d_ys{u}", f"ys_st{u}", sp.dma_start(
                        ys_d.rearrange("(n u p) d -> n u p d", u=UN, p=P)[n, u], y[:, :]), 16)

                def next_tokens(u):
                    tokens_in(u)
                    M.wait(sp, f"xg_P{u}")
                    M.wait(pool, f"xg_P{u}")
                    gather(u, (n + 2) % turns)

                gate_and_up(0)
                gate_and_up(1)
                c0 = hidden_in(0)
                gate_and_up(2)
                down_out(0, c0)
                c1 = hidden_in(1)
                next_tokens(0)
                down_out(1, c1)
                c2 = hidden_in(2)
                next_tokens(1)
                next_tokens(2)
                down_out(2, c2)
            M.wait(pool, *[f"xg{u}" for u in range(UN)])
            M.wait(sp, *[f"ys_st{u}" for u in range(UN)])
        of_experts.close()
        nc.all_engine_barrier()
        with of_attention, ExitStack() as st:
            ring = {"A": Ring(M, "banks_A", [psum[:, k, :] for k in (0, 1, 2)]),
                    "X": Ring(M, "banks_X", [psum[:, k, :] for k in (3, 4, 5)])}
            outs = {"A": Ring(M, "bank_A", [psum[:, 6, :]]), "X": Ring(M, "bank_X", [psum[:, 7, :]])}
            for name, shape in (("xq", [KD, D]), ("xk", [KD, P]),
                                ("xv", [KD, P]), ("xfc", [KD, D]), ("w_base", [KD, D]), ("low_in", [KD, RW + NR])):
                load[name] = sb(st, "w5_" + name, [P] + shape)
            low_out = sb(st, "low_out", [RW, D])
            bias = sb(st, "bias", [P, 3, D])
            rbias = sb(st, "rbias", [P, NR])
            lower = sb(st, "lower", [P, NR, NR])

            def load_weights5():
                for n, name in enumerate(("b_out", "b_fc", "b_base")):
                    M.mark("d_bias", "w5_" + name, sp.dma_start(bias[:, n, :], io[name].broadcast_to([P, D])), 16)
                for name in ("xk", "xv", "xq", "xfc", "low_in", "w_base"):
                    M.mark("d_w5", "w5_" + name, sp.dma_start(load[name][:, :, :], rows(io[name])), 16)
                M.mark("d_w5", "w5_low_out", sp.dma_start(low_out[:, :], io["low_out"]), 16)
                M.mark("d_w5", "w5_b_router", sp.dma_start(rbias[:, :], io["b_router"].broadcast_to([P, NR])), 16)
                M.mark("d_w5", "w5_lower", sp.dma_start(lower[:, :, :], io["lower"]), 16)

            idx5 = sb(st, "idx5", [P, 2, TT], U32)
            wy = sb(st, "wy", [P, 2, TT])
            yg = sb(st, "yg", [P, 2, TT, D])
            xa1 = sb(st, "xa1", [P, TT, D])
            xb1 = sb(st, "xb1", [P, TT, D])
            xn1 = sb(st, "xn1", [P, TT, D])
            xT1 = sb(st, "xT1", [P, KD, S])
            qT1 = sb(st, "qT1", [P, KD, S])
            kT1 = sb(st, "kT1", [P, KD, S])
            v1 = sb(st, "v1", [P, TT, D])
            oT1 = sb(st, "oT1", [P, KD, S])
            x4 = sb(st, "x4", [P, TT, D])
            xa2 = sb(st, "xa2", [P, TT, D])
            xb2 = sb(st, "xb2", [P, TT, D])
            xn2 = sb(st, "xn2", [P, TT, D])
            xT2 = sb(st, "xT2", [P, KD, S])
            cT5 = sb(st, "cT5", [P, KD, S])
            q_part = [sb(st, f"q_part{n}", [P, KD, S], F32R) for n in range(2)]
            k_part = [sb(st, f"k_part{n}", [P, S], F32R) for n in range(2)]
            q_stack = sb(st, "q_stack", [P, HX // 2, S])
            k_stack = sb(st, "k_stack", [P, GX // 2, S])
            m_col = Ring(M, "m_col", [sb(st, f"m_col{k}", [P, TT, HPT]) for k in range(2)])
            m_part = [Ring(M, f"m_part{n}", [sb(st, f"m_part{n}{k}", [HPT, S], F32R) for k in range(2)]) for n in range(2)]
            va = sb(st, "va", [P, TT, GX, DA])
            ex = Ring(M, "ex", [sb(st, f"ex{k}", [P, TT, S]) for k in range(4)])
            oe = Ring(M, "oe", [sb(st, f"oe{k}", [P, S]) for k in range(3)])
            rl = Ring(M, "rl", [sb(st, f"rl{k}", [P, TT, HPT]) for k in range(2)])
            on = Ring(M, "on", [sb(st, f"on{k}", [P, TT, P]) for k in range(2)])
            oT2 = sb(st, "oT2", [P, KD, S])
            prob = {g: Ring(M, "prob" + g, [sb(st, f"prob{g}{k}", [P, TT, S]) for k in range(4)]) for g in "A"}
            probT = {g: Ring(M, "probT" + g, [sb(st, f"probT{g}{k}", [P, TT, S]) for k in range(3)]) for g in "A"}
            stat = {g: Ring(M, "stat" + g, [sb(st, f"stat{g}{k}", [P, 7, TT * TT]) for k in range(6)]) for g in "A"}
            ln_of = {g: [sb(st, f"ln{g}_{n}", [P, TT] + e) for n, e in (("st", [6]), ("mv", [2]), ("ve", []), ("rs", []))]
                     for g in "AX"}
            low = sb(st, "low", [P, TT, RW + NR])
            lowT = sb(st, "lowT", [RW, S])
            g_, ge, gm = (sb(st, "g" + n, [P, TT, NR]) for n in "gem")
            g_gt, g_eq = (sb(st, "g_" + n, [P, TT, NR, NR]) for n in ("gt", "eq"))
            gr = sb(st, "gr", [P, 3, TT])
            M.mark("dve", "va0", dve.memset(va[:, :, :, :], 0.0))
            M.wait(dve, "va0")
            M.mark("dve", "va1", dve.memset(va[:, :, :, DX:DX + 1], 1.0))
            for half in range(2):
                i = dve.memset(k_stack[64 * half + 32:64 * half + 64, :, :], 1.0)
            M.mark("dve", "k_ones", i)
            M.wait(sp, "k_ones")
            M.wait(pe, "w5_w_out")
            M.wait(act, "va1")

            def project(g, tag, src_ready, lhs, rhs, n, release):
                M.wait(pe, *src_ready)
                bank = ring[g].take(pe, release)
                for k in range(KD):
                    i = pe.matmul(bank[:, 0:n], lhs(k), rhs(k), start=k == 0, stop=k == KD - 1)
                M.mark("pe", tag, i)
                return bank

            def turn5(g, tag, src, ready, dst, free):
                for t in range(TT):
                    M.wait(pe, ready(t))
                    bank = ring[g].take(pe, f"{tag}_T{t}")
                    for k in range(KD):
                        i = pe.transpose(bank[:, k * P:(k + 1) * P], src[:, t, k * P:(k + 1) * P], ident[:, :])
                    M.mark("pe", f"{tag}_P{t}", i)
                    M.wait(act, f"{tag}_P{t}")
                    M.wait(act, free[0], ago=free[1])
                    M.mark("act", f"{tag}_T{t}", act.copy(dst[:, :, t * P:(t + 1) * P],
                                                         bank.rearrange("p (k c) -> p k c", k=KD)))
                    yield 850, 0

            def attend(g, heads, ready, oT, oT_free, skew=3):
                buf, opened, stats, banks_of = {}, {}, {}, {}
                n_heads = len(heads)
                per = n_heads // KD

                def scores(h):
                    q, k, _, _, _, _ = heads[h]
                    M.wait(pe, *ready)
                    bank = ring[g].take(pe, f"{g}e{h}")
                    for t in range(TT):
                        i = pe.matmul(bank[:, t * S:(t + 1) * S], q(t), k, start=True, stop=True)
                    M.mark("pe", f"{g}s{h}", i)
                    banks_of[h] = bank
                    maxima(h)

                pairs = lambda s3, n: s3[:, n, :].rearrange("p (t j) -> p t j", j=TT)
                over_j = lambda s3, n: bc(s3[:, n, 0:TT], [P, TT, TT], 2)

                def maxima(h):
                    s3 = stats[h] = stat[g].take(dve, f"{g}n{h}")
                    M.wait(dve, f"{g}s{h}")
                    M.mark("dve", f"{g}m{h}", dve.tensor_reduce(
                        s3[:, 0, :], banks_of[h].rearrange("p (t k) -> p t k", k=P), AX, ALU.max, negate=True))

                def maximum_of_both(h):
                    s3 = stats[h]
                    M.wait(dve, f"{g}m{h}")
                    M.mark("dve", f"{g}ma{h}", dve.tensor_tensor(
                        s3[:, 1, 0:TT], pairs(s3, 0)[:, :, 0], pairs(s3, 0)[:, :, 1], ALU.min))
                    M.wait(pool, f"{g}ma{h}")
                    M.mark("pool", f"{g}mb{h}", pool.tensor_tensor(pairs(s3, 2), over_j(s3, 1), pairs(s3, 0), ALU.subtract))

                def exponentials(h):
                    s3, bank = stats[h], banks_of[h]
                    p = buf[h] = prob[g].take(act, f"{g}pt{h}")
                    M.wait(act, f"{g}m{h}")
                    for n in range(TT * TT):
                        t, j = n // TT, n % TT
                        act.activation(p[:, t, j * P:(j + 1) * P], bank[:, n * P:(n + 1) * P], ACT.Exp,
                                       bias=s3[:, 0, n:n + 1], accum_out=s3[:, 4, n:n + 1])
                    M.wait(act, f"{g}mb{h}")
                    M.mark("act", f"{g}e{h}", act.activation(s3[:, 3, :], s3[:, 2, :], ACT.Exp))
                    M.wait(pool, f"{g}e{h}")
                    M.mark("pool", f"{g}ra{h}", pool.tensor_tensor(s3[:, 5, :], s3[:, 3, :], s3[:, 4, :], ALU.mult))
                    M.wait(pool, f"{g}ra{h}")
                    M.mark("pool", f"{g}rb{h}", pool.tensor_tensor(
                        s3[:, 6, 0:TT], pairs(s3, 5)[:, :, 0], pairs(s3, 5)[:, :, 1], ALU.add))
                    M.wait(pool, f"{g}rb{h}")
                    M.mark("pool", f"{g}rc{h}", pool.tensor_tensor(s3[:, 1, 0:TT], s3[:, 6, 0:TT], minus1[:, :], ALU.pow))
                    M.wait(pool, f"{g}rc{h}")
                    M.mark("pool", f"{g}rd{h}", pool.tensor_tensor(pairs(s3, 2), pairs(s3, 5), over_j(s3, 1), ALU.mult))

                def scale(h):
                    s3, p = stats[h], buf[h]
                    M.wait(dve, f"{g}rd{h}")
                    for n in range(TT * TT):
                        t, j = n // TT, n % TT
                        i = dve.tensor_scalar(p[:, t, j * P:(j + 1) * P], p[:, t, j * P:(j + 1) * P],
                                              s3[:, 2, n:n + 1], None, ALU.mult)
                    M.mark("dve", f"{g}n{h}", i)

                def flip(h):
                    M.wait(pe, f"{g}n{h}")
                    bank = ring[g].take(pe, f"{g}pT{h}")
                    for kt in range(TT):
                        for t in range(TT):
                            i = pe.transpose(bank[:, kt * S + t * P:kt * S + (t + 1) * P],
                                             buf[h][:, t, kt * P:(kt + 1) * P], ident[:, :])
                    M.mark("pe", f"{g}pt{h}", i)
                    e, key = (act, "act") if h % 2 else (dve, "dve")
                    b = buf[h] = probT[g].take(e, f"{g}pv{h}")
                    M.wait(e, f"{g}pt{h}")
                    copy = e.copy if e is act else e.tensor_copy
                    M.mark(key, f"{g}pT{h}", copy(b[:, :, :], bank.rearrange("p (t k) -> p t k", t=TT)))

                def values(h):
                    _, _, v, quad, opens, closes = heads[h]
                    m = h // per
                    if h % per == 0:
                        opened[m] = outs[g].take(pe, f"{g}o{m}")
                    M.wait(pe, f"{g}pT{h}")
                    for kt in range(TT):
                        i = pe.matmul(opened[m][quad:quad + DA, 0:S], v(kt), buf[h][:, kt, :],
                                      start=opens and kt == 0, stop=closes and kt == TT - 1, skip_group_check=True)
                    M.mark("pe", f"{g}pv{h}", i)
                    if h % per == per - 1:
                        M.wait(act, f"{g}pv{h}")
                        M.wait(act, oT_free, ago=1)
                        M.mark("act", f"{g}o{m}", act.copy(oT[:, m, :], opened[m][:, 0:S]))

                for n in range(n_heads + skew + 1):
                    if n < n_heads:
                        scores(n)
                        yield 854, (1000 if n < skew else 0)
                    if n < n_heads:
                        maximum_of_both(n)
                    if 0 < n <= n_heads:
                        scale(n - 1)
                    if skew <= n < n_heads + skew:
                        flip(n - skew)
                    if n < n_heads:
                        exponentials(n)
                    yield 854, 0
                    if n >= skew + 1:
                        values(n - skew - 1)
                        yield 854, (1000 if n >= n_heads else 0)

            def routed_in(b, first=False):
                pick = lambda t: t[:, :, :].rearrange("p c (b t) -> p c b t", t=TT)[:, :, b, :]
                M.wait(dve, "g1_1", ago=1)
                M.mark("dve", "idx5", dve.tensor_copy(idx5[:, :, :], pick(slot_of)))
                M.mark("dve", "wy", dve.tensor_copy(wy[:, :, :], pick(w_of)))
                M.wait(pool, "x3_1", ago=1)
                wait_apart(pool, "idx5")
                for c in range(2):
                    for t in range(TT):
                        M.mark("g_yg", f"g{c}_{t}", pool.indirect_dma_start(
                            out=yg[:, c, t, :], out_offset=None, in_=ys_d,
                            in_offset=bass.IndirectOffsetOnAxis(ap=idx5[:, c, t:t + 1], axis=0)), 16)
                if not first:
                    M.wait(sp, "xb4_1")
                M.wait(sp, "ln4_n1", ago=1)
                M.mark("d_xa", "xa", sp.dma_start(xa1[:, :, :], tokens(x2s_d)[b]), 16)
                yield 0, 6000
                M.wait(dve, "xa", "g1_1", "wy")
                for c in range(2):
                    for t in range(TT):
                        M.mark("dve", f"x3_{t}" if c else f"x3a_{t}", dve.scalar_tensor_tensor(
                            xa1[:, t, :], yg[:, c, t, :], wy[:, c, t:t + 1], xa1[:, t, :], ALU.mult, ALU.add))
                    yield 0, 1200
                    M.wait(dve, f"x3_{TT - 1}" if c else f"x3a_{TT - 1}")
                M.wait(dve, "x4_P1", ago=1)
                yield from norm(ln_of["A"], "ln4", xa1, xn1)
                yield from turn5("A", "x4", xn1, lambda t: f"ln4_n{t}", xT1, ("Pv_1", 1 if first else 0))

            def self_attention(b, peeled):
                M.wait(pool, "x3_1", "x4r_1", ago=1)
                for t in range(TT):
                    M.mark("pool", f"xb4_{t}", pool.tensor_tensor(xb1[:, t, :], xa1[:, t, :], bias[:, 0, :], ALU.add))
                M.wait(pe, "x4_T1", ago=1)
                w = load["w_qkv"]
                for m in range(KD):
                    for n, dst in ((0, qT1), (1, kT1)):
                        bank = project("A", f"P{n}_{m}", [], lambda k: w[:, k, n * D + m * P:n * D + (m + 1) * P],
                                       lambda k: xT1[:, k, :], S, f"q{n}_{m}")
                        M.wait(act, f"P{n}_{m}")
                        M.wait(act, f"As{HA - 1}", ago=1)
                        M.mark("act", f"q{n}_{m}", act.activation(dst[:, m, :], bank[:, 0:S], ACT.Copy,
                                                                 scale=1.0 if n else float(DA) ** -0.5))
                        yield 1700, 0
                for t in range(TT):
                    bank = project("A", f"Pv_{t}", [], lambda k: xT1[:, k, t * P:(t + 1) * P],
                                   lambda k: w[:, k, 2 * D:3 * D], D, f"v5_{t}")
                    M.wait(dve, f"Pv_{t}")
                    M.wait(dve, f"Apv{HA - 1}", ago=1)
                    M.mark("dve", f"v5_{t}", dve.tensor_copy(v1[:, t, :], bank))
                    yield 3400, 0

                def head4(h):
                    m, r = h // HG, slice(DA * (h % HG), DA * (h % HG) + DA)
                    return (lambda t: qT1[r, m, t * P:(t + 1) * P], kT1[r, m, :],
                            lambda kt: v1[:, kt, h * DA:(h + 1) * DA], DA * (h % HG), True, True)
                yield from side_by_side(attend("A", [head4(h) for h in range(HA)], [f"q1_{KD - 1}", "v5_0", "v5_1"], oT1, "Aout1"),
                                        routed_in((b + 1) % B), 20)
                for t in range(TT):
                    bank = project("A", f"Aout{t}", [f"Ao{KD - 1}"], lambda k: oT1[:, k, t * P:(t + 1) * P],
                                   lambda k: load["w_out"][:, k, :], D, f"x4r_{t}")
                    M.wait(dve, f"Aout{t}", f"xb4_{t}")
                    if not peeled:
                        M.wait(dve, "xb5_1", "ln5_n1")
                    M.mark("dve", f"x4r_{t}", dve.tensor_tensor(x4[:, t, :], bank, xb1[:, t, :], ALU.add))
                    yield 3400, 0

            def cross_attention_and_ffn(b):
                M.wait(sp, f"X2_{HX - 1}", ago=1)
                M.mark("d_cT5", "cT5", sp.dma_start(cT5[:, :, :], ctxT_d[b]), 16)
                M.wait(dve, "x4r_1", ago=1)
                M.wait(dve, "x6_P1", ago=1)
                yield from norm(ln_of["X"], "ln5", x4, xn2)
                for t in range(TT):
                    M.wait(pool, "x4r_1", "out_st", ago=1)
                    M.mark("pool", f"xb5_{t}", pool.tensor_tensor(xb2[:, t, :], x4[:, t, :], bias[:, 1, :], ALU.add))
                bank = project("X", "Pxk", ["cT5"], lambda k: load["xk"][:, k, :], lambda k: cT5[:, k, :], S, "k_low")
                M.wait(act, "Pxk")
                M.wait(act, "k_write1", ago=1)
                M.mark("act", "k_high", act.copy(k_part[0][:, :], bank[:, 0:S]))
                M.wait(dve, "k_high")
                M.wait(dve, "k_write1", ago=1)
                M.mark("dve", "k_low", dve.tensor_tensor(k_part[1][:, :], bank[:, 0:S], k_part[0][:, :].bitcast(F32), ALU.subtract))
                M.wait(sp, "k_low")
                M.wait(sp, "k_read", ago=1)
                for n in range(2):
                    M.mark("d_kw", f"k_write{n}", sp.dma_start(k_parts_d[n], k_part[n][:, :].bitcast(F32)), 16)
                M.wait(sp, "k_write1")
                for half in range(2):
                    for row, n in enumerate((0, 0, 1)):
                        i = sp.dma_start(k_stack[64 * half + DX * row:64 * half + DX * (row + 1), :, :],
                                         k_parts_d[n, 64 * half:64 * half + 64, :].rearrange("(g d) s -> d g s", d=DX))
                        M.mark("d_kr", "k_read" if (half, row) == (1, 2) else f"k_read{half}{row}", i, 16)
                yield 1700, 0
                yield from turn5("X", "x5", xn2, lambda t: f"ln5_n{t}", xT2, ("ffn1", 1))
                for t in range(TT):
                    bank = project("X", f"xv_{t}", ["cT5"], lambda k: cT5[:, k, t * P:(t + 1) * P],
                                   lambda k: load["xv"][:, k, :], P, f"va_{t}")
                    M.wait(act, f"xv_{t}")
                    M.wait(act, f"Xv{HX - 1}", ago=1)
                    M.mark("act", f"va_{t}", act.copy(va[:, t, :, 0:DX],
                                                     bank[:, 0:P].rearrange("p (g d) -> p g d", g=GX)))
                    if t == 0:
                        yield 1700, 0
                for m in range(KD):
                    half = m // 2
                    bank = project("X", f"Pxq_{m}", ["x5_T1"], lambda k: load["xq"][:, k, m * P:(m + 1) * P],
                                   lambda k: xT2[:, k, :], S, f"q_low{m}")
                    M.wait(act, f"Pxq_{m}")
                    M.wait(act, f"q_write{half}1", ago=1)
                    M.mark("act", f"q_high{m}", act.activation(q_part[0][:, m, :], bank[:, 0:S], ACT.Copy, scale=float(DX) ** -0.5))
                    M.wait(dve, f"q_high{m}")
                    M.wait(dve, f"q_write{half}1", ago=1)
                    M.mark("dve", f"q_low{m}", dve.scalar_tensor_tensor(
                        q_part[1][:, m, :], bank[:, 0:S], float(DX) ** -0.5, q_part[0][:, m, :].bitcast(F32), ALU.mult, ALU.subtract))
                    if m % 2:
                        M.wait(sp, f"q_low{m}")
                        M.wait(sp, f"q_read{half}2", ago=1)
                        mine = slice(half * D // 2, (half + 1) * D // 2)
                        for n in range(2):
                            M.mark(f"d_qw{half}", f"q_write{half}{n}", sp.dma_start(
                                q_parts_d[n, mine, :].rearrange("(m p) s -> p m s", p=P),
                                q_part[n][:, m - 1:m + 1, :].bitcast(F32)), 16)
                        M.wait(sp, f"q_write{half}1")
                        for row, n in enumerate((0, 1, 0)):
                            M.mark(f"d_qr{half}", f"q_read{half}{row}", sp.dma_start(
                                q_stack[64 * half + DX * row:64 * half + DX * (row + 1), :, :],
                                q_parts_d[n, mine, :].rearrange("(h d) s -> d h s", d=DX)), 16)
                    yield 1700, (5000 if m == KD - 1 else 0)

                yield from cross_heads()
                for t in range(TT):
                    bank = project("X", f"Xout{t}", [f"oT2_{KD - 1}"], lambda k: oT2[:, k, t * P:(t + 1) * P],
                                   lambda k: load["xfc"][:, k, :], D, f"x5r_{t}")
                    M.wait(dve, f"Xout{t}", f"xb5_{t}")
                    M.wait(dve, "xb6_1", ago=1)
                    M.mark("dve", f"x5r_{t}", dve.tensor_tensor(xa2[:, t, :], bank, xb2[:, t, :], ALU.add))
                    yield 3400, 800 * t
                M.wait(dve, "x5r_1")

                M.wait(dve, "x5_P1")
                yield from norm(ln_of["X"], "ln6", xa2, xn2)
                yield from turn5("X", "x6", xn2, lambda t: f"ln6_n{t}", xT2, (f"Pxq_{KD - 1}", 0))
                for t in range(TT):
                    M.wait(pool, "x5r_1")
                    M.mark("pool", f"xb6_{t}", pool.tensor_tensor(xb2[:, t, :], xa2[:, t, :], bias[:, 2, :], ALU.add))
                for t in range(TT):
                    bank = project("X", f"Plow_{t}", ["x6_T1"], lambda k: xT2[:, k, t * P:(t + 1) * P],
                                   lambda k: load["low_in"][:, k, :], RW + NR, f"low_{t}")
                    M.wait(act, f"Plow_{t}")
                    M.wait(act, "low_P1", ago=1)
                    M.mark("act", f"low_{t}", act.copy(low[:, t, :], bank[:, 0:RW + NR]))
                    yield 1700, 0
                base = []
                for t in range(TT):
                    base.append(ring["X"].take(pe, f"x6r_{t}"))
                    for k in range(KD):
                        pe.matmul(base[t], xT2[:, k, t * P:(t + 1) * P], load["w_base"][:, k, :], start=k == 0, stop=False)
                yield 6800, 0
                each = lambda n: bc(gr[:, n, :], [P, TT, NR], 2)

                def V(name, ins):
                    M.mark("dve", name, ins)
                    yield 0, 250
                    M.wait(dve, name)

                M.wait(dve, "low_1")
                yield from V("g0", dve.tensor_tensor(g_[:, :, :], low[:, :, RW:], bc(rbias[:, :], [P, TT, NR], 1), ALU.add))
                yield from V("g1", dve.tensor_reduce(gr[:, 0, :], g_[:, :, :], AX, ALU.max))
                yield from V("g2", dve.tensor_tensor(g_[:, :, :], g_[:, :, :], each(0), ALU.subtract))
                M.wait(act, "g2")
                M.mark("act", "gexp", act.activation(ge[:, :, :], g_[:, :, :], ACT.Exp))
                yield 0, 2400
                M.wait(dve, "gexp")
                yield from V("g3", dve.tensor_reduce(gr[:, 1, :], ge[:, :, :], AX, ALU.add))
                yield from V("g4", dve.reciprocal(gr[:, 2, :], gr[:, 1, :]))
                yield from V("g5", dve.tensor_tensor(ge[:, :, :], ge[:, :, :], each(2), ALU.mult))
                cube = [P, TT, NR, NR]
                other = lambda t: ge[:, t, :].unsqueeze(1).broadcast_to([P, NR, NR])
                own = lambda t: bc(ge[:, t, :], [P, NR, NR], 2)
                for t in range(TT):
                    dve.tensor_tensor(g_gt[:, t, :, :], other(t), own(t), ALU.is_gt)
                    i = dve.tensor_tensor(g_eq[:, t, :, :], other(t), own(t), ALU.is_equal)
                yield from V("g6", i)
                yield from V("g7", dve.tensor_tensor(g_eq[:, :, :, :], g_eq[:, :, :, :], bc(lower[:, :, :], cube, 1), ALU.mult))
                yield from V("g8", dve.tensor_tensor(g_gt[:, :, :, :], g_gt[:, :, :, :], g_eq[:, :, :, :], ALU.add))
                yield from V("g9", dve.tensor_reduce(g_[:, :, :], g_gt[:, :, :, :], AX, ALU.add))
                yield from V("gf", dve.scalar_tensor_tensor(gm[:, :, :], g_[:, :, :], 1.5, ge[:, :, :], ALU.is_lt, ALU.mult))
                lowv = low[:, :, 0:RR * NR].rearrange("p t (e r) -> p t e r", r=RR)
                for t in range(TT):
                    i = dve.tensor_tensor(lowv[:, t, :, :], lowv[:, t, :, :], bc(gm[:, t, :], [P, NR, RR], 2), ALU.mult)
                M.mark("dve", "gated", i)
                yield 0, 1500
                M.wait(pe, "gated")
                bank = ring["X"].take(pe, "lowT")
                for t in range(TT):
                    i = pe.transpose(bank[0:RW, t * P:(t + 1) * P], low[:, t, 0:RW], ident[:, :])
                    M.mark("pe", f"low_P{t}", i)
                M.wait(act, "low_P1")
                M.wait(act, "ffn1", ago=1)
                M.mark("act", "lowT", act.copy(lowT[:, :], bank[0:RW, 0:S]))
                yield 430, 0
                for t in range(TT):
                    M.wait(pe, "lowT")
                    M.mark("pe", f"ffn{t}", pe.matmul(base[t], lowT[:, t * P:(t + 1) * P], low_out[:, :], start=False, stop=True))
                    M.wait(dve, f"ffn{t}", f"xb6_{t}")
                    M.mark("dve", f"x6r_{t}", dve.tensor_tensor(xb2[:, t, :], base[t], xb2[:, t, :], ALU.add))
                    yield 850, 0
                M.wait(sp, "x6r_1")
                M.mark("d_out", "out_st", sp.dma_start(tokens(io["out"])[b], xb2[:, :, :]), 16)

            def cross_heads():
                cols, opened, exps = {}, {}, {}

                def maximum(h):
                    half, slot = h // (HX // 2), h % (HX // 2)
                    r = slice(64 * half, 64 * half + 3 * DX)
                    M.wait(pe, "k_read", f"q_read{half}2")
                    bank = ring["X"].take(pe, f"X1m{h}")
                    for t in range(TT):
                        i = pe.matmul(bank[:, t * S:(t + 1) * S], q_stack[r, slot, t * P:(t + 1) * P].bitcast(F32R),
                                      k_stack[r, slot // 4, :].bitcast(F32R), start=True, stop=True)
                    M.mark("pe", f"X1_{h}", i)
                    tile = h // HPT
                    if h % HPT == 0:
                        cols[tile] = m_col.take(dve, f"mT{tile}")
                    M.wait(dve, f"X1_{h}")
                    M.mark("dve", f"X1m{h}", dve.tensor_reduce(
                        cols[tile][:, :, h % HPT], bank.rearrange("p (t k) -> p t k", t=TT), AX, ALU.max, negate=True))

                def maximum_rows(tile):
                    half, slot = tile // 2, HPT * (tile % 2)
                    M.wait(pe, f"X1m{tile * HPT + HPT - 1}")
                    bank = ring["X"].take(pe, f"m_low{tile}")
                    for t in range(TT):
                        i = pe.transpose(bank[0:HPT, t * P:(t + 1) * P], cols[tile][:, t, :], ident[:, :])
                    M.mark("pe", f"mT{tile}", i)
                    high, low_ = m_part[0].take(act, f"m_in{tile}1"), m_part[1].take(dve, f"m_in{tile}1")
                    M.wait(act, f"mT{tile}")
                    M.mark("act", f"m_high{tile}", act.copy(high[:, :], bank[0:HPT, 0:S]))
                    M.wait(dve, f"m_high{tile}")
                    M.mark("dve", f"m_low{tile}", dve.tensor_tensor(
                        low_[:, :], bank[0:HPT, 0:S], high[:, :].bitcast(F32), ALU.subtract))
                    M.wait(sp, f"m_low{tile}")
                    for n, part in enumerate((high, low_)):
                        row = 64 * half + 3 * DX + n
                        M.mark(f"d_m{tile % 2}", f"m_in{tile}{n}", sp.dma_start(
                            q_stack[row:row + 1, slot:slot + HPT, :], part[:, :].bitcast(F32)), 16)

                def exponential(h):
                    half, slot = h // (HX // 2), h % (HX // 2)
                    r = slice(64 * half, 64 * half + 3 * DX + 2)
                    M.wait(pe, f"m_in{h // HPT}1")
                    bank = ring["X"].take(pe, f"X2e{h}")
                    for kt in range(TT):
                        i = pe.matmul(bank[:, kt * S:(kt + 1) * S], k_stack[r, slot // 4, kt * P:(kt + 1) * P].bitcast(F32R),
                                      q_stack[r, slot, :].bitcast(F32R), start=True, stop=True)
                    M.mark("pe", f"X2_{h}", i)
                    e = exps[h] = ex.take(act, f"Xv{h}")
                    M.wait(act, f"X2_{h}")
                    M.mark("act", f"X2e{h}", act.activation(e[:, :, :].rearrange("p t s -> p (t s)"), bank, ACT.Exp))

                def values_and_sum(h):
                    quad = DA * (h % 4)
                    if h % 4 == 0:
                        opened[h // 4] = outs["X"].take(pe, f"oe{h // 4}")
                    out = opened[h // 4]
                    M.wait(pe, f"X2e{h}", "va_1")
                    for kt in range(TT):
                        i = pe.matmul(out[quad:quad + DA, 0:S], va[:, kt, h // 4, :], exps[h][:, kt, :],
                                      start=kt == 0, stop=kt == TT - 1, skip_group_check=True)
                    M.mark("pe", f"Xv{h}", i)
                    if h % 4 == 3:
                        buf = exps[f"o{h // 4}"] = oe.take(act, f"oeT{h // HPT}")
                        M.wait(act, f"Xv{h}")
                        M.mark("act", f"oe{h // 4}", act.copy(buf[:, :], out[:, 0:S]))

                def divide(tile):
                    M.wait(pe, f"oe{2 * tile + 1}")
                    bank = ring["X"].take(pe, f"on{tile}")
                    for t in range(TT):
                        for u in range(2):
                            i = pe.transpose(bank[:, (2 * t + u) * P:(2 * t + u + 1) * P],
                                             exps[f"o{2 * tile + u}"][:, t * P:(t + 1) * P], ident[:, :])
                    M.mark("pe", f"oeT{tile}", i)
                    heads = bank.rearrange("p (t h d) -> p t h d", t=TT, d=DA)
                    r, o = rl.take(dve, f"on{tile}"), on.take(dve, f"onT{tile}")
                    M.wait(dve, f"oeT{tile}")
                    M.mark("dve", f"rl{tile}", dve.reciprocal(r[:, :, :], heads[:, :, :, DX]))
                    M.wait(dve, f"rl{tile}")
                    for t in range(TT):
                        i = dve.tensor_tensor(o[:, t, :].rearrange("p (h d) -> p h d", d=DX), heads[:, t, :, 0:DX],
                                              bc(r[:, t, :], [P, HPT, DX], 2), ALU.mult)
                    M.mark("dve", f"on{tile}", i)
                    exps[f"n{tile}"] = o

                def turn_back(tile):
                    M.wait(pe, f"on{tile}")
                    bank = ring["X"].take(pe, f"oT2_{tile}")
                    for t in range(TT):
                        i = pe.transpose(bank[:, t * P:(t + 1) * P], exps[f"n{tile}"][:, t, :], ident[:, :])
                    M.mark("pe", f"onT{tile}", i)
                    M.wait(act, f"onT{tile}")
                    M.wait(act, "Xout1", ago=1)
                    M.mark("act", f"oT2_{tile}", act.copy(oT2[:, tile, :], bank[:, 0:S]))

                lag = HPT + 6
                for n in range(HX + lag + 7):
                    if n < HX:
                        maximum(n)
                        yield 213, (400 if n < lag else 0)
                    if n >= HPT and n % HPT == 0 and n <= HX:
                        maximum_rows(n // HPT - 1)
                        yield 430, 0
                    if lag <= n < HX + lag:
                        exponential(n - lag)
                    if lag + 2 <= n < HX + lag + 2:
                        values_and_sum(n - lag - 2)
                        yield 1070, (1000 if n >= HX + lag else 0)
                    h = n - lag - 4
                    if 0 <= h < HX and h % HPT == HPT - 1:
                        divide(h // HPT)
                        yield 900, (1500 if n >= HX + lag else 0)
                    h -= 2
                    if 0 <= h < HX and h % HPT == HPT - 1:
                        turn_back(h // HPT)
                        yield 430, (700 if n >= HX + lag else 0)

            M.prefix = "zeroth_"
            alone(routed_in(0, first=True))
            M.prefix = ""
            M.wait(sp, "zeroth_g1_1")
            load_weights5()
            nc.all_engine_barrier()
            M.close()
            M.wait(pool, "w5_b_base")
            M.prefix = "first_"
            ahead = alone(self_attention(0, True))
            M.prefix = ""
            M.wait(pe, "w5_lower")
            M.wait(pool, "w5_lower")
            M.wait(dve, "w5_lower")
            nc.all_engine_barrier()
            with M.loop(B - 1) as b:
                together((cross_attention_and_ffn(b), 1.01 * ahead), (self_attention(b + 1, False), ahead))
            M.wait(sp, "out_st")
            nc.all_engine_barrier()
            M.prefix = "last_"
            alone(cross_attention_and_ffn(B - 1))
            M.wait(sp, "out_st")
        M.close()
        return M


def _tables():
    ident = np.eye(P, dtype=np.float32)
    start = 2.0 ** (-2.0 ** (-(np.log2(HA) - 3)))
    slopes = np.array([start * start ** i for i in range(HA)])
    pos = np.arange(S)
    dist = pos[None, :] - np.arange(P)[:, None]
    full = np.where(dist[:, None, :] >= 0, np.exp(-slopes[None, :, None] * np.maximum(dist, 0)[:, None, :]), 0.0)
    dmask = np.concatenate([full, full[:, :, :P]], axis=2).astype(np.float32)
    quarter = DA // 4
    freq = np.concatenate([(1.0 / 1024.0) ** np.linspace(0.0, 1.0, quarter, dtype=np.float32),
                           np.zeros(quarter, np.float32)]).astype(np.float32)
    theta = (pos.astype(np.float32)[:, None] * freq[None, :]).astype(np.float32).astype(np.float64)
    rot = np.stack([np.cos(theta), np.sin(theta), -np.sin(theta)]).astype(np.float32)
    rot = rot.reshape(3, TT, P, DA // 2).transpose(2, 0, 1, 3)
    tri = np.triu(np.ones((P, P), np.float32), 1)
    rconst = np.tile(np.concatenate([NE - np.arange(NE), P * np.arange(NT), np.arange(SLOTS)]).astype(np.float32), (P, 1))
    token_ids = (np.arange(NT)[None, :] * P + np.arange(P)[:, None]).astype(np.uint32)
    return {"ident": ident, "dmask": dmask, "rot": rot, "tri": tri, "rconst": rconst, "token_ids": token_ids}


def kernel(**inputs):
    import concourse.bacc as bacc
    from concourse.bass_utils import run_bass_kernel_spmd as run

    a = {k: np.asarray(v) for k, v in inputs.items()}
    flip = lambda w, axis: np.flip(w.reshape(w.shape[:axis] + (KD, P) + w.shape[axis + 1:]), axis + 1).reshape(w.shape)
    laid = dict(_tables())
    laid.update({
        "x": a["x"],
        "ctx": flip(a["ctx_2048"], 2),
        "wq": a["L0_attn_Wq"], "wk": a["L0_attn_Wk"], "wv": a["L0_attn_Wv"], "wo": a["L0_attn_Wo"],
        "rms_w": a["L0_attn_rms_w"].reshape(KD, P).T,
        "ssm_kernel": a["L0_xattn_ssm_kernel"],
        "skip": a["L0_xattn_D"].reshape(HC, 1),
        "shared_gate_up": np.concatenate([a["L0_ffn_shared_wg"], a["L0_ffn_shared_wu"], a["L0_ffn_gate_w"]]).T,
        "shared_down": a["L0_ffn_shared_wd"].T,
        "exp_gate_up": np.concatenate([a["L0_ffn_exp_wg"], a["L0_ffn_exp_wu"]], axis=1).transpose(0, 2, 1),
        "exp_down": a["L0_ffn_exp_wd"].transpose(0, 2, 1),
    })
    qkv = a["L1_attn_w_qkv"].T
    laid.update({
        "w_qkv": qkv, "w_out": a["L1_attn_w_out"].T, "b_out": a["L1_attn_b_out"].reshape(1, D),
        "xq": a["L1_xattn_Wq"].T, "xk": flip(a["L1_xattn_Wk"].T, 0), "xv": flip(a["L1_xattn_Wv"].T, 0),
        "xfc": a["L1_xattn_Wfc"].T, "b_fc": a["L1_xattn_bfc"].reshape(1, D),
        "w_base": a["L1_ffn_W_base"], "b_base": a["L1_ffn_b_base"].reshape(1, D),
        "low_in": np.concatenate([a["L1_ffn_A_r"].transpose(1, 0, 2).reshape(D, NR * RR), a["L1_ffn_A_s"],
                                  a["L1_ffn_W_router"]], axis=1),
        "low_out": np.concatenate([a["L1_ffn_B_r"].reshape(NR * RR, D), a["L1_ffn_B_s"]]),
        "b_router": a["L1_ffn_b_router"].reshape(1, NR),
        "lower": np.tile(np.tril(np.ones((NR, NR), np.float32), -1), (P, 1, 1)),
    })
    laid = {k: np.ascontiguousarray(v) for k, v in laid.items()}

    def program(known):
        nc = bacc.Bacc("TRN2", target_bir_lowering=False, num_devices=1)
        io = {k: nc.dram_tensor("in_" + k, v.shape, mybir.dt.from_np(v.dtype), kind="ExternalInput").ap()
              for k, v in laid.items()}
        io["out"] = nc.dram_tensor("out_0_dram", (B, S, D), F32, kind="ExternalOutput").ap()
        return nc, build(nc, io, known)

    _, counted = program(None)
    nc, _ = program(counted)
    r = run(nc, [{"in_" + k: v for k, v in laid.items()}], core_ids=[0])
    return r.results[0]["out_0_dram"]
```
